# Optimizing a Trainium2 kernel written in Bass

```python
import numpy as np
import jax
import jax.numpy as jnp

def _softmax(x, axis=-1):
    return jax.nn.softmax(x, axis=axis)

def _gelu(x):
    return jax.nn.gelu(x, approximate=True)

def _silu(x):
    return jax.nn.silu(x)

def _sigmoid(x):
    return jax.nn.sigmoid(x)

def _layernorm(x, axis=-1, eps=1e-05):
    m = jnp.mean(x, axis=axis, keepdims=True)
    v = jnp.var(x, axis=axis, keepdims=True)
    return (x - m) / jnp.sqrt(v + eps)

def _scatter_add(tgt, idx, src, axis=0):
    return tgt.at[idx].add(src)

def _segment_sum(src, seg, n):
    return jax.ops.segment_sum(src, seg, n)
kernel_name = 'mk_sandwich_d2_jaxref_r8_bdbc2e'

def setup_inputs(seed: int=0):
    np.random.seed(seed)
    _w = jnp.asarray

    def _L0_attn_setup():
        import jax, jax.numpy as jnp
        import numpy as np
        H = 128
        NH = 16
        HD = H // NH
        BETA = 1.0
        STEPS = 2
        EPS_NORM = 1e-12
        EPS_LN = 1e-05

        def _l2norm(x):
            n = jnp.linalg.norm(x, axis=-1, keepdims=True)
            return x / jnp.maximum(n, EPS_NORM)
        key = jax.random.key(seed)
        ks = jax.random.split(key, 10)
        s = 1.0 / np.sqrt(H)
        return {'hidden_states': jax.random.normal(ks[0], (2, 256, H), jnp.float32), 'Wq': jax.random.normal(ks[1], (H, H), jnp.float32) * s, 'bq': jnp.zeros((H,), jnp.float32), 'Wk': jax.random.normal(ks[2], (H, H), jnp.float32) * s, 'bk': jnp.zeros((H,), jnp.float32), 'Wv': jax.random.normal(ks[3], (H, H), jnp.float32) * s, 'bv': jnp.zeros((H,), jnp.float32), 'Wo': jax.random.normal(ks[4], (H, H), jnp.float32) * s, 'bo': jnp.zeros((H,), jnp.float32), 'ln_w': jnp.ones((H,), jnp.float32), 'ln_b': jnp.zeros((H,), jnp.float32)}
    _L0_attn_in = _L0_attn_setup()

    def _L0_ffn_setup():
        import jax, jax.numpy as jnp
        import numpy as np
        D_MODEL = 128
        N_EXPERTS = 8
        TOP_K = 2
        HIDDEN = 4 * D_MODEL
        key = jax.random.key(seed)
        ks = jax.random.split(key, 6)
        B, S = (2, 256)
        x = jax.random.normal(ks[0], (B, S, D_MODEL), dtype=jnp.float32)
        shared_w1 = jax.random.normal(ks[1], (HIDDEN, D_MODEL), dtype=jnp.float32) * 0.02
        shared_w2 = jax.random.normal(ks[2], (D_MODEL, HIDDEN), dtype=jnp.float32) * 0.02
        experts_w1 = jax.random.normal(ks[3], (N_EXPERTS, HIDDEN, D_MODEL), dtype=jnp.float32) * 0.02
        experts_w2 = jax.random.normal(ks[4], (N_EXPERTS, D_MODEL, HIDDEN), dtype=jnp.float32) * 0.02
        gate_w = jax.random.normal(ks[5], (N_EXPERTS, D_MODEL), dtype=jnp.float32) * 0.02
        return {'x': x, 'shared_w1': shared_w1, 'shared_w2': shared_w2, 'experts_w1': experts_w1, 'experts_w2': experts_w2, 'gate_w': gate_w}
    _L0_ffn_in = _L0_ffn_setup()

    def _L1_attn_setup():
        import jax, jax.numpy as jnp
        import numpy as np
        DIM = 128
        HEADS = 16
        HEAD_DIM = DIM // HEADS
        WS = 64
        SEQ = 256
        BATCH = 2
        SCALE = HEAD_DIM ** (-0.5)

        def _split_heads_windowed(t, h, ws):
            b, L, hd = t.shape
            n, d = (L // ws, hd // h)
            return t.reshape(b, n, ws, h, d).transpose(0, 3, 1, 2, 4)

        def _split_heads(t, h):
            b, L, hd = t.shape
            d = hd // h
            return t.reshape(b, L, h, d).transpose(0, 2, 1, 3)
        key = jax.random.key(seed)
        ks = jax.random.split(key, 11)
        inner = HEADS * HEAD_DIM
        return {'x': jax.random.normal(ks[0], (BATCH, SEQ, DIM), jnp.float32), 'w_v': jax.random.normal(ks[1], (DIM, inner), jnp.float32) * 0.02, 'b_v': jax.random.normal(ks[2], (inner,), jnp.float32) * 0.02, 'w_wqk': jax.random.normal(ks[3], (DIM, 2 * inner), jnp.float32) * 0.02, 'b_wqk': jax.random.normal(ks[4], (2 * inner,), jnp.float32) * 0.02, 'w_qk': jax.random.normal(ks[5], (DIM, 2 * inner), jnp.float32) * 0.02, 'b_qk': jax.random.normal(ks[6], (2 * inner,), jnp.float32) * 0.02, 'w_out': jax.random.normal(ks[7], (inner, DIM), jnp.float32) * 0.02, 'b_out': jax.random.normal(ks[8], (DIM,), jnp.float32) * 0.02, 'w_pos_embedding': jax.random.normal(ks[9], (2 * WS - 1,), jnp.float32), 'pos_embedding': jax.random.normal(ks[10], (2 * SEQ - 1,), jnp.float32)}
    _L1_attn_in = _L1_attn_setup()

    def _L1_ffn_setup():
        import jax, jax.numpy as jnp
        import numpy as np
        B, S, D = (2, 256, 128)
        E, K, F = (16, 2, 64)
        FS = 128
        key = jax.random.key(seed)
        ks = jax.random.split(key, 8)

        def w(k, shape, fan_in):
            return jax.random.normal(k, shape, jnp.float32) / np.sqrt(fan_in).astype(np.float32)
        return {'x': jax.random.normal(ks[0], (B, S, D), jnp.float32), 'Wr': w(ks[1], (D, E), D), 'Wg': w(ks[2], (E, D, F), D), 'Wu': w(ks[3], (E, D, F), D), 'Wd': w(ks[4], (E, F, D), F), 'Sg': w(ks[5], (D, FS), D), 'Su': w(ks[6], (D, FS), D), 'Sd': w(ks[7], (FS, D), FS)}
    _L1_ffn_in = _L1_ffn_setup()
    _d = {'L0_attn_hidden_states': _L0_attn_in['hidden_states'], 'L0_attn_Wq': _L0_attn_in['Wq'], 'L0_attn_bq': _L0_attn_in['bq'], 'L0_attn_Wk': _L0_attn_in['Wk'], 'L0_attn_bk': _L0_attn_in['bk'], 'L0_attn_Wv': _L0_attn_in['Wv'], 'L0_attn_bv': _L0_attn_in['bv'], 'L0_attn_Wo': _L0_attn_in['Wo'], 'L0_attn_bo': _L0_attn_in['bo'], 'L0_attn_ln_w': _L0_attn_in['ln_w'], 'L0_attn_ln_b': _L0_attn_in['ln_b'], 'L0_ffn_shared_w1': _L0_ffn_in['shared_w1'], 'L0_ffn_shared_w2': _L0_ffn_in['shared_w2'], 'L0_ffn_experts_w1': _L0_ffn_in['experts_w1'], 'L0_ffn_experts_w2': _L0_ffn_in['experts_w2'], 'L0_ffn_gate_w': _L0_ffn_in['gate_w'], 'L1_attn_w_v': _L1_attn_in['w_v'], 'L1_attn_b_v': _L1_attn_in['b_v'], 'L1_attn_w_wqk': _L1_attn_in['w_wqk'], 'L1_attn_b_wqk': _L1_attn_in['b_wqk'], 'L1_attn_w_qk': _L1_attn_in['w_qk'], 'L1_attn_b_qk': _L1_attn_in['b_qk'], 'L1_attn_w_out': _L1_attn_in['w_out'], 'L1_attn_b_out': _L1_attn_in['b_out'], 'L1_attn_w_pos_embedding': _L1_attn_in['w_pos_embedding'], 'L1_attn_pos_embedding': _L1_attn_in['pos_embedding'], 'L1_ffn_Wr': _L1_ffn_in['Wr'], 'L1_ffn_Wg': _L1_ffn_in['Wg'], 'L1_ffn_Wu': _L1_ffn_in['Wu'], 'L1_ffn_Wd': _L1_ffn_in['Wd'], 'L1_ffn_Sg': _L1_ffn_in['Sg'], 'L1_ffn_Su': _L1_ffn_in['Su'], 'L1_ffn_Sd': _L1_ffn_in['Sd']}
    _x0 = _d['L0_attn_hidden_states']
    _d['L0_attn_hidden_states'] = jax.random.normal(jax.random.fold_in(jax.random.key(seed), 1), (16, 256, 128), dtype=_x0.dtype)
    del _x0
    return _d

def reference(L0_attn_hidden_states, L0_attn_Wq, L0_attn_bq, L0_attn_Wk, L0_attn_bk, L0_attn_Wv, L0_attn_bv, L0_attn_Wo, L0_attn_bo, L0_attn_ln_w, L0_attn_ln_b, L0_ffn_shared_w1, L0_ffn_shared_w2, L0_ffn_experts_w1, L0_ffn_experts_w2, L0_ffn_gate_w, L1_attn_w_v, L1_attn_b_v, L1_attn_w_wqk, L1_attn_b_wqk, L1_attn_w_qk, L1_attn_b_qk, L1_attn_w_out, L1_attn_b_out, L1_attn_w_pos_embedding, L1_attn_pos_embedding, L1_ffn_Wr, L1_ffn_Wg, L1_ffn_Wu, L1_ffn_Wd, L1_ffn_Sg, L1_ffn_Su, L1_ffn_Sd):

    def _L0_attn_ref(hidden_states, Wq, bq, Wk, bk, Wv, bv, Wo, bo, ln_w, ln_b):
        import jax, jax.numpy as jnp
        import numpy as np
        H = 128
        NH = 16
        HD = H // NH
        BETA = 1.0
        STEPS = 2
        EPS_NORM = 1e-12
        EPS_LN = 1e-05

        def _l2norm(x):
            n = jnp.linalg.norm(x, axis=-1, keepdims=True)
            return x / jnp.maximum(n, EPS_NORM)
        B, S, _ = hidden_states.shape
        residual = hidden_states
        mu = jnp.mean(hidden_states, axis=-1, keepdims=True)
        var = jnp.mean(jnp.square(hidden_states - mu), axis=-1, keepdims=True)
        x = (hidden_states - mu) * jax.lax.rsqrt(var + EPS_LN) * ln_w + ln_b
        q = (x @ Wq + bq).reshape(B, S, NH, HD)
        k = (x @ Wk + bk).reshape(B, S, NH, HD)
        v = (x @ Wv + bv).reshape(B, S, NH, HD)
        q = _l2norm(q)
        k = _l2norm(k)
        state = q
        for _ in range(STEPS):
            sim = jnp.einsum('bqhd,bkhd->bqhk', state, k)
            att = jax.nn.softmax(BETA * sim, axis=-1)
            state = jnp.einsum('bqhk,bkhd->bqhd', att, v)
        o = state.reshape(B, S, H) @ Wo + bo
        return residual + o

    def _L0_ffn_ref(x, shared_w1, shared_w2, experts_w1, experts_w2, gate_w):
        import jax, jax.numpy as jnp
        import numpy as np
        D_MODEL = 128
        N_EXPERTS = 8
        TOP_K = 2
        HIDDEN = 4 * D_MODEL
        B, S, D = x.shape
        T = B * S
        x_flat = x.reshape(T, D)
        shared = jnp.einsum('td,dh->th', x_flat, shared_w1.T)
        shared = jnp.einsum('th,hd->td', jax.nn.silu(shared), shared_w2.T)
        gate_logits = x_flat @ gate_w.T
        top_k_gates, top_k_idx = jax.lax.top_k(gate_logits, TOP_K)
        top_k_gates = jax.nn.softmax(top_k_gates, axis=1)
        gates = jnp.zeros((T, N_EXPERTS), dtype=x.dtype)
        gates = gates.at[jnp.arange(T)[:, None], top_k_idx].set(top_k_gates)
        h = jnp.einsum('td,ehd->teh', x_flat, experts_w1)
        expert_out = jnp.einsum('teh,edh->ted', jax.nn.silu(h), experts_w2)
        selected = jnp.einsum('ted,te->td', expert_out, gates)
        return (shared + selected).reshape(B, S, D)

    def _L1_attn_ref(x, w_v, b_v, w_wqk, b_wqk, w_qk, b_qk, w_out, b_out, w_pos_embedding, pos_embedding):
        import jax, jax.numpy as jnp
        import numpy as np
        DIM = 128
        HEADS = 16
        HEAD_DIM = DIM // HEADS
        WS = 64
        SEQ = 256
        BATCH = 2
        SCALE = HEAD_DIM ** (-0.5)

        def _split_heads_windowed(t, h, ws):
            b, L, hd = t.shape
            n, d = (L // ws, hd // h)
            return t.reshape(b, n, ws, h, d).transpose(0, 3, 1, 2, 4)

        def _split_heads(t, h):
            b, L, hd = t.shape
            d = hd // h
            return t.reshape(b, L, h, d).transpose(0, 2, 1, 3)
        b, L, _ = x.shape
        h, ws = (HEADS, WS)
        v = x @ w_v + b_v
        wqk = x @ w_wqk + b_wqk
        wq, wk = jnp.split(wqk, 2, axis=-1)
        wq = _split_heads_windowed(wq, h, ws)
        wk = _split_heads_windowed(wk, h, ws)
        wv = _split_heads_windowed(v, h, ws)
        wdots = jnp.einsum('bhnid,bhnjd->bhnij', wq, wk) * SCALE
        w_bias = w_pos_embedding[ws - 1 - jnp.arange(ws)]
        wdots = wdots + w_bias
        wattn = jax.nn.softmax(wdots, axis=-1)
        wout = jnp.einsum('bhnij,bhnjd->bhnid', wattn, wv)
        n = L // ws
        wout = wout.transpose(0, 2, 3, 1, 4).reshape(b, L, h * HEAD_DIM)
        qk = x @ w_qk + b_qk
        q, k = jnp.split(qk, 2, axis=-1)
        q = _split_heads(q, h)
        k = _split_heads(k, h)
        vg = _split_heads(v, h)
        dots = jnp.einsum('bhid,bhjd->bhij', q, k)
        g_bias = pos_embedding[L - 1 - jnp.arange(L)]
        dots = dots + g_bias
        attn = jax.nn.softmax(dots, axis=-1)
        out = jnp.einsum('bhij,bhjd->bhid', attn, vg)
        out = out.transpose(0, 2, 1, 3).reshape(b, L, h * HEAD_DIM)
        return (wout + out) @ w_out + b_out

    def _L1_ffn_ref(x, Wr, Wg, Wu, Wd, Sg, Su, Sd):
        import jax, jax.numpy as jnp
        import numpy as np
        B, S, D = (2, 256, 128)
        E, K, F = (16, 2, 64)
        FS = 128
        b, s, d = x.shape
        T = b * s
        xf = x.reshape(T, d)
        shared = jax.nn.silu(xf @ Sg) * (xf @ Su) @ Sd
        probs = jax.nn.softmax(xf @ Wr, axis=-1)
        topk_p, topk_i = jax.lax.top_k(probs, K)
        n_exp = Wr.shape[1]
        cw = jnp.zeros((T, n_exp), x.dtype).at[jnp.arange(T)[:, None], topk_i].add(topk_p)

        def step(acc, ew):
            wg, wu, wd, c = ew
            y = jax.nn.silu(xf @ wg) * (xf @ wu) @ wd
            return (acc + y * c[:, None], None)
        routed, _ = jax.lax.scan(step, jnp.zeros_like(xf), (Wg, Wu, Wd, cw.T))
        return (routed + shared).reshape(b, s, d)
    x = L0_attn_hidden_states
    x = x + _layernorm(_L0_attn_ref(_layernorm(x, axis=-1), L0_attn_Wq, L0_attn_bq, L0_attn_Wk, L0_attn_bk, L0_attn_Wv, L0_attn_bv, L0_attn_Wo, L0_attn_bo, L0_attn_ln_w, L0_attn_ln_b), axis=-1)
    x = x + _layernorm(_L0_ffn_ref(_layernorm(x, axis=-1), L0_ffn_shared_w1, L0_ffn_shared_w2, L0_ffn_experts_w1, L0_ffn_experts_w2, L0_ffn_gate_w), axis=-1)
    x = x + _layernorm(_L1_attn_ref(_layernorm(x, axis=-1), L1_attn_w_v, L1_attn_b_v, L1_attn_w_wqk, L1_attn_b_wqk, L1_attn_w_qk, L1_attn_b_qk, L1_attn_w_out, L1_attn_b_out, L1_attn_w_pos_embedding, L1_attn_pos_embedding), axis=-1)
    x = x + _layernorm(_L1_ffn_ref(_layernorm(x, axis=-1), L1_ffn_Wr, L1_ffn_Wg, L1_ffn_Wu, L1_ffn_Wd, L1_ffn_Sg, L1_ffn_Su, L1_ffn_Sd), axis=-1)
    return x

_drawn_inputs = setup_inputs


def setup_inputs(seed=0):
    import zlib

    import numpy as np

    out = dict(_drawn_inputs(seed))
    spreads = {'L0_attn_bq': (0.0, 0.8),
     'L0_attn_bk': (0.0, 0.8),
     'L0_attn_bv': (0.0, 0.1),
     'L0_attn_bo': (0.0, 0.1),
     'L0_attn_ln_w': (1.0, 0.551),
     'L0_attn_ln_b': (0.0, 0.1)}
    factors = {'L0_attn_Wq': 4.756,
     'L1_attn_w_wqk': 4.695,
     'L1_attn_b_wqk': 8.0,
     'L1_attn_w_qk': 2.945,
     'L1_attn_b_qk': 8.0}
    for name, (base, spread) in spreads.items():
        noise = np.random.default_rng([zlib.crc32(name.encode()), seed]).standard_normal(out[name].shape)
        drawn = base * np.exp(spread * noise) if base else spread * noise
        out[name] = jnp.asarray(drawn.astype(out[name].dtype))
    for name, factor in factors.items():
        out[name] = (out[name] * factor).astype(out[name].dtype)
    return out
```

```python
from contextlib import ExitStack

import numpy as np

import concourse.bass as bass
from concourse import mybir

F32 = mybir.dt.float32
F32R = mybir.dt.float32r
ALU = mybir.AluOpType
ACT = mybir.ActivationFunctionType
AX = mybir.AxisListType

P = 128
D = 128
B, S = 16, 256
TILES = B * S // P
TPB = S // P
H, HD = 16, 8
G = 4
NG = H // G
UNITS = B * NG
SLOT = 32
SHIFT, BIAS_HI, BIAS_LO, WIN_A, WIN_B = 24, 25, 26, 27, 28
EPS = 1e-5
FAR = -1.0e30
RING = 8


def clip(n, top):
    return min(max(n, 0), top)


def before(step, lead=0):
    return clip(-(-step // NG) + lead, B)


class Step:

    def __init__(self, k, i=None, first=1, size=2 * NG):
        self.k, self.i, self.first, self.size = k, i, first, size

    def at(self, count):
        n = count(self.k)
        if self.i is None:
            return n
        grow = count(self.k + self.size) - n
        if grow == 0:
            return n
        return (self.i - self.first) * grow + n


X_FIRST = 2
ROUND = 2 * NG


def wait(eng, sem, value):
    if not isinstance(value, int) or value > 0:
        eng.wait_ge(sem, value)


def tiles(st, lead):
    return bass.ds(st.at(lambda k: (k // NG + lead) * TPB * D), TPB * D)


def stacked(v):
    return v.rearrange("p n s -> p (n s)").bitcast(F32)


def hold(eng, sem, value, passed):
    wait(eng, sem, value)
    if not isinstance(value, int):
        eng.sem_inc(passed, 1)


def first_attention(nc, X, Z, ident, a):
    FIRST, LAST = -3 * NG, UNITS + 3 * NG
    LOOP = (1, 6)

    def steps(eng):
        for k in range(FIRST, LOOP[0] * ROUND):
            yield Step(k)
        with eng.Fori(*LOOP) as i:
            for j in range(ROUND):
                yield Step(LOOP[0] * ROUND + j, i, LOOP[0])
        for k in range(LOOP[1] * ROUND, LAST):
            yield Step(k)

    def unit(n):
        return 0 <= n < UNITS

    def batch(n):
        return 0 <= n < B

    with ExitStack() as ctx:
        def sb(name, shape, dt=F32):
            return ctx.enter_context(nc.sbuf_tensor("a0_" + name, shape, dt))

        def pb(name, shape):
            return ctx.enter_context(nc.psum_tensor("a0_" + name, shape, F32))

        def sem(name):
            return ctx.enter_context(nc.semaphore("a0_" + name))

        z1 = sb("z1", [P, TPB, D])
        qk = sb("qk", [P, 2, TPB, D])
        sq = sb("sq", [P, 2, TPB, D])
        ss = sb("ss", [P, 2 * TPB * H])
        rn = sb("rn", [P, 2 * TPB * H])
        vt = sb("vt", [P, 2, TPB, D])
        qt = sb("qt", [P, 2, TPB * H, SLOT], F32R)
        kt = sb("kt", [P, 2, TPB * H, SLOT], F32R)
        state = sb("state", [P, TPB * G, HD])
        qt2 = sb("qt2", [P, 2, TPB * G, SLOT], F32R)
        r1 = sb("r1", [P, TPB * G])
        r2 = sb("r2", [P, TPB * G])
        out2 = sb("out2", [P, 2, TPB, D])
        y = sb("y", [P, TPB, D])
        bn = sb("bn", [P, 2 * TPB, 6])
        mv_a = sb("mv_a", [P, 2 * TPB, 2])
        mv_b = sb("mv_b", [P, 2 * TPB, 2])
        rs_a = sb("rs_a", [P, 2 * TPB])
        rs_b = sb("rs_b", [P, 2 * TPB])
        ve = sb("ve", [P, 2 * TPB])
        half = sb("half", [P, 2 * TPB * H])
        xT = sb("xT", [P, S])
        yT = sb("yT", [P, S])
        ks = sb("ks", [P, 2, S], F32R)
        kpad = sb("kpad", [P, RING, G, S], F32R)
        qs1 = sb("qs1", [P, RING, S], F32R)
        qs2 = sb("qs2", [P, 2, S], F32R)
        qs2m = sb("qs2m", [P, S], F32R)
        v32 = sb("v32", [P, RING, TPB, G, SLOT])
        p1 = sb("p1", [P, G, TPB, S])
        p2 = sb("p2", [P, G, TPB, S])
        o1 = sb("o1", [P, S])
        o2 = sb("o2", [P, S])
        ps_s = pb("ps_s", [P, 2, 1024])
        ps_m = pb("ps_m", [P, 2, S])
        ps_o = pb("ps_o", [P, 512])[:, 0:S]
        ps_a = pb("ps_a", [P, 512])[:, 0:S]
        ps_b = pb("ps_b", [P, 512])[:, 0:S]

        tiles_ready = sem("tiles_ready")
        scores_full, exp_done = sem("scores_full"), sem("exp_done")
        o1_full, o1_copied = sem("o1_full"), sem("o1_copied")
        o2_full, o2_copied = sem("o2_full"), sem("o2_copied")
        max_full, max_done = sem("max_full"), sem("max_done")
        a_full, a_done = sem("a_full"), sem("a_done")
        b_full, b_done = sem("b_full"), sem("b_done")
        qt2_ready = sem("qt2_ready")
        kpad_loaded = [sem(f"kpad_loaded{n}") for n in range(RING)]
        v_ready = sem("v_ready")
        recip1, state_ready, recip2 = sem("recip1"), sem("state_ready"), sem("recip2")
        z1_ready, stats_a, stats_b = sem("z1_ready"), sem("stats_a"), sem("stats_b")
        rs_a_ready, rs_b_ready, pool_ve = sem("rs_a_ready"), sem("rs_b_ready"), sem("pool_ve")
        squares, norms, clipped, rn_ready = sem("squares"), sem("norms"), sem("clipped"), sem("rn_ready")
        qk_scaled, parts_hi, stacks_ready = sem("qk_scaled"), sem("parts_hi"), sem("stacks_ready")
        bn_done, y_ready, x_part, x_new, z_new = (
            sem("bn_done"), sem("y_ready"), sem("x_part"), sem("x_new"), sem("z_new"))
        z0_ready = sem("z0_ready")
        consts = sem("consts")
        passed = sem("passed")
        block = ctx.enter_context(nc.Block())

        def a_count(k, task):
            n = 2 * clip(k + NG, UNITS) + before(k, 2) + before(k, -2)
            live = [("K", unit(k + NG)), ("Q", unit(k + NG)),
                    ("xT", k % NG == 0 and batch(k // NG + 2)), ("yT", k % NG == 0 and batch(k // NG - 2))]
            for name, on in live:
                n += on
                if name == task:
                    return n

        def b_count(k, task):
            n = (clip(k - 1, UNITS) * 2 + clip(k - 2, UNITS) + clip(k - 4, UNITS)
                 + 3 * before(k - 1, 2) + before(k - 1, -2))
            b = k // NG
            live = [("O1", unit(k - 1)), ("qp", k % NG == 1 and batch(b + 2)), ("kp", k % NG == 1 and batch(b + 2)),
                    ("vp", k % NG == 1 and batch(b + 2)), ("T1", unit(k - 1)), ("O2", unit(k - 4)),
                    ("op", k % NG == 1 and batch(b - 2)), ("T2", unit(k - 2))]
            for name, on in live:
                n += on
                if name == task:
                    return n

        def chunks(k, which):
            n = 2 * clip(k, UNITS) + 2 * clip(k - 3, UNITS)
            order = [unit(k), unit(k), unit(k - 3), unit(k - 3)]
            return n + sum(order[:which + 1])

        def bn_count(k, which):
            n = before(k - 2, -2) + before(k - 2, 3) + before(k - 3, -2) + before(k - 3, 3)
            return n + batch(k // NG - 2) + (which == 1)

        @block.sync
        def _(sp):
            a["load"](sp)
            for st in steps(sp):
                k = st.k
                if not unit(k + NG):
                    continue
                hold(sp, a_done, st.at(lambda k: a_count(k, "K")), passed)
                if k - NG >= 0:
                    hold(sp, o2_full, st.at(lambda k: k - NG + 1), passed)
                u = k + NG
                for j in range(G):
                    rows = slice(SLOT * j, SLOT * j + SLOT)
                    sp.dma_start(kpad[rows, u % RING, j, :].bitcast(F32), ks[rows, u % 2, :].bitcast(F32)
                                 ).then_inc(kpad_loaded[u % RING], 16)

        @block.tensor
        def _(pe):
            pe.wait_ge(consts, 5)
            pe.wait_ge(a["loaded"], 16 * a["loads"])

            def wait_b(st, task):
                wait(pe, b_done, st.at(lambda k: b_count(k, task) - 1))

            def wait_a(st, task):
                wait(pe, a_done, st.at(lambda k: a_count(k, task) - 1))

            def score_chunk(st, which, q):
                u = st.k if which < 2 else st.k - 3
                wait(pe, exp_done, st.at(lambda k: chunks(k, which) - 2))
                n = chunks(st.k, which) - 1
                for jj in range(2):
                    j = 2 * (which % 2) + jj
                    for t in range(TPB):
                        last = nc.tensor.matmul(ps_s[:, n % 2, jj * 512 + t * S:jj * 512 + (t + 1) * S],
                                                kpad[:, u % RING, j, t * P:(t + 1) * P], q, start=True, stop=True)
                last.then_inc(scores_full, 1)

            def maxima(st, part):
                if not unit(st.k - 2):
                    return
                u, t, c = st.k - 2, part // 2, part % 2
                wait(pe, max_done, st.at(lambda k: 4 * clip(k - 2, UNITS) + part))
                nc.tensor.matmul(ps_m[:, :, :].rearrange("p a b -> p (a b)"), qs2[:, u % 2, t * P:(t + 1) * P],
                                 kpad[:, u % RING, 2 * c:2 * c + 2, :].rearrange("p a b -> p (a b)"),
                                 start=True, stop=True).then_inc(max_full, 1)

            def attend(u, probs, full):
                for t in range(TPB):
                    for j in range(G):
                        last = nc.tensor.matmul(ps_o[SLOT * j:SLOT * (j + 1), :], v32[:, u % RING, t, j, :],
                                                probs[:, j, t, :], start=t == 0, stop=t == TPB - 1)
                last.then_inc(full, 1)

            def transposes(out, parts, done):
                for t in range(TPB):
                    last = nc.tensor.transpose(out[:, t * P:(t + 1) * P], parts(t), ident[:, :])
                last.then_inc(done, 1)

            for st in steps(pe):
                k = st.k
                b, r = k // NG, k % NG
                if unit(k):
                    pe.wait_ge(kpad_loaded[k % RING], st.at(lambda k: 64 * (k // RING + 1)))
                    pe.wait_ge(a_done, st.at(lambda k: a_count(k - NG, "Q")))
                    score_chunk(st, 0, qs1[:, k % RING, :])
                if unit(k - 1):
                    wait_b(st, "O1")
                    pe.wait_ge(o1_copied, st.at(lambda k: k))
                    transposes(ps_b, lambda t: o1[:, t * P:(t + 1) * P], b_full)
                if unit(k - 2):
                    pe.wait_ge(b_done, st.at(lambda k: b_count(k - 1, "T1")))
                maxima(st, 0)
                if unit(k):
                    score_chunk(st, 1, qs1[:, k % RING, :])
                if r == 1 and batch(b + 2):
                    pe.wait_ge(a_done, st.at(lambda k: a_count(k - 1, "xT")))
                    for n, task in enumerate(("qp", "kp", "vp")):
                        wait_b(st, task)
                        for t in range(TPB):
                            last = nc.tensor.matmul(ps_b[:, t * P:(t + 1) * P], xT[:, t * P:(t + 1) * P],
                                                    a["wqkv"][:, n * D:(n + 1) * D], start=True, stop=True)
                        last.then_inc(b_full, 1)
                maxima(st, 1)
                if unit(k - 3):
                    pe.wait_ge(b_done, st.at(lambda k: b_count(k - 1, "T2")))
                    score_chunk(st, 2, qs2m[:, :])
                if unit(k - 1):
                    wait_b(st, "T1")
                    pe.wait_ge(qt2_ready, st.at(lambda k: k))
                    transposes(ps_b, lambda t: stacked(qt2[:, (k - 1) % 2, t * G:(t + 1) * G, :]), b_full)
                maxima(st, 2)
                if unit(k):
                    pe.wait_ge(exp_done, st.at(lambda k: chunks(k, 1)))
                    pe.wait_ge(v_ready, st.at(lambda k: k + 1))
                    wait(pe, o2_copied, st.at(lambda k: clip(k - 3, UNITS)))
                    attend(k, p1, o1_full)
                maxima(st, 3)
                if unit(k - 3):
                    score_chunk(st, 3, qs2m[:, :])
                if unit(k - 4):
                    wait_b(st, "O2")
                    pe.wait_ge(o2_copied, st.at(lambda k: k - 3))
                    transposes(ps_b, lambda t: o2[:, t * P:(t + 1) * P], b_full)
                if unit(k + NG):
                    nb, g = (k + NG) // NG, r
                    pe.wait_ge(stacks_ready, st.at(lambda k: 2 * ((k + NG) // NG + 1)))
                    wait_a(st, "K")
                    transposes(ps_a, lambda t: stacked(kt[:, nb % 2, t * H + g * G:t * H + (g + 1) * G, :]), a_full)
                    wait_a(st, "Q")
                    transposes(ps_a, lambda t: stacked(qt[:, nb % 2, t * H + g * G:t * H + (g + 1) * G, :]), a_full)
                if r == 0 and batch(b + 2):
                    pe.wait_ge(z1_ready, st.at(lambda k: k // NG + 3))
                    wait_a(st, "xT")
                    transposes(ps_a, lambda t: z1[:, t, :], a_full)
                if r == 0 and batch(b - 2):
                    pe.wait_ge(b_done, st.at(lambda k: b_count(k - 1, "O2")))
                    wait_a(st, "yT")
                    transposes(ps_a, lambda t: out2[:, b % 2, t, :], a_full)
                if r == 1 and batch(b - 2):
                    pe.wait_ge(a_done, st.at(lambda k: a_count(k - 1, "yT")))
                    wait_b(st, "op")
                    for t in range(TPB):
                        last = nc.tensor.matmul(ps_b[:, t * P:(t + 1) * P], yT[:, t * P:(t + 1) * P],
                                                a["wo"][:, :], start=True, stop=True)
                    last.then_inc(b_full, 1)
                if unit(k - 2):
                    wait_b(st, "T2")
                    pe.wait_ge(max_done, st.at(lambda k: 4 * (k - 1)))
                    transposes(ps_b, lambda t: stacked(qt2[:, k % 2, t * G:(t + 1) * G, :]), b_full)
                if unit(k - 3):
                    pe.wait_ge(exp_done, st.at(lambda k: chunks(k, 3)))
                    wait(pe, o1_copied, st.at(lambda k: clip(k + 1, UNITS)))
                    attend(k - 3, p2, o2_full)

        @block.scalar
        def _(act):
            def exps(st, which, probs, full, used):
                act.wait_ge(scores_full, st.at(lambda k: chunks(k, which)))
                if which % 2 == 0:
                    wait(act, full, st.at(used))
                n = chunks(st.k, which) - 1
                c = which % 2
                nc.scalar.activation(probs[:, 2 * c:2 * c + 2, :, :].rearrange("p a b c -> p (a b c)"),
                                     ps_s[:, n % 2, :], ACT.Exp).then_inc(exp_done, 1)

            act.wait_ge(consts, 5)
            act.wait_ge(a["loaded"], 16 * a["loads"])
            for st in steps(act):
                k = st.k
                b, r = k // NG, k % NG
                if unit(k):
                    exps(st, 0, p1, o1_full, lambda k: k)
                if unit(k - 4):
                    act.wait_ge(o2_full, st.at(lambda k: k - 3))
                    nc.scalar.copy(o2[:, :], ps_o).then_inc(o2_copied, 1)
                if unit(k):
                    exps(st, 1, p1, o1_full, lambda k: k)
                if unit(k - 3):
                    exps(st, 2, p2, o2_full, lambda k: k - 3)
                if unit(k):
                    act.wait_ge(o1_full, st.at(lambda k: k + 1))
                    nc.scalar.copy(o1[:, :], ps_o).then_inc(o1_copied, 1)
                if unit(k - 3):
                    exps(st, 3, p2, o2_full, lambda k: k - 3)
                if unit(k + NG):
                    u = k + NG
                    act.wait_ge(a_full, st.at(lambda k: a_count(k, "K")))
                    if unit(u - 2):
                        act.wait_ge(kpad_loaded[(u - 2) % RING], st.at(lambda k: 64 * ((k + NG - 2) // RING + 1)))
                    nc.scalar.copy(ks[:, u % 2, :], ps_a).then_inc(a_done, 1)
                    act.wait_ge(a_full, st.at(lambda k: a_count(k, "Q")))
                    nc.scalar.copy(qs1[:, u % RING, :], ps_a).then_inc(a_done, 1)
                if r == 0 and batch(b + 2):
                    act.wait_ge(a_full, st.at(lambda k: a_count(k, "xT")))
                    nc.scalar.activation(xT[:, :], ps_a, ACT.Identity, scale=a["ln_w"][:, 0:1],
                                         bias=a["ln_b"][:, 0:1]).then_inc(a_done, 1)
                if r == 0 and batch(b - 2):
                    act.wait_ge(a_full, st.at(lambda k: a_count(k, "yT")))
                    nc.scalar.copy(yT[:, :], ps_a).then_inc(a_done, 1)

        @block.vector
        def _(dve):
            nc.vector.memset(mv_a[:, :, :], 1.0).then_inc(consts, 1)
            nc.vector.memset(mv_b[:, :, :], 1.0).then_inc(consts, 1)
            dve.wait_ge(consts, 5)
            dve.wait_ge(a["loaded"], 16 * a["loads"])

            def normalise(x, mv, rs, n, out):
                for t in range(TPB):
                    last = nc.vector.tensor_scalar(out(t), x(t), mv[:, n + t, 0:1], rs[:, n + t:n + t + 1],
                                                   ALU.subtract, ALU.mult)
                return last

            def heads_out(v):
                return v.rearrange("p (n s) -> p n s", s=SLOT)

            for st in steps(dve):
                k = st.k
                b, r = k // NG, k % NG
                if unit(k - 1):
                    dve.wait_ge(b_full, st.at(lambda k: b_count(k, "O1")))
                    src = heads_out(ps_b)
                    nc.vector.reciprocal(r1[:, :], src[:, :, HD]).then_inc(recip1, 1)
                    dve.wait_ge(recip1, st.at(lambda k: k))
                    new = qt2[:, (k - 1) % 2, :, :]
                    nc.vector.memset(new[:, :, SHIFT].bitcast(F32), 0.0)
                    nc.vector.tensor_tensor(state[:, :, :], src[:, :, 0:HD],
                                            r1[:, :].unsqueeze(2).to_broadcast([P, TPB * G, HD]), ALU.mult)
                    nc.vector.tensor_tensor(
                        new[:, :, 0:2 * HD].rearrange("p n (c d) -> p n c d", c=2),
                        src[:, :, 0:HD].unsqueeze(2).to_broadcast([P, TPB * G, 2, HD]),
                        r1[:, :].unsqueeze(2).unsqueeze(3).to_broadcast([P, TPB * G, 2, HD]),
                        ALU.mult).then_inc(b_done, 1)
                    dve.wait_ge(b_done, st.at(lambda k: b_count(k, "O1")))
                    nc.vector.tensor_tensor(new[:, :, 2 * HD:3 * HD], state[:, :, :],
                                            new[:, :, 0:HD].bitcast(F32), ALU.subtract).then_inc(qt2_ready, 1)
                if r == 1 and batch(b + 2):
                    for n, task in enumerate(("qp", "kp", "vp")):
                        dve.wait_ge(b_full, st.at(lambda k: b_count(k, task)))
                        bias = a["bqkv"][:, n * D:(n + 1) * D].unsqueeze(1).to_broadcast([P, TPB, D])
                        if n == 2:
                            wait(dve, v_ready, st.at(lambda k: NG * (k // NG + 1)))
                        dst = vt[:, b % 2, :, :] if n == 2 else qk[:, n, :, :]
                        nc.vector.tensor_tensor(dst, ps_b.rearrange("p (t d) -> p t d", d=D), bias,
                                                ALU.add).then_inc(b_done, 1)
                    dve.wait_ge(b_done, st.at(lambda k: b_count(k, "kp")))
                    flat = "p a t d -> p (a t d)"
                    wait(dve, stacks_ready, st.at(lambda k: 2 * (k // NG + 2)))
                    nc.vector.tensor_tensor(sq[:].rearrange(flat), qk[:].rearrange(flat), qk[:].rearrange(flat),
                                            ALU.mult).then_inc(squares, 1)
                    dve.wait_ge(squares, st.at(lambda k: k // NG + 3))
                    nc.vector.tensor_reduce(ss[:, :], sq[:].rearrange("p a t (h d) -> p (a t h) d", d=HD), AX.X,
                                            ALU.add).then_inc(norms, 1)
                if r == 2 and batch(b - 2):
                    dve.wait_ge(b_done, st.at(lambda k: b_count(k - 1, "op")))
                    zz = Z[:, tiles(st, -2)]
                    yy = y[:].rearrange("p t d -> p (t d)")
                    nc.vector.tensor_tensor(yy, yy, zz, ALU.add).then_inc(y_ready, 1)
                    hold(dve, y_ready, st.at(lambda k: k // NG - 1), passed)
                    for t in range(TPB):
                        last = nc.vector.bn_stats(bn[:, t, :], y[:, t, :])
                    last.then_inc(bn_done, 1)
                    hold(dve, bn_done, st.at(lambda k: bn_count(k, 0)), passed)
                    for t in range(TPB):
                        last = nc.vector.bn_aggr(mv_a[:, t, :], bn[:, t, :])
                    if not batch(b + 3):
                        last.then_inc(stats_a, 1)
                if r == 2 and batch(b + 3):
                    dve.wait_ge(a["x_loaded"][b + 3 >= X_FIRST], 16)
                    xx = X[:, tiles(st, 3)].rearrange("p (t d) -> p t d", d=D)
                    for t in range(TPB):
                        last = nc.vector.bn_stats(bn[:, TPB + t, :], xx[:, t, :])
                    last.then_inc(bn_done, 1)
                    hold(dve, bn_done, st.at(lambda k: bn_count(k, 1)), passed)
                    for t in range(TPB):
                        last = nc.vector.bn_aggr(mv_a[:, TPB + t, :], bn[:, TPB + t, :])
                    last.then_inc(stats_a, 1)
                if r == 3 and batch(b - 2):
                    dve.wait_ge(rs_a_ready, st.at(lambda k: k // NG + 4))
                    normalise(lambda t: y[:, t, :], mv_a, rs_a, 0, lambda t: y[:, t, :]).then_inc(x_part, 1)
                    dve.wait_ge(x_part, st.at(lambda k: k // NG - 1))
                    xx = X[:, tiles(st, -2)]
                    nc.vector.tensor_tensor(xx, xx, y[:].rearrange("p t d -> p (t d)"), ALU.add).then_inc(x_new, 1)
                    hold(dve, x_new, st.at(lambda k: k // NG - 1), passed)
                    xx = xx.rearrange("p (t d) -> p t d", d=D)
                    for t in range(TPB):
                        last = nc.vector.bn_stats(bn[:, t, :], xx[:, t, :])
                    last.then_inc(bn_done, 1)
                    hold(dve, bn_done, st.at(lambda k: bn_count(k, 0)), passed)
                    for t in range(TPB):
                        last = nc.vector.bn_aggr(mv_b[:, t, :], bn[:, t, :])
                    if not batch(b + 3):
                        last.then_inc(stats_b, 1)
                if r == 3 and batch(b + 3):
                    dve.wait_ge(rs_a_ready, st.at(lambda k: k // NG + 4))
                    zz = Z[:, tiles(st, 3)].rearrange("p (t d) -> p t d", d=D)
                    xx = X[:, tiles(st, 3)].rearrange("p (t d) -> p t d", d=D)
                    normalise(lambda t: xx[:, t, :], mv_a, rs_a, TPB, lambda t: zz[:, t, :]).then_inc(z0_ready, 1)
                    hold(dve, z0_ready, st.at(lambda k: k // NG + 4), passed)
                    for t in range(TPB):
                        last = nc.vector.bn_stats(bn[:, TPB + t, :], zz[:, t, :])
                    last.then_inc(bn_done, 1)
                    hold(dve, bn_done, st.at(lambda k: bn_count(k, 1)), passed)
                    for t in range(TPB):
                        last = nc.vector.bn_aggr(mv_b[:, TPB + t, :], bn[:, TPB + t, :])
                    last.then_inc(stats_b, 1)
                if r == 3 and batch(b + 2):
                    dve.wait_ge(rn_ready, st.at(lambda k: 4 * (k // NG + 3)))
                    nc.vector.tensor_tensor(
                        sq[:].rearrange("p a t (h d) -> p (a t h) d", d=HD),
                        qk[:].rearrange("p a t (h d) -> p (a t h) d", d=HD),
                        rn[:, :].unsqueeze(2).to_broadcast([P, 2 * TPB * H, HD]), ALU.mult).then_inc(qk_scaled, 1)
                def maxima(t):
                    for c in range(2):
                        dve.wait_ge(max_full, st.at(lambda k: 4 * clip(k - 2, UNITS) + 2 * t + c + 1))
                        first = t * G + 2 * c
                        nc.vector.tensor_reduce(qt2[:, k % 2, first:first + 2, SHIFT],
                                                ps_m[:, :, :], AX.X, ALU.max,
                                                negate=True).then_inc(max_done, 1)

                if unit(k - 2):
                    maxima(0)
                if unit(k - 1):
                    dve.wait_ge(b_full, st.at(lambda k: b_count(k, "T1")))
                    nc.vector.tensor_copy(qs2[:, (k - 1) % 2, :], ps_b).then_inc(b_done, 1)
                if unit(k - 2):
                    maxima(1)
                if unit(k - 4):
                    dve.wait_ge(b_full, st.at(lambda k: b_count(k, "O2")))
                    src = heads_out(ps_b)
                    nc.vector.reciprocal(r2[:, :], src[:, :, HD]).then_inc(recip2, 1)
                    dve.wait_ge(recip2, st.at(lambda k: k - 3))
                    dst = out2[:, (b - 1) % 2, :, r * G * HD:(r + 1) * G * HD]
                    nc.vector.tensor_tensor(
                        dst.rearrange("p t (h d) -> p t h d", d=HD),
                        src[:, :, 0:HD].rearrange("p (t h) d -> p t h d", t=TPB),
                        r2[:, :].rearrange("p (t h) -> p t h", t=TPB).unsqueeze(3).to_broadcast([P, TPB, G, HD]),
                        ALU.mult).then_inc(b_done, 1)
                if r == 1 and batch(b - 2):
                    dve.wait_ge(b_full, st.at(lambda k: b_count(k, "op")))
                    nc.vector.tensor_tensor(y[:, :, :], ps_b.rearrange("p (t d) -> p t d", d=D),
                                            a["bo"][:, :].unsqueeze(1).to_broadcast([P, TPB, D]),
                                            ALU.add).then_inc(b_done, 1)
                if unit(k - 2):
                    dve.wait_ge(b_full, st.at(lambda k: b_count(k, "T2")))
                    nc.vector.tensor_copy(qs2m[:, :], ps_b).then_inc(b_done, 1)
                if r == 3 and batch(b - 2):
                    dve.wait_ge(rs_b_ready, st.at(lambda k: k // NG + 4))
                    zz = Z[:, tiles(st, -2)].rearrange("p (t d) -> p t d", d=D)
                    xx = X[:, tiles(st, -2)].rearrange("p (t d) -> p t d", d=D)
                    normalise(lambda t: xx[:, t, :], mv_b, rs_b, 0, lambda t: zz[:, t, :]).then_inc(z_new, 1)
                if r == 3 and batch(b + 3):
                    dve.wait_ge(rs_b_ready, st.at(lambda k: k // NG + 4))
                    if batch(b + 2):
                        dve.wait_ge(a_done, st.at(lambda k: a_count(k - 3, "xT")))
                    zz = Z[:, tiles(st, 3)].rearrange("p (t d) -> p t d", d=D)
                    normalise(lambda t: zz[:, t, :], mv_b, rs_b, TPB, lambda t: z1[:, t, :]).then_inc(z1_ready, 1)
            dve.wait_ge(z_new, B)

        @block.gpsimd
        def _(pool):
            nc.gpsimd.memset(half[:, :], -0.5)
            nc.gpsimd.memset(kpad[:].rearrange("p a b c -> p (a b c)").bitcast(F32), 0.0)
            nc.gpsimd.memset(v32[:].rearrange("p a b c d -> p (a b c d)"), 0.0).then_inc(pool_ve, 1)
            nc.gpsimd.memset(qt[:].rearrange("p a b c -> p (a b c)").bitcast(F32), 0.0)
            nc.gpsimd.memset(kt[:].rearrange("p a b c -> p (a b c)").bitcast(F32), 0.0).then_inc(pool_ve, 1)
            nc.gpsimd.memset(qt2[:].rearrange("p a b c -> p (a b c)").bitcast(F32), 0.0).then_inc(consts, 1)
            pool.wait_ge(pool_ve, 2)
            nc.gpsimd.memset(v32[:, :, :, :, HD].rearrange("p a b c -> p (a b c)"), 1.0).then_inc(consts, 1)
            nc.gpsimd.memset(kt[:, :, :, SHIFT].bitcast(F32), 1.0).then_inc(consts, 1)
            pool.wait_ge(consts, 5)

            def rstd(st, stats, mv, rs, ready, n):
                hold(pool, stats, st.at(n), passed)
                nc.gpsimd.tensor_scalar(ve[:, :], mv[:, :, 1], EPS, None, ALU.add).then_inc(pool_ve, 1)
                hold(pool, pool_ve, st.at(lambda k: 2 + 2 * (k // NG + 3) + k % NG - 1), passed)
                nc.gpsimd.tensor_tensor(rs[:, :], ve[:, :], half[:, 0:2 * TPB], ALU.pow).then_inc(ready, 1)

            def norm_powers(st, part):
                c = 2 * TPB * H // 4
                nc.gpsimd.tensor_tensor(rn[:, part * c:(part + 1) * c], ss[:, part * c:(part + 1) * c],
                                        half[:, 0:c], ALU.pow).then_inc(rn_ready, 1)

            for st in steps(pool):
                k = st.k
                b, r = k // NG, k % NG
                if unit(k + NG):
                    u = k + NG
                    hold(pool, b_done, st.at(lambda k: b_count(NG * (k // NG - 1) + 1, "vp")), passed)
                    hold(pool, o2_full, st.at(lambda k: clip(k - NG + 1, UNITS)), passed)
                    hs = slice(r * G * HD, (r + 1) * G * HD)
                    nc.gpsimd.tensor_copy(v32[:, u % RING, :, :, 0:HD],
                                          vt[:, (b + 1) % 2, :, hs].rearrange("p t (h d) -> p t h d", d=HD)
                                          ).then_inc(v_ready, 1)
                if r == 1 and batch(b + 2):
                    hold(pool, norms, st.at(lambda k: k // NG + 3), passed)
                    nc.gpsimd.tensor_scalar(ss[:, :], ss[:, :], 1e-24, None, ALU.max).then_inc(clipped, 1)
                    hold(pool, clipped, st.at(lambda k: k // NG + 3), passed)
                    norm_powers(st, 0)
                    norm_powers(st, 1)
                if r == 2 and batch(b + 2):
                    norm_powers(st, 2)
                if r == 2 and (batch(b - 2) or batch(b + 3)):
                    rstd(st, stats_a, mv_a, rs_a, rs_a_ready, lambda k: k // NG + 4)
                if r == 2 and batch(b + 2):
                    norm_powers(st, 3)
                if r == 3 and (batch(b - 2) or batch(b + 3)):
                    rstd(st, stats_b, mv_b, rs_b, rs_b_ready, lambda k: k // NG + 4)
                if r == 3 and batch(b + 2):
                    hold(pool, qk_scaled, st.at(lambda k: k // NG + 3), passed)
                    if k >= 0:
                        hold(pool, a_done, st.at(lambda k: a_count(k - NG, "Q")), passed)
                    val = sq[:].rearrange("p a t (h d) -> p a (t h) d", d=HD)
                    n = TPB * H
                    qd, kd = qt[:, b % 2, :, :], kt[:, b % 2, :, :]
                    nc.gpsimd.tensor_copy(qd[:, :, 0:2 * HD].rearrange("p n (c d) -> p n c d", c=2),
                                          val[:, 0, :, :].unsqueeze(2).to_broadcast([P, n, 2, HD]))
                    nc.gpsimd.tensor_copy(
                        kd[:, :, 0:4 * HD].rearrange("p n (c d) -> p n c d", c=2)[:, :, :, 0:HD],
                        val[:, 1, :, :].unsqueeze(2).to_broadcast([P, n, 2, HD])).then_inc(parts_hi, 1)
                    hold(pool, parts_hi, st.at(lambda k: k // NG + 3), passed)
                    nc.gpsimd.tensor_tensor(qd[:, :, 2 * HD:3 * HD], val[:, 0, :, :], qd[:, :, 0:HD].bitcast(F32),
                                            ALU.subtract).then_inc(stacks_ready, 1)
                    nc.gpsimd.tensor_tensor(kd[:, :, HD:2 * HD], val[:, 1, :, :], kd[:, :, 0:HD].bitcast(F32),
                                            ALU.subtract).then_inc(stacks_ready, 1)


def second_attention(nc, X, Z, ident, a):
    FIRST, LAST = -2 * NG, UNITS + 2 * NG
    LOOP = (1, 7)
    KEEP = 4
    W = S // 4
    SCALE = float(HD) ** -0.5
    WINDOWED, GLOBAL = 0, 1

    def steps(eng):
        for k in range(FIRST, LOOP[0] * ROUND):
            yield Step(k)
        with eng.Fori(*LOOP) as i:
            for j in range(ROUND):
                yield Step(LOOP[0] * ROUND + j, i, LOOP[0])
        for k in range(LOOP[1] * ROUND, LAST):
            yield Step(k)

    def unit(n):
        return 0 <= n < UNITS

    def batch(n):
        return 0 <= n < B

    with ExitStack() as ctx:
        def sb(name, shape, dt=F32):
            return ctx.enter_context(nc.sbuf_tensor("a1_" + name, shape, dt))

        def pb(name):
            return ctx.enter_context(nc.psum_tensor("a1_" + name, [P, 512], F32))

        def sem(name):
            return ctx.enter_context(nc.semaphore("a1_" + name))

        proj = sb("proj", [P, 4, TPB, D])
        vt = sb("vt", [P, 2, TPB, D])
        qt = sb("qt", [P, 2, 2, TPB * H, SLOT], F32R)
        kt = sb("kt", [P, 2, 2, TPB * H, SLOT], F32R)
        rg, rw = sb("rg", [P, TPB * G]), sb("rw", [P, TPB * G])
        og, ow = sb("og", [P, TPB * G, HD]), sb("ow", [P, TPB * G, HD])
        out = sb("out", [P, 2, TPB, D])
        y = sb("y", [P, TPB, D])
        bn = sb("bn", [P, TPB, 6])
        mv_y, mv_x = sb("mv_y", [P, TPB, 2]), sb("mv_x", [P, TPB, 2])
        rs_y, rs_x = sb("rs_y", [P, TPB]), sb("rs_x", [P, TPB])
        ve = sb("ve", [P, TPB])
        half = sb("half", [P, TPB])
        bias_hi, bias_lo = sb("bias_hi", [P, TPB + 1], F32R), sb("bias_lo", [P, TPB + 1], F32R)
        bwq = sb("bwq", [P, D])
        zc = sb("zc", [P, S])
        xT, yT = sb("xT", [P, S]), sb("yT", [P, S])
        ks = sb("ks", [P, 2, 2, S], F32R)
        kpad = sb("kpad", [P, KEEP, 2, G, S], F32R)
        qs = sb("qs", [P, 2, 2, S], F32R)
        qsm = sb("qsm", [P, 2, S], F32R)
        v32 = sb("v32", [P, KEEP, TPB, G, SLOT])
        pg = sb("pg", [P, G, TPB, S])
        pw = sb("pw", [P, G, TPB, P])
        otg, otw = sb("otg", [P, S]), sb("otw", [P, S])
        ps_s = ctx.enter_context(nc.psum_tensor("a1_ps_s", [P, 2, 1024], F32))
        ps_m, ps_o = pb("ps_m"), pb("ps_o")[:, 0:S]
        ps_a, ps_b = pb("ps_a")[:, 0:S], pb("ps_b")[:, 0:S]

        scores_full, exp_done = sem("scores_full"), sem("exp_done")
        g_full, g_copied, w_full, w_copied = sem("g_full"), sem("g_copied"), sem("w_full"), sem("w_copied")
        max_full, max_done = sem("max_full"), sem("max_done")
        a_full, a_done, b_full, b_done = sem("a_full"), sem("a_done"), sem("b_full"), sem("b_done")
        kpad_loaded = [sem(f"kpad_loaded{n}") for n in range(KEEP)]
        v_ready, stacks_ready, parts_hi = sem("v_ready"), sem("stacks_ready"), sem("parts_hi")
        recip_g, recip_w, zc_ready = sem("recip_g"), sem("recip_w"), sem("zc_ready")
        out_ready = sem("out_ready")
        bn_done, stats_y, stats_x = sem("bn_done"), sem("stats_y"), sem("stats_x")
        rs_y_ready, rs_x_ready, pool_step = sem("rs_y_ready"), sem("rs_x_ready"), sem("pool_step")
        x_part, x_new, z_new = sem("x_part"), sem("x_new"), sem("z_new")
        cleared, set_up, consts = sem("cleared"), sem("set_up"), sem("consts")
        passed = sem("passed")
        block = ctx.enter_context(nc.Block())

        def a_count(k, task):
            n = 2 * clip(k + 1, UNITS) + 2 * clip(k + 2, UNITS) + before(k - 2, 2) + before(k - 2, -1)
            b, r = k // NG, k % NG
            live = [("Qg", unit(k + 1)), ("Qw", unit(k + 1)), ("Kg", unit(k + 2)), ("Kw", unit(k + 2)),
                    ("xT", r == 2 and batch(b + 2)), ("yT", r == 2 and batch(b - 1))]
            for name, on in live:
                n += on
                if name == task:
                    return n

        def b_count(k, task):
            n = 2 * clip(k - 2, UNITS) + 2 * clip(k, UNITS) + 5 * before(k - 3, 2) + before(k - 3, -1)
            b, r = k // NG, k % NG
            live = [("Og", unit(k - 2)), ("Ow", unit(k - 2)), ("Mg", unit(k))]
            live += [(name, r == 3 and batch(b + 2)) for name in ("wq", "wk", "q", "k", "v")]
            live += [("op", r == 3 and batch(b - 1)), ("Mw", unit(k))]
            for name, on in live:
                n += on
                if name == task:
                    return n

        def chunk(k, which):
            return 3 * clip(k - 1, UNITS) + which + 1

        def maxes(k, part):
            return 6 * clip(k, UNITS) + part + 1

        @block.sync
        def _(sp):
            sp.wait_ge(consts, 3)
            for st in steps(sp):
                u = st.k + 2
                if not unit(u):
                    continue
                if unit(u - KEEP):
                    hold(sp, w_full, st.at(lambda k: k + 2 - KEEP + 1), passed)
                for kind, task in ((GLOBAL, "Kg"), (WINDOWED, "Kw")):
                    hold(sp, a_done, st.at(lambda k: a_count(k, task)), passed)
                    for j in range(G):
                        rows = slice(SLOT * j, SLOT * j + SLOT)
                        sp.dma_start(kpad[rows, u % KEEP, kind, j, :].bitcast(F32),
                                     ks[rows, u % 2, kind, :].bitcast(F32)).then_inc(kpad_loaded[u % KEEP], 16)

        @block.tensor
        def _(pe):
            def wait_a(st, task):
                wait(pe, a_done, st.at(lambda k: a_count(k, task) - 1))

            def wait_b(st, task):
                wait(pe, b_done, st.at(lambda k: b_count(k, task) - 1))

            def transposes(dst, parts, done):
                for t in range(TPB):
                    last = nc.tensor.transpose(dst[:, t * P:(t + 1) * P], parts(t), ident[:, :])
                last.then_inc(done, 1)

            def global_scores(st, c):
                u = st.k - 1
                wait(pe, exp_done, st.at(lambda k: chunk(k, c) - 2))
                n = chunk(st.k, c) - 1
                for jj in range(2):
                    for t in range(TPB):
                        last = nc.tensor.matmul(ps_s[:, n % 2, jj * 512 + t * S:jj * 512 + (t + 1) * S],
                                                kpad[:, u % KEEP, GLOBAL, 2 * c + jj, t * P:(t + 1) * P],
                                                qsm[:, GLOBAL, :], start=True, stop=True)
                last.then_inc(scores_full, 1)

            def window_scores(st):
                u = st.k - 1
                wait(pe, exp_done, st.at(lambda k: chunk(k, 2) - 2))
                n = chunk(st.k, 2) - 1
                for j in range(G):
                    for t in range(TPB):
                        tile = slice(t * P, (t + 1) * P)
                        last = nc.tensor.matmul(ps_s[:, n % 2, (j * TPB + t) * P:(j * TPB + t + 1) * P],
                                                kpad[:, u % KEEP, WINDOWED, j, tile], qsm[:, WINDOWED, tile],
                                                start=True, stop=True)
                last.then_inc(scores_full, 1)

            def maxima(st, part):
                if not unit(st.k):
                    return
                u = st.k
                wait(pe, max_done, st.at(lambda k: maxes(k, part) - 1))
                if part < 4:
                    t, c = part // 2, part % 2
                    nc.tensor.matmul(ps_m[:, :], qs[:, u % 2, GLOBAL, t * P:(t + 1) * P],
                                     kpad[:, u % KEEP, GLOBAL, 2 * c:2 * c + 2, :].rearrange("p a b -> p (a b)"),
                                     start=True, stop=True).then_inc(max_full, 1)
                else:
                    tile = slice((part - 4) * P, (part - 3) * P)
                    nc.tensor.matmul(ps_m[:, :].rearrange("p (a b) -> p a b", a=G), qs[:, u % 2, WINDOWED, tile],
                                     kpad[:, u % KEEP, WINDOWED, :, tile], start=True,
                                     stop=True).then_inc(max_full, 1)

            pe.wait_ge(consts, 3)
            for st in steps(pe):
                k = st.k
                b, r, m = k // NG, k % NG, k - 1
                if unit(m):
                    pe.wait_ge(b_done, st.at(lambda k: b_count(k - 1, "Mg")))
                    global_scores(st, 0)
                if unit(k - 2):
                    wait_b(st, "Og")
                    pe.wait_ge(g_copied, st.at(lambda k: k - 1))
                    transposes(ps_b, lambda t: otg[:, t * P:(t + 1) * P], b_full)
                if unit(k):
                    pe.wait_ge(kpad_loaded[k % KEEP], st.at(lambda k: 128 * (k // KEEP + 1)))
                    pe.wait_ge(a_done, st.at(lambda k: a_count(k - 1, "Qw")))
                maxima(st, 0)
                if unit(m):
                    global_scores(st, 1)
                maxima(st, 1)
                if unit(m):
                    pe.wait_ge(b_done, st.at(lambda k: b_count(k - 1, "Mw")))
                    window_scores(st)
                maxima(st, 2)
                if unit(k - 2):
                    wait_b(st, "Ow")
                    pe.wait_ge(w_copied, st.at(lambda k: k - 1))
                    transposes(ps_b, lambda t: otw[:, t * P:(t + 1) * P], b_full)
                if unit(k + 1):
                    u = k + 1
                    nb, g = u // NG, u % NG
                    for kind, task in ((GLOBAL, "Qg"), (WINDOWED, "Qw")):
                        if kind == GLOBAL:
                            pe.wait_ge(stacks_ready, st.at(lambda k: (k + 1) // NG + 1))
                        wait_a(st, task)
                        transposes(ps_a, lambda t: stacked(qt[:, nb % 2, kind, t * H + g * G:t * H + (g + 1) * G, :]),
                                   a_full)
                maxima(st, 3)
                if unit(m):
                    pe.wait_ge(exp_done, st.at(lambda k: chunk(k, 1)))
                    pe.wait_ge(v_ready, st.at(lambda k: k))
                    wait(pe, w_copied, st.at(lambda k: k - 1))
                    for t in range(TPB):
                        for j in range(G):
                            last = nc.tensor.matmul(ps_o[SLOT * j:SLOT * (j + 1), :], v32[:, m % KEEP, t, j, :],
                                                    pg[:, j, t, :], start=t == 0, stop=t == TPB - 1)
                    last.then_inc(g_full, 1)
                maxima(st, 4)
                if unit(k + 2):
                    u = k + 2
                    nb, g = u // NG, u % NG
                    for kind, task in ((GLOBAL, "Kg"), (WINDOWED, "Kw")):
                        if kind == GLOBAL:
                            pe.wait_ge(stacks_ready, st.at(lambda k: (k + 2) // NG + 1))
                        wait_a(st, task)
                        transposes(ps_a, lambda t: stacked(kt[:, nb % 2, kind, t * H + g * G:t * H + (g + 1) * G, :]),
                                   a_full)
                if unit(k):
                    wait_b(st, "Mg")
                    pe.wait_ge(max_done, st.at(lambda k: maxes(k, 3)))
                    transposes(ps_b, lambda t: stacked(qt[:, b % 2, GLOBAL, t * H + r * G:t * H + (r + 1) * G, :]),
                               b_full)
                maxima(st, 5)
                if unit(m):
                    pe.wait_ge(exp_done, st.at(lambda k: chunk(k, 2)))
                    pe.wait_ge(g_copied, st.at(lambda k: k))
                    for t in range(TPB):
                        for j in range(G):
                            last = nc.tensor.matmul(ps_o[SLOT * j:SLOT * (j + 1), t * P:(t + 1) * P],
                                                    v32[:, m % KEEP, t, j, :], pw[:, j, t, :], start=True, stop=True)
                    last.then_inc(w_full, 1)
                if r == 2 and batch(b + 2):
                    wait_a(st, "xT")
                    pe.wait_ge(zc_ready, st.at(lambda k: k // NG + 3))
                    transposes(ps_a, lambda t: zc[:, t * P:(t + 1) * P], a_full)
                if r == 2 and batch(b - 1):
                    pe.wait_ge(out_ready, st.at(lambda k: NG * (k // NG)))
                    wait_a(st, "yT")
                    transposes(ps_a, lambda t: out[:, (b - 1) % 2, t, :], a_full)
                if r == 3 and batch(b + 2):
                    pe.wait_ge(a_done, st.at(lambda k: a_count(k - 1, "xT")))
                    for task, n in (("wq", 1), ("wk", 2), ("q", 3), ("k", 4), ("v", 0)):
                        wait_b(st, task)
                        for t in range(TPB):
                            last = nc.tensor.matmul(ps_b[:, t * P:(t + 1) * P], xT[:, t * P:(t + 1) * P],
                                                    a["w"][:, n * D:(n + 1) * D], start=True, stop=True)
                        last.then_inc(b_full, 1)
                if r == 3 and batch(b - 1):
                    pe.wait_ge(a_done, st.at(lambda k: a_count(k - 1, "yT")))
                    wait_b(st, "op")
                    for t in range(TPB):
                        last = nc.tensor.matmul(ps_b[:, t * P:(t + 1) * P], yT[:, t * P:(t + 1) * P], a["wo"][:, :],
                                                start=True, stop=True)
                    last.then_inc(b_full, 1)
                if unit(k):
                    wait_b(st, "Mw")
                    pe.wait_ge(max_done, st.at(lambda k: maxes(k, 5)))
                    transposes(ps_b, lambda t: stacked(qt[:, b % 2, WINDOWED, t * H + r * G:t * H + (r + 1) * G, :]),
                               b_full)

        @block.scalar
        def _(act):
            for st in steps(act):
                k = st.k
                b, r, m = k // NG, k % NG, k - 1
                if unit(m):
                    wait(act, g_full, st.at(lambda k: k - 1))
                    for c in range(2):
                        act.wait_ge(scores_full, st.at(lambda k: chunk(k, c)))
                        nc.scalar.activation(pg[:, 2 * c:2 * c + 2, :, :].rearrange("p a b c -> p (a b c)"),
                                             ps_s[:, (chunk(k, c) - 1) % 2, :], ACT.Exp).then_inc(exp_done, 1)
                    wait(act, w_full, st.at(lambda k: k - 1))
                    act.wait_ge(scores_full, st.at(lambda k: chunk(k, 2)))
                    nc.scalar.activation(pw[:, :, :, :].rearrange("p a b c -> p (a b c)"),
                                         ps_s[:, (chunk(k, 2) - 1) % 2, :], ACT.Exp).then_inc(exp_done, 1)
                if unit(k + 1):
                    for kind, task in ((GLOBAL, "Qg"), (WINDOWED, "Qw")):
                        act.wait_ge(a_full, st.at(lambda k: a_count(k, task)))
                        nc.scalar.copy(qs[:, (k + 1) % 2, kind, :], ps_a).then_inc(a_done, 1)
                if unit(m):
                    act.wait_ge(g_full, st.at(lambda k: k))
                    nc.scalar.copy(otg[:, :], ps_o).then_inc(g_copied, 1)
                if unit(k + 2):
                    u = k + 2
                    if unit(u - 2):
                        act.wait_ge(kpad_loaded[(u - 2) % KEEP], st.at(lambda k: 128 * (k // KEEP + 1)))
                    for kind, task in ((GLOBAL, "Kg"), (WINDOWED, "Kw")):
                        act.wait_ge(a_full, st.at(lambda k: a_count(k, task)))
                        nc.scalar.copy(ks[:, u % 2, kind, :], ps_a).then_inc(a_done, 1)
                if unit(m):
                    act.wait_ge(w_full, st.at(lambda k: k))
                    nc.scalar.copy(otw[:, :], ps_o).then_inc(w_copied, 1)
                if r == 2 and batch(b + 2):
                    act.wait_ge(a_full, st.at(lambda k: a_count(k, "xT")))
                    nc.scalar.copy(xT[:, :], ps_a).then_inc(a_done, 1)
                if r == 2 and batch(b - 1):
                    act.wait_ge(a_full, st.at(lambda k: a_count(k, "yT")))
                    nc.scalar.copy(yT[:, :], ps_a).then_inc(a_done, 1)

        @block.vector
        def _(dve):
            nc.vector.tensor_copy(bias_hi[:, :], a["pos"][:, :]).then_inc(set_up, 1)
            nc.vector.tensor_scalar(bwq[:, :], a["b"][:, D:2 * D], SCALE, None, ALU.mult)
            dve.wait_ge(set_up, 1)
            nc.vector.tensor_tensor(bias_lo[:, :], a["pos"][:, :], bias_hi[:, :].bitcast(F32),
                                    ALU.subtract).then_inc(set_up, 1)
            dve.wait_ge(set_up, 2)
            dve.wait_ge(cleared, 1)
            nc.vector.memset(kt[0:W, :, WINDOWED, :, WIN_B].bitcast(F32), 1.0)
            nc.vector.memset(kt[W:P, :, WINDOWED, :, WIN_A].bitcast(F32), 1.0)
            nc.vector.memset(qt[0:W, :, WINDOWED, :, WIN_A].bitcast(F32), FAR)
            nc.vector.memset(qt[W:P, :, WINDOWED, :, WIN_B].bitcast(F32), FAR)
            for par in range(2):
                for kind in (WINDOWED, GLOBAL):
                    for t in range(TPB):
                        c = t if kind == GLOBAL else TPB
                        for slot, part in ((BIAS_HI, bias_hi), (BIAS_LO, bias_lo)):
                            last = nc.vector.tensor_copy(kt[:, par, kind, t * H:(t + 1) * H, slot],
                                                         part[:, c:c + 1].bitcast(F32).to_broadcast([P, H]))
            last.then_inc(consts, 1)

            def normalise(x, mv, rs, dst):
                for t in range(TPB):
                    last = nc.vector.tensor_scalar(dst(t), x(t), mv[:, t, 0:1], rs[:, t:t + 1],
                                                   ALU.subtract, ALU.mult)
                return last

            def heads_out():
                return ps_b.rearrange("p (n s) -> p n s", s=SLOT)

            def maxima(part):
                if not unit(k):
                    return
                dve.wait_ge(max_full, st.at(lambda k: maxes(k, part)))
                if part < 4:
                    n = (part // 2) * H + r * G + 2 * (part % 2)
                    dst, src = qt[:, b % 2, GLOBAL, n:n + 2, SHIFT], ps_m[:, :].rearrange("p (j s) -> p j s", s=S)
                else:
                    n = (part - 4) * H + r * G
                    dst, src = qt[:, b % 2, WINDOWED, n:n + G, SHIFT], ps_m[:, :].rearrange("p (j s) -> p j s", s=P)
                nc.vector.tensor_reduce(dst, src, AX.X, ALU.max, negate=True).then_inc(max_done, 1)

            for st in steps(dve):
                k = st.k
                b, r = k // NG, k % NG
                if unit(k - 2):
                    dve.wait_ge(b_full, st.at(lambda k: b_count(k, "Og")))
                    nc.vector.reciprocal(rg[:, :], heads_out()[:, :, HD]).then_inc(recip_g, 1)
                    dve.wait_ge(recip_g, st.at(lambda k: k - 1))
                    nc.vector.tensor_tensor(og[:, :, :], heads_out()[:, :, 0:HD],
                                            rg[:, :].unsqueeze(2).to_broadcast([P, TPB * G, HD]),
                                            ALU.mult).then_inc(b_done, 1)
                if r == 0 and batch(b - 2):
                    dve.wait_ge(rs_y_ready, st.at(lambda k: k // NG - 1))
                    normalise(lambda t: y[:, t, :], mv_y, rs_y, lambda t: y[:, t, :]).then_inc(x_part, 1)
                    dve.wait_ge(x_part, st.at(lambda k: k // NG - 1))
                    xx = X[:, tiles(st, -2)]
                    nc.vector.tensor_tensor(xx, xx, y[:].rearrange("p t d -> p (t d)"), ALU.add).then_inc(x_new, 1)
                    hold(dve, x_new, st.at(lambda k: k // NG - 1), passed)
                    for t in range(TPB):
                        last = nc.vector.bn_stats(bn[:, t, :], xx[:, t * D:(t + 1) * D])
                    last.then_inc(bn_done, 1)
                    hold(dve, bn_done, st.at(lambda k: 2 * (k // NG - 1)), passed)
                    for t in range(TPB):
                        last = nc.vector.bn_aggr(mv_x[:, t, :], bn[:, t, :])
                    last.then_inc(stats_x, 1)
                if r == 1 and batch(b - 2):
                    dve.wait_ge(rs_x_ready, st.at(lambda k: k // NG - 1))
                    xx, zz = X[:, tiles(st, -2)], Z[:, tiles(st, -2)]
                    normalise(lambda t: xx[:, t * D:(t + 1) * D], mv_x, rs_x,
                              lambda t: zz[:, t * D:(t + 1) * D]).then_inc(z_new, 1)
                maxima(0)
                maxima(1)
                maxima(2)
                if unit(k - 2):
                    dve.wait_ge(b_full, st.at(lambda k: b_count(k, "Ow")))
                    nc.vector.reciprocal(rw[:, :], heads_out()[:, :, HD]).then_inc(recip_w, 1)
                    dve.wait_ge(recip_w, st.at(lambda k: k - 1))
                    nc.vector.tensor_tensor(ow[:, :, :], heads_out()[:, :, 0:HD],
                                            rw[:, :].unsqueeze(2).to_broadcast([P, TPB * G, HD]),
                                            ALU.mult).then_inc(b_done, 1)
                    dve.wait_ge(b_done, st.at(lambda k: b_count(k, "Ow")))
                    g = (k - 2) % NG
                    dst = out[:, ((k - 2) // NG) % 2, :, g * G * HD:(g + 1) * G * HD]
                    nc.vector.tensor_tensor(dst, og[:].rearrange("p (t h) d -> p t (h d)", t=TPB),
                                            ow[:].rearrange("p (t h) d -> p t (h d)", t=TPB),
                                            ALU.add).then_inc(out_ready, 1)
                maxima(3)
                maxima(4)
                if unit(k):
                    dve.wait_ge(b_full, st.at(lambda k: b_count(k, "Mg")))
                    nc.vector.tensor_copy(qsm[:, GLOBAL, :], ps_b).then_inc(b_done, 1)
                maxima(5)
                if r == 3 and batch(b + 2):
                    wait(dve, stacks_ready, st.at(lambda k: k // NG + 2))
                    for n, task in enumerate(("wq", "wk", "q", "k", "v")):
                        dve.wait_ge(b_full, st.at(lambda k: b_count(k, task)))
                        src = ps_b.rearrange("p (t d) -> p t d", d=D)
                        if task == "wq":
                            nc.vector.scalar_tensor_tensor(
                                out=proj[:, n, :, :], in0=src, scalar=SCALE,
                                in1=bwq[:, :].unsqueeze(1).to_broadcast([P, TPB, D]), op0=ALU.mult,
                                op1=ALU.add).then_inc(b_done, 1)
                            continue
                        c = (n + 1) % 5
                        if task == "v":
                            wait(dve, v_ready, st.at(lambda k: NG * (k // NG + 1)))
                        nc.vector.tensor_tensor(vt[:, b % 2, :, :] if task == "v" else proj[:, n, :, :], src,
                                                a["b"][:, c * D:(c + 1) * D].unsqueeze(1).to_broadcast([P, TPB, D]),
                                                ALU.add).then_inc(b_done, 1)
                if r == 3 and batch(b - 1):
                    dve.wait_ge(b_full, st.at(lambda k: b_count(k, "op")))
                    nc.vector.tensor_tensor(y[:, :, :], ps_b.rearrange("p (t d) -> p t d", d=D),
                                            a["bo"][:, :].unsqueeze(1).to_broadcast([P, TPB, D]),
                                            ALU.add).then_inc(b_done, 1)
                    hold(dve, b_done, st.at(lambda k: b_count(k, "op")), passed)
                    for t in range(TPB):
                        last = nc.vector.bn_stats(bn[:, t, :], y[:, t, :])
                    last.then_inc(bn_done, 1)
                    hold(dve, bn_done, st.at(lambda k: 2 * (k // NG) - 1), passed)
                    for t in range(TPB):
                        last = nc.vector.bn_aggr(mv_y[:, t, :], bn[:, t, :])
                    last.then_inc(stats_y, 1)
                if unit(k):
                    dve.wait_ge(b_full, st.at(lambda k: b_count(k, "Mw")))
                    nc.vector.tensor_copy(qsm[:, WINDOWED, :], ps_b).then_inc(b_done, 1)
            dve.wait_ge(z_new, B)

        @block.gpsimd
        def _(pool):
            nc.gpsimd.memset(half[:, :], -0.5)
            nc.gpsimd.memset(kt[:].rearrange("p a b c d -> p (a b c d)").bitcast(F32), 0.0)
            nc.gpsimd.memset(qt[:].rearrange("p a b c d -> p (a b c d)").bitcast(F32), 0.0).then_inc(pool_step, 1)
            nc.gpsimd.memset(v32[:].rearrange("p a b c d -> p (a b c d)"), 0.0).then_inc(pool_step, 1)
            pool.wait_ge(pool_step, 2)
            nc.gpsimd.memset(kt[:].rearrange("p a b c d -> p (a b) c d")[:, :, :, SHIFT].bitcast(F32), 1.0)
            nc.gpsimd.memset(qt[:].rearrange("p a b c d -> p (a b) c d")[:, :, :, BIAS_HI:BIAS_LO + 1].bitcast(F32),
                             1.0).then_inc(cleared, 1)
            nc.gpsimd.memset(v32[:, :, :, :, HD].rearrange("p a b c -> p (a b c)"), 1.0).then_inc(consts, 1)
            nc.gpsimd.memset(kpad[:].rearrange("p a b c d -> p (a b c d)").bitcast(F32), 0.0).then_inc(consts, 1)
            pool.wait_ge(consts, 3)

            def rstd(st, stats, mv, rs, ready, n):
                hold(pool, stats, st.at(lambda k: k // NG + (0 if n else -1)), passed)
                nc.gpsimd.tensor_scalar(ve[:, :], mv[:, :, 1], EPS, None, ALU.add).then_inc(pool_step, 1)
                hold(pool, pool_step, st.at(lambda k: 2 + 2 * (k // NG - 1) + (1 if n else 0)), passed)
                nc.gpsimd.tensor_tensor(rs[:, :], ve[:, :], half[:, :], ALU.pow).then_inc(ready, 1)

            for st in steps(pool):
                k = st.k
                b, r = k // NG, k % NG
                if r == 0 and batch(b + 1):
                    hold(pool, b_done, st.at(lambda k: b_count(k - 1, "k")), passed)
                    if unit(k - 1):
                        hold(pool, b_done, st.at(lambda k: b_count(k - 1, "Mw")), passed)
                    n, par = TPB * H, (b + 1) % 2
                    val = proj[:].rearrange("p a t (h d) -> p a (t h) d", d=HD)
                    for kind in (WINDOWED, GLOBAL):
                        qd, kd = qt[:, par, kind, :, :], kt[:, par, kind, :, :]
                        nc.gpsimd.memset(qd[:, :, SHIFT].bitcast(F32), 0.0)
                        nc.gpsimd.tensor_copy(qd[:, :, 0:2 * HD].rearrange("p n (c d) -> p n c d", c=2),
                                              val[:, 2 * kind, :, :].unsqueeze(2).to_broadcast([P, n, 2, HD]))
                        nc.gpsimd.tensor_copy(
                            kd[:, :, 0:4 * HD].rearrange("p n (c d) -> p n c d", c=2)[:, :, :, 0:HD],
                            val[:, 2 * kind + 1, :, :].unsqueeze(2).to_broadcast([P, n, 2, HD])).then_inc(parts_hi, 1)
                    hold(pool, parts_hi, st.at(lambda k: 2 * (k // NG + 2)), passed)
                    for kind in (WINDOWED, GLOBAL):
                        qd, kd = qt[:, par, kind, :, :], kt[:, par, kind, :, :]
                        nc.gpsimd.tensor_tensor(qd[:, :, 2 * HD:3 * HD], val[:, 2 * kind, :, :],
                                                qd[:, :, 0:HD].bitcast(F32), ALU.subtract)
                        last = nc.gpsimd.tensor_tensor(kd[:, :, HD:2 * HD], val[:, 2 * kind + 1, :, :],
                                                       kd[:, :, 0:HD].bitcast(F32), ALU.subtract)
                    last.then_inc(stacks_ready, 1)
                if r == 1 and batch(b + 2):
                    if batch(b + 1):
                        hold(pool, a_done, st.at(lambda k: a_count(k - 3, "xT")), passed)
                    nc.gpsimd.tensor_copy(zc[:, :], Z[:, tiles(st, 2)]).then_inc(zc_ready, 1)
                if r == 3 and batch(b - 1):
                    rstd(st, stats_y, mv_y, rs_y, rs_y_ready, 1)
                if r == 0 and batch(b - 2):
                    rstd(st, stats_x, mv_x, rs_x, rs_x_ready, 0)
                if unit(k + 2):
                    u = k + 2
                    hold(pool, b_done, st.at(lambda k: b_count(NG * ((k + 2) // NG - 2) + 3, "v")), passed)
                    hold(pool, w_full, st.at(lambda k: clip(k + 2 - KEEP + 1, UNITS)), passed)
                    hs = slice((u % NG) * G * HD, (u % NG + 1) * G * HD)
                    nc.gpsimd.tensor_copy(v32[:, u % KEEP, :, :, 0:HD],
                                          vt[:, (u // NG) % 2, :, hs].rearrange("p t (h d) -> p t h d", d=HD)
                                          ).then_inc(v_ready, 1)


TOK = 512
TT = TOK // P
NT = B * S // TOK


def token_steps(eng, last, first=1):
    for k in range(first):
        yield Step(k)
    with eng.Fori(first, NT - 1) as i:
        yield Step(first, i, first, 1)
    for k in range(NT - 1, last + 1):
        yield Step(k)


def block_of(st, lead=0):
    return bass.ds(st.at(lambda k: (k + lead) * TT * D), TT * D)


class Chain:

    def __init__(self, eng, sem, per_step):
        self.eng, self.sem, self.per_step, self.n = eng, sem, per_step, 0

    def begin(self, st):
        assert self.n in (0, self.per_step)
        self.st, self.n = st, 0

    def __call__(self, instruction, passed=None):
        self.n += 1
        n = self.n
        instruction.then_inc(self.sem, 1)
        value = self.st.at(lambda k: k * self.per_step + n)
        if passed:
            hold(self.eng, self.sem, value, passed)
        else:
            self.eng.wait_ge(self.sem, value)


def best(nc, link, val, rev, top, first, key, sel):
    shape = list(val.shape)
    link(nc.vector.tensor_reduce(top, val, AX.X, ALU.max))
    link(nc.vector.tensor_tensor(key, val, top.unsqueeze(2).to_broadcast(shape), ALU.is_equal))
    link(nc.vector.tensor_tensor(key, key, rev.unsqueeze(1).to_broadcast(shape), ALU.mult))
    link(nc.vector.tensor_reduce(first, key, AX.X, ALU.max))
    link(nc.vector.tensor_tensor(sel, key, first.unsqueeze(2).to_broadcast(shape), ALU.is_equal))


BEST_LINKS = 5


def statistics(nc, link, x, bn, mv, passed):
    for t in range(TT):
        last = nc.vector.bn_stats(bn[:, t, :], x[:, t * D:(t + 1) * D])
    link(last, passed)
    for t in range(TT):
        last = nc.vector.bn_aggr(mv[:, t, :], bn[:, t, :])
    return last


def normalise_tiles(nc, x, mv, rs, out):
    for t in range(TT):
        last = nc.vector.tensor_scalar(out[:, t * D:(t + 1) * D], x[:, t * D:(t + 1) * D], mv[:, t, 0:1],
                                       rs[:, t:t + 1], ALU.subtract, ALU.mult)
    return last


def first_ffn(nc, X, Z, ident, a):
    E = 8
    NE = E + 1
    HC = 4
    HID = HC * P
    LINKS = 2 * BEST_LINKS + 1 + 6 + 4

    with ExitStack() as ctx:
        def sb(name, shape, dt=F32):
            return ctx.enter_context(nc.sbuf_tensor("f0_" + name, shape, dt))

        def pb(name, shape):
            return ctx.enter_context(nc.psum_tensor("f0_" + name, shape, F32))

        def sem(name):
            return ctx.enter_context(nc.semaphore("f0_" + name))

        w1h, w1l = sb("w1h", [P, NE * HID], F32R), sb("w1l", [P, NE * HID], F32R)
        gwh, gwl = sb("gwh", [P, E], F32R), sb("gwl", [P, E], F32R)
        zc = sb("zc", [P, TOK])
        xh, xl = sb("xh", [P, TOK], F32R), sb("xl", [P, TOK], F32R)
        s = sb("s", [P, 3, HC, TOK])
        acc = sb("acc", [P, TOK])
        lg, key, sel1, sel2, far = [sb(n, [P, TT, E]) for n in ("lg", "key", "sel1", "sel2", "far")]
        gate = sb("gate", [P, TT, E])
        m1, m2, first, diff, e2, den, g1, g2 = [
            sb(n, [P, TT]) for n in ("m1", "m2", "first", "diff", "e2", "den", "g1", "g2")]
        bn, mv, rs, ve = sb("bn", [P, TT, 6]), sb("mv", [P, TT, 2]), sb("rs", [P, TT]), sb("ve", [P, TT])
        half, euler = sb("half", [P, TT]), sb("euler", [P, TT])
        ps_u = pb("ps_u", [P, 2, 1024])
        ps_y = pb("ps_y", [P, 3, TOK])
        ps_x = pb("ps_x", [P, TOK])

        w1h_ready, w1l_ready, gw_ready, gw_hi = sem("w1h_ready"), sem("w1l_ready"), sem("gw_ready"), sem("gw_hi")
        zc_ready, x_full, xh_ready, x_ready = sem("zc_ready"), sem("x_full"), sem("xh_ready"), sem("x_ready")
        logits_full, logits_copied = sem("logits_full"), sem("logits_copied")
        up_full, silu_done, y_full, y_done = sem("up_full"), sem("silu_done"), sem("y_full"), sem("y_done")
        link_sem, diff_ready, e2_ready = sem("link"), sem("diff_ready"), sem("e2_ready")
        stats_ready, rs_ready, ve_ready = sem("stats_ready"), sem("rs_ready"), sem("ve_ready")
        z_new, consts = sem("z_new"), sem("consts")
        passed = sem("passed")
        block = ctx.enter_context(nc.Block())

        @block.tensor
        def _(pe):
            def transpose_x(value):
                for t in range(TT):
                    last = nc.tensor.transpose(ps_x[:, t * P:(t + 1) * P], zc[:, t * P:(t + 1) * P], ident[:, :])
                last.then_inc(x_full, 1)

            def up(st, e):
                for c2 in range(2):
                    wait(pe, silu_done, st.at(lambda k: 2 * NE * k + 2 * e + c2 + 1 - 2))
                    for c in (2 * c2, 2 * c2 + 1):
                        dst = ps_u[:, c2, (c % 2) * TOK:(c % 2 + 1) * TOK]
                        w = slice(e * HID + c * P, e * HID + (c + 1) * P)
                        nc.tensor.matmul(dst, w1h[:, w], xh[:, :], start=True, stop=False)
                        nc.tensor.matmul(dst, w1h[:, w], xl[:, :], start=False, stop=False)
                        last = nc.tensor.matmul(dst, w1l[:, w], xh[:, :], start=False, stop=True)
                    last.then_inc(up_full, 1)

            def down(st, e):
                pe.wait_ge(silu_done, st.at(lambda k: 2 * NE * k + 2 * e + 2))
                wait(pe, y_done, st.at(lambda k: NE * k + e + 1 - 3))
                for t in range(TT):
                    for c in range(HC):
                        last = nc.tensor.matmul(ps_y[:, e % 3, t * D:(t + 1) * D], s[:, e % 3, c, t * P:(t + 1) * P],
                                                a["w2"][:, (e * HC + c) * D:(e * HC + c + 1) * D],
                                                start=c == 0, stop=c == HC - 1)
                last.then_inc(y_full, 1)

            pe.wait_ge(zc_ready, 1)
            transpose_x(0)
            pe.wait_ge(gw_ready, 1)
            for st in token_steps(pe, NT - 1):
                pe.wait_ge(x_ready, st.at(lambda k: k + 1))
                for t in range(TT):
                    tok, dst = slice(t * P, (t + 1) * P), ps_x[:, t * E:(t + 1) * E]
                    nc.tensor.matmul(dst, xh[:, tok], gwh[:, :], start=True, stop=False)
                    nc.tensor.matmul(dst, xh[:, tok], gwl[:, :], start=False, stop=False)
                    last = nc.tensor.matmul(dst, xl[:, tok], gwh[:, :], start=False, stop=True)
                last.then_inc(logits_full, 1)
                for e in range(NE):
                    if st.k == 0:
                        pe.wait_ge(w1h_ready, e + 1)
                        pe.wait_ge(w1l_ready, e + 1)
                    up(st, e)
                    if e == NE - 1 and st.k < NT - 1:
                        pe.wait_ge(zc_ready, st.at(lambda k: k + 2))
                        pe.wait_ge(logits_copied, st.at(lambda k: k + 1))
                        transpose_x(1)
                    if e > 0:
                        down(st, e - 1)
                down(st, NE - 1)

        @block.scalar
        def _(act):
            for e in range(NE):
                nc.scalar.copy(w1h[:, e * HID:(e + 1) * HID],
                               a["w1"][:, e * HID:(e + 1) * HID]).then_inc(w1h_ready, 1)
            for st in token_steps(act, NT - 1):
                for e in range(NE):
                    for c2 in range(2):
                        act.wait_ge(up_full, st.at(lambda k: 2 * NE * k + 2 * e + c2 + 1))
                        if c2 == 0:
                            wait(act, y_full, st.at(lambda k: NE * k + e + 1 - 3))
                        nc.scalar.activation(s[:, e % 3, 2 * c2:2 * c2 + 2, :].rearrange("p a b -> p (a b)"),
                                             ps_u[:, c2, :], ACT.Silu).then_inc(silu_done, 1)

        @block.vector
        def _(dve):
            link = Chain(dve, link_sem, LINKS)

            def split_x(st, lead):
                dve.wait_ge(x_full, st.at(lambda k: k + lead + 1))
                nc.vector.tensor_copy(xh[:, :], ps_x[:, :]).then_inc(xh_ready, 1)
                dve.wait_ge(xh_ready, st.at(lambda k: k + lead + 1))
                nc.vector.tensor_tensor(xl[:, :], ps_x[:, :], xh[:, :].bitcast(F32), ALU.subtract).then_inc(x_ready, 1)

            nc.vector.tensor_copy(gwh[:, :], a["gate"][:, :]).then_inc(gw_hi, 1)
            dve.wait_ge(gw_hi, 1)
            nc.vector.tensor_tensor(gwl[:, :], a["gate"][:, :], gwh[:, :].bitcast(F32),
                                    ALU.subtract).then_inc(gw_ready, 1)
            split_x(Step(0), 0)
            for e in range(NE):
                dve.wait_ge(w1h_ready, e + 1)
                cols = slice(e * HID, (e + 1) * HID)
                nc.vector.tensor_tensor(w1l[:, cols], a["w1"][:, cols], w1h[:, cols].bitcast(F32),
                                        ALU.subtract).then_inc(w1l_ready, 1)
            for st in token_steps(dve, NT - 1):
                link.begin(st)
                dve.wait_ge(logits_full, st.at(lambda k: k + 1))
                nc.vector.tensor_copy(lg[:].rearrange("p t e -> p (t e)"),
                                      ps_x[:, 0:TT * E]).then_inc(logits_copied, 1)
                dve.wait_ge(logits_copied, st.at(lambda k: k + 1))
                rev = a["rev"][:, 0:E]
                best(nc, link, lg[:, :, :], rev, m1[:, :], first[:, :], key[:, :, :], sel1[:, :, :])
                link(nc.vector.scalar_tensor_tensor(out=far[:, :, :], in0=sel1[:, :, :], scalar=FAR,
                                                    in1=lg[:, :, :], op0=ALU.mult, op1=ALU.add))
                best(nc, link, far[:, :, :], rev, m2[:, :], first[:, :], key[:, :, :], sel2[:, :, :])
                nc.vector.tensor_tensor(diff[:, :], m2[:, :], m1[:, :], ALU.subtract).then_inc(diff_ready, 1)
                dve.wait_ge(e2_ready, st.at(lambda k: k + 1))
                link(nc.vector.tensor_scalar(den[:, :], e2[:, :], 1.0, None, ALU.add))
                link(nc.vector.reciprocal(g1[:, :], den[:, :]))
                link(nc.vector.tensor_tensor(g2[:, :], e2[:, :], g1[:, :], ALU.mult))
                shape = [P, TT, E]
                link(nc.vector.tensor_tensor(sel1[:, :, :], sel1[:, :, :],
                                             g1[:, :].unsqueeze(2).to_broadcast(shape), ALU.mult))
                link(nc.vector.tensor_tensor(sel2[:, :, :], sel2[:, :, :],
                                             g2[:, :].unsqueeze(2).to_broadcast(shape), ALU.mult))
                link(nc.vector.tensor_tensor(gate[:, :, :], sel1[:, :, :], sel2[:, :, :], ALU.add))
                for e in range(NE):
                    if e == NE - 2 and st.k < NT - 1:
                        split_x(st, 1)
                    dve.wait_ge(y_full, st.at(lambda k: NE * k + e + 1))
                    src = ps_y[:, e % 3, :]
                    if e == 0:
                        nc.vector.tensor_copy(acc[:, :], src).then_inc(y_done, 1)
                        continue
                    dve.wait_ge(y_done, st.at(lambda k: NE * k + e))
                    for t in range(TT):
                        tok = slice(t * D, (t + 1) * D)
                        last = nc.vector.scalar_tensor_tensor(out=acc[:, tok], in0=src[:, tok],
                                                              scalar=gate[:, t, e - 1:e], in1=acc[:, tok],
                                                              op0=ALU.mult, op1=ALU.add)
                    last.then_inc(y_done, 1)
                hold(dve, y_done, st.at(lambda k: NE * k + NE), passed)
                statistics(nc, link, acc, bn, mv, passed).then_inc(stats_ready, 1)
                dve.wait_ge(rs_ready, st.at(lambda k: 2 * k + 1))
                link(normalise_tiles(nc, acc, mv, rs, acc))
                xx = X[:, block_of(st)]
                link(nc.vector.tensor_tensor(xx, xx, acc[:, :], ALU.add), passed)
                statistics(nc, link, xx, bn, mv, passed).then_inc(stats_ready, 1)
                dve.wait_ge(rs_ready, st.at(lambda k: 2 * k + 2))
                normalise_tiles(nc, xx, mv, rs, Z[:, block_of(st)]).then_inc(z_new, 1)
            dve.wait_ge(z_new, NT)

        @block.gpsimd
        def _(pool):
            nc.gpsimd.memset(half[:, :], -0.5)
            nc.gpsimd.memset(euler[:, :], float(np.exp(1.0))).then_inc(consts, 1)
            nc.gpsimd.tensor_copy(zc[:, :], Z[:, 0:TOK]).then_inc(zc_ready, 1)
            pool.wait_ge(consts, 1)
            for st in token_steps(pool, NT - 1):
                hold(pool, diff_ready, st.at(lambda k: k + 1), passed)
                nc.gpsimd.tensor_tensor(e2[:, :], euler[:, :], diff[:, :], ALU.pow).then_inc(e2_ready, 1)
                if st.k < NT - 1:
                    hold(pool, x_full, st.at(lambda k: k + 1), passed)
                    nc.gpsimd.tensor_copy(zc[:, :], Z[:, block_of(st, 1)]).then_inc(zc_ready, 1)
                for n in range(2):
                    hold(pool, stats_ready, st.at(lambda k: 2 * k + n + 1), passed)
                    nc.gpsimd.tensor_scalar(ve[:, :], mv[:, :, 1], EPS, None, ALU.add).then_inc(ve_ready, 1)
                    hold(pool, ve_ready, st.at(lambda k: 2 * k + n + 1), passed)
                    nc.gpsimd.tensor_tensor(rs[:, :], ve[:, :], half[:, :], ALU.pow).then_inc(rs_ready, 1)


def second_ffn(nc, X, Z, ident, a, out):
    E = 16
    NQ = E // 2 + 1
    LAST = NT
    LINKS = 2 * BEST_LINKS + 8

    def live(n):
        return 0 <= n < NT

    with ExitStack() as ctx:
        def sb(name, shape, dt=F32):
            return ctx.enter_context(nc.sbuf_tensor("f1_" + name, shape, dt))

        def pb(name, shape):
            return ctx.enter_context(nc.psum_tensor("f1_" + name, shape, F32))

        def sem(name):
            return ctx.enter_context(nc.semaphore("f1_" + name))

        wh, wl = sb("wh", [P, NQ, 2, P], F32R), sb("wl", [P, NQ, 2, P], F32R)
        rwh, rwl = sb("rwh", [P, E], F32R), sb("rwl", [P, E], F32R)
        pick = sb("pick", [P, NQ - 1, P], F32R)
        zc = sb("zc", [P, TOK])
        xh, xl = sb("xh", [P, TOK], F32R), sb("xl", [P, TOK], F32R)
        s = sb("s", [P, 3, TOK])
        h = sb("h", [P, NQ, TOK])
        p = sb("p", [P, 2, TOK])
        lg, ex, key, sel1, sel2, far = [sb(n, [P, TT, E]) for n in ("lg", "ex", "key", "sel1", "sel2", "far")]
        cw = sb("cw", [P, TT, P], F32R)
        gt = sb("gt", [P, TOK], F32R)
        m1, m2, first, total, inv = [sb(n, [P, TT]) for n in ("m1", "m2", "first", "total", "inv")]
        bn, mv, rs, ve = sb("bn", [P, TT, 6]), sb("mv", [P, TT, 2]), sb("rs", [P, TT]), sb("ve", [P, TT])
        half = sb("half", [P, TT])
        acc = sb("acc", [P, TOK])
        ps_g, ps_u = pb("ps_g", [P, 3, TOK]), pb("ps_u", [P, 3, TOK])
        ps_x, ps_y = pb("ps_x", [P, TOK]), pb("ps_y", [P, TOK])

        wh_ready, wl_ready, rw_hi, rw_ready = sem("wh_ready"), sem("wl_ready"), sem("rw_hi"), sem("rw_ready")
        zc_ready, xh_ready, x_full, x_done = sem("zc_ready"), sem("xh_ready"), sem("x_full"), sem("x_done")
        gate_full, up_full, silu_done, h_done = sem("gate_full"), sem("up_full"), sem("silu_done"), sem("h_done")
        down_done, y_copied, cw_ready = sem("down_done"), sem("y_copied"), sem("cw_ready")
        shifted, ex_ready, link_sem = sem("shifted"), sem("ex_ready"), sem("link")
        stats_ready, rs_ready, ve_ready, y_ready = sem("stats_ready"), sem("rs_ready"), sem("ve_ready"), sem("y_ready")
        x_new, stored, consts = sem("x_new"), sem("stored"), sem("consts")
        passed = sem("passed")
        block = ctx.enter_context(nc.Block())

        def x_count(k, task, q=0):
            n = clip(k, NT) * 2 + (NQ - 1) * clip(k - 1, NT) + min(k + 1, NT)
            if task == "start":
                return n
            n += live(k)
            if task == "logits":
                return n
            if task == "gates":
                return n + q
            n += (NQ - 1) * live(k - 1)
            if task == "cw":
                return n + live(k + 1) + live(k)
            return n + live(k + 1)

        @block.sync
        def _(sp):
            for st in token_steps(sp, LAST, 2):
                if live(st.k - 1):
                    hold(sp, x_new, st.at(lambda k: k), passed)
                    sp.dma_start(out[bass.ds(st.at(lambda k: (k - 1) * TOK), TOK), :].rearrange(
                        "(t p) d -> p t d", p=P), X[:, block_of(st, -1)].rearrange("p (t d) -> p t d", d=D)
                        ).then_inc(stored, 16)
            sp.wait_ge(stored, 16 * NT)

        @block.tensor
        def _(pe):
            def take_x(st, task, q=0):
                wait(pe, x_done, st.at(lambda k: x_count(k, task, q) - 1))

            def transpose_x():
                for t in range(TT):
                    last = nc.tensor.transpose(ps_x[:, t * P:(t + 1) * P], zc[:, t * P:(t + 1) * P], ident[:, :])
                last.then_inc(x_full, 1)

            def down(st, q):
                if q == 0:
                    wait(pe, y_copied, st.at(lambda k: k - 1))
                else:
                    pe.wait_ge(x_done, st.at(lambda k: x_count(k, "gates", q)))
                for t in range(TT):
                    src = h[:, 0, t * P:(t + 1) * P] if q == 0 else p[:, q % 2, t * P:(t + 1) * P]
                    last = nc.tensor.matmul(ps_y[:, t * D:(t + 1) * D], src, a["wd"][:, q * D:(q + 1) * D],
                                            start=q == 0 and t == 0, stop=q == NQ - 1 and t == TT - 1,
                                            skip_group_check=True)
                last.then_inc(down_done, 1)

            pe.wait_ge(zc_ready, 1)
            transpose_x()
            pe.wait_ge(rw_ready, 1)
            pe.wait_ge(consts, 2)
            for st in token_steps(pe, LAST, 2):
                k = st.k
                if live(k):
                    pe.wait_ge(x_done, st.at(lambda k: x_count(k, "start")))
                    for t in range(TT):
                        tok, dst = slice(t * P, (t + 1) * P), ps_x[:, t * E:(t + 1) * E]
                        nc.tensor.matmul(dst, xh[:, tok], rwh[:, :], start=True, stop=False)
                        nc.tensor.matmul(dst, xh[:, tok], rwl[:, :], start=False, stop=False)
                        last = nc.tensor.matmul(dst, xl[:, tok], rwh[:, :], start=False, stop=True)
                    last.then_inc(x_full, 1)
                for q in range(NQ):
                    if live(k):
                        if k == 0:
                            pe.wait_ge(wh_ready, q + 1)
                            pe.wait_ge(wl_ready, q + 1)
                        for ps, half_, free, full in ((ps_g, 0, silu_done, gate_full), (ps_u, 1, h_done, up_full)):
                            wait(pe, free, st.at(lambda k: NQ * k + q + 1 - 3))
                            dst = ps[:, q % 3, :]
                            nc.tensor.matmul(dst, wh[:, q, half_, :], xh[:, :], start=True, stop=False)
                            nc.tensor.matmul(dst, wh[:, q, half_, :], xl[:, :], start=False, stop=False)
                            nc.tensor.matmul(dst, wl[:, q, half_, :], xh[:, :], start=False,
                                             stop=True).then_inc(full, 1)
                    if live(k - 1):
                        if q > 0:
                            take_x(st, "gates", q)
                            nc.tensor.matmul(ps_x[:, :], pick[:, q - 1, :], gt[:, :], start=True,
                                             stop=True).then_inc(x_full, 1)
                        if q == 0:
                            down(st, 0)
                        elif q > 1:
                            down(st, q - 1)
                if live(k + 1):
                    pe.wait_ge(zc_ready, st.at(lambda k: k + 2))
                    take_x(st, "xT")
                    transpose_x()
                if live(k - 1):
                    down(st, NQ - 1)
                if live(k):
                    pe.wait_ge(cw_ready, st.at(lambda k: k + 1))
                    take_x(st, "cw")
                    for t in range(TT):
                        last = nc.tensor.transpose(ps_x[:, t * P:(t + 1) * P], cw[:, t, :].bitcast(F32), ident[:, :])
                    last.then_inc(x_full, 1)

        @block.scalar
        def _(act):
            for q in range(NQ):
                nc.scalar.copy(wh[:, q, :, :].rearrange("p a b -> p (a b)"),
                               a["wgu"][:, q * 2 * P:(q + 1) * 2 * P]).then_inc(wh_ready, 1)
            for st in token_steps(act, NT - 1, 2):
                for q in range(NQ):
                    act.wait_ge(gate_full, st.at(lambda k: NQ * k + q + 1))
                    wait(act, h_done, st.at(lambda k: NQ * k + q + 1 - 3))
                    nc.scalar.activation(s[:, q % 3, :], ps_g[:, q % 3, :], ACT.Silu).then_inc(silu_done, 1)
                    if q == 2:
                        act.wait_ge(shifted, st.at(lambda k: k + 1))
                        nc.scalar.activation(ex[:].rearrange("p t e -> p (t e)"), lg[:].rearrange("p t e -> p (t e)"),
                                             ACT.Exp).then_inc(ex_ready, 1)

        @block.vector
        def _(dve):
            link = Chain(dve, link_sem, LINKS)

            def split_x(st, value, lead):
                dve.wait_ge(x_full, value)
                nc.vector.tensor_copy(xh[:, :], ps_x[:, :]).then_inc(xh_ready, 1)
                dve.wait_ge(xh_ready, st.at(lambda k: k + lead + 1))
                nc.vector.tensor_tensor(xl[:, :], ps_x[:, :], xh[:, :].bitcast(F32), ALU.subtract).then_inc(x_done, 1)

            nc.vector.tensor_copy(rwh[:, :], a["router"][:, :]).then_inc(rw_hi, 1)
            nc.vector.tensor_copy(pick[:].rearrange("p a b -> p (a b)"), a["pick"][:, :]).then_inc(consts, 1)
            dve.wait_ge(rw_hi, 1)
            nc.vector.tensor_tensor(rwl[:, :], a["router"][:, :], rwh[:, :].bitcast(F32),
                                    ALU.subtract).then_inc(rw_ready, 1)
            split_x(Step(0), 1, 0)
            for q in range(NQ):
                dve.wait_ge(wh_ready, q + 1)
                nc.vector.tensor_tensor(wl[:, q, :, :].rearrange("p a b -> p (a b)"),
                                        a["wgu"][:, q * 2 * P:(q + 1) * 2 * P],
                                        wh[:, q, :, :].rearrange("p a b -> p (a b)").bitcast(F32),
                                        ALU.subtract).then_inc(wl_ready, 1)
            dve.wait_ge(consts, 2)
            for st in token_steps(dve, LAST, 2):
                k = st.k

                def probabilities():
                    dve.wait_ge(ex_ready, st.at(lambda k: k + 1))
                    link(nc.vector.tensor_reduce(total[:, :], ex[:, :, :], AX.X, ALU.add))
                    link(nc.vector.reciprocal(inv[:, :], total[:, :]))
                    link(nc.vector.tensor_tensor(ex[:, :, :], ex[:, :, :], inv[:, :].unsqueeze(2).to_broadcast(
                        [P, TT, E]), ALU.mult))

                if live(k):
                    link.begin(st)
                    dve.wait_ge(x_full, st.at(lambda k: x_count(k, "logits")))
                    nc.vector.tensor_copy(lg[:].rearrange("p t e -> p (t e)"), ps_x[:, 0:TT * E]).then_inc(x_done, 1)
                    dve.wait_ge(x_done, st.at(lambda k: x_count(k, "logits")))
                    link(nc.vector.tensor_reduce(m1[:, :], lg[:, :, :], AX.X, ALU.max))
                    nc.vector.tensor_tensor(lg[:, :, :], lg[:, :, :], m1[:, :].unsqueeze(2).to_broadcast([P, TT, E]),
                                            ALU.subtract).then_inc(shifted, 1)
                for q in range(NQ):
                    if live(k - 1) and q > 0:
                        dve.wait_ge(x_full, st.at(lambda k: x_count(k, "gates", q)))
                        if q > 1:
                            dve.wait_ge(down_done, st.at(lambda k: NQ * (k - 1) + q - 1))
                        nc.vector.tensor_tensor(p[:, q % 2, :], h[:, q, :], ps_x[:, :], ALU.mult).then_inc(x_done, 1)
                    if live(k):
                        if q == 0 and live(k - 1):
                            dve.wait_ge(down_done, st.at(lambda k: NQ * (k - 1) + 1))
                        elif live(k - 1):
                            dve.wait_ge(x_done, st.at(lambda k: x_count(k, "gates", q)))
                        dve.wait_ge(silu_done, st.at(lambda k: NQ * k + q + 1))
                        dve.wait_ge(up_full, st.at(lambda k: NQ * k + q + 1))
                        nc.vector.tensor_tensor(h[:, q, :], s[:, q % 3, :], ps_u[:, q % 3, :],
                                                ALU.mult).then_inc(h_done, 1)
                        rev = a["rev"][:, 0:E]
                        if q == 3:
                            probabilities()
                        if q == 4:
                            best(nc, link, ex[:, :, :], rev, m1[:, :], first[:, :], key[:, :, :], sel1[:, :, :])
                        if q == 5:
                            link(nc.vector.scalar_tensor_tensor(out=far[:, :, :], in0=sel1[:, :, :], scalar=FAR,
                                                                in1=ex[:, :, :], op0=ALU.mult, op1=ALU.add))
                            best(nc, link, far[:, :, :], rev, m2[:, :], first[:, :], key[:, :, :], sel2[:, :, :])
                        if q == 6:
                            link(nc.vector.tensor_tensor(sel1[:, :, :], sel1[:, :, :], sel2[:, :, :], ALU.add))
                            link(nc.vector.tensor_tensor(ex[:, :, :], sel1[:, :, :], ex[:, :, :], ALU.mult))
                            link(nc.vector.tensor_copy(cw[:, :, 0:E], ex[:, :, :]))
                            nc.vector.tensor_tensor(cw[:, :, E:2 * E], ex[:, :, :], cw[:, :, 0:E].bitcast(F32),
                                                    ALU.subtract).then_inc(cw_ready, 1)
                if live(k + 1):
                    split_x(st, st.at(lambda k: x_count(k, "xT")), 1)
                if live(k):
                    dve.wait_ge(x_full, st.at(lambda k: x_count(k, "cw")))
                    nc.vector.tensor_copy(gt[:, :], ps_x[:, :]).then_inc(x_done, 1)
                if live(k - 1):
                    dve.wait_ge(down_done, st.at(lambda k: NQ * k))
                    nc.vector.tensor_copy(acc[:, :], ps_y[:, :]).then_inc(y_copied, 1)
                    hold(dve, y_copied, st.at(lambda k: k), passed)
                    for t in range(TT):
                        last = nc.vector.bn_stats(bn[:, t, :], acc[:, t * D:(t + 1) * D])
                    last.then_inc(y_ready, 1)
                    hold(dve, y_ready, st.at(lambda k: 2 * k - 1), passed)
                    for t in range(TT):
                        last = nc.vector.bn_aggr(mv[:, t, :], bn[:, t, :])
                    last.then_inc(stats_ready, 1)
                    dve.wait_ge(rs_ready, st.at(lambda k: k))
                    normalise_tiles(nc, acc, mv, rs, acc).then_inc(y_ready, 1)
                    dve.wait_ge(y_ready, st.at(lambda k: 2 * k))
                    xx = X[:, block_of(st, -1)]
                    nc.vector.tensor_tensor(xx, xx, acc[:, :], ALU.add).then_inc(x_new, 1)

        @block.gpsimd
        def _(pool):
            nc.gpsimd.tensor_copy(zc[:, :], Z[:, 0:TOK]).then_inc(zc_ready, 1)
            nc.gpsimd.memset(half[:, :], -0.5)
            nc.gpsimd.memset(cw[:].rearrange("p t e -> p (t e)").bitcast(F32), 0.0).then_inc(consts, 1)
            for st in token_steps(pool, LAST, 2):
                if live(st.k + 1):
                    hold(pool, x_full, st.at(lambda k: x_count(k, "start")), passed)
                    nc.gpsimd.tensor_copy(zc[:, :], Z[:, block_of(st, 1)]).then_inc(zc_ready, 1)
                if live(st.k - 1):
                    hold(pool, stats_ready, st.at(lambda k: k), passed)
                    nc.gpsimd.tensor_scalar(ve[:, :], mv[:, :, 1], EPS, None, ALU.add).then_inc(ve_ready, 1)
                    hold(pool, ve_ready, st.at(lambda k: k), passed)
                    nc.gpsimd.tensor_tensor(rs[:, :], ve[:, :], half[:, :], ALU.pow).then_inc(rs_ready, 1)


def sandwich(nc, args, out):
    with ExitStack() as ctx:
        def sb(name, shape):
            return ctx.enter_context(nc.sbuf_tensor(name, shape, F32))

        def sem(name):
            return ctx.enter_context(nc.semaphore(name))

        X, Z = sb("X", [P, TILES * D]), sb("Z", [P, TILES * D])
        names = ["ident", "wqkv", "wo0", "bqkv", "bo0", "ln_w", "ln_b",
                 "w1", "w2", "gate", "rev", "w_in", "wo1", "b_in", "bo1", "pos", "wgu", "wd", "router", "pick"]
        t = {n: sb(n, [P, args[n].shape[1]]) for n in names}
        early = names[:7]
        loaded, later = sem("loaded"), sem("later")
        x_loaded = [sem("x_first"), sem("x_rest")]
        x_dram = args["x"].rearrange("(n p) d -> p n d", p=P)
        X3 = X[:, :].rearrange("p (n d) -> p n d", d=D)
        cut = X_FIRST * TPB

        def load(sp):
            sp.dma_start(X3[:, 0:cut, :], x_dram[:, 0:cut, :]).then_inc(x_loaded[0], 16)
            for n in early:
                sp.dma_start(t[n][:, :], args[n]).then_inc(loaded, 16)
            sp.dma_start(X3[:, cut:, :], x_dram[:, cut:, :]).then_inc(x_loaded[1], 16)
            for n in names[7:]:
                sp.dma_start(t[n][:, :], args[n]).then_inc(later, 16)
            sp.wait_ge(later, 16 * len(names[7:]))

        first_attention(nc, X, Z, t["ident"], dict(
            wqkv=t["wqkv"], wo=t["wo0"], bqkv=t["bqkv"], bo=t["bo0"], ln_w=t["ln_w"], ln_b=t["ln_b"],
            x_loaded=x_loaded, loaded=loaded, loads=len(early), load=load))
        first_ffn(nc, X, Z, t["ident"], dict(w1=t["w1"], w2=t["w2"], gate=t["gate"], rev=t["rev"]))
        second_attention(nc, X, Z, t["ident"], dict(w=t["w_in"], wo=t["wo1"], b=t["b_in"], bo=t["bo1"], pos=t["pos"]))
        second_ffn(nc, X, Z, t["ident"], dict(wgu=t["wgu"], wd=t["wd"], router=t["router"], rev=t["rev"],
                                              pick=t["pick"]), out)


def lay_out(i):
    def rows(*vectors):
        v = np.concatenate(vectors)
        return np.ascontiguousarray(np.broadcast_to(v, (P, v.shape[0])))

    def chunks_of(w):
        e, d, hid = w.shape
        return w.reshape(e, d, hid // P, P).transpose(3, 0, 2, 1).reshape(P, -1)

    w1 = np.concatenate([i["L0_ffn_shared_w1"][None], i["L0_ffn_experts_w1"]])
    w2 = np.concatenate([i["L0_ffn_shared_w2"][None], i["L0_ffn_experts_w2"]])
    n, d, f = i["L1_ffn_Wg"].shape
    pairs = [i[w].reshape(n // 2, 2, d, f).transpose(2, 0, 1, 3).reshape(d, n // 2, 2 * f)
             for w in ("L1_ffn_Wg", "L1_ffn_Wu")]
    wgu = np.stack([np.concatenate([sh[:, None, :], w], 1)
                    for sh, w in zip((i["L1_ffn_Sg"], i["L1_ffn_Su"]), pairs)], 2)
    wd = np.concatenate([i["L1_ffn_Sd"][None], i["L1_ffn_Wd"].reshape(n // 2, 2 * f, d)])
    p = np.arange(P)
    pos, wpos = i["L1_attn_pos_embedding"], i["L1_attn_w_pos_embedding"]
    pick = np.zeros((P, n // 2, P), np.float32)
    for e in range(n):
        for row in (e, n + e):
            pick[row, e // 2, (e % 2) * f:(e % 2 + 1) * f] = 1
    return {
        "x": i["L0_attn_hidden_states"].reshape(B * S, D),
        "ident": np.eye(P, dtype=np.float32),
        "wqkv": np.concatenate([i["L0_attn_Wq"], i["L0_attn_Wk"], i["L0_attn_Wv"]], 1),
        "wo0": i["L0_attn_Wo"],
        "bqkv": rows(i["L0_attn_bq"], i["L0_attn_bk"], i["L0_attn_bv"]),
        "bo0": rows(i["L0_attn_bo"]),
        "ln_w": i["L0_attn_ln_w"][:, None],
        "ln_b": i["L0_attn_ln_b"][:, None],
        "w1": w1.transpose(2, 0, 1).reshape(D, -1),
        "w2": chunks_of(w2),
        "gate": i["L0_ffn_gate_w"].T,
        "rev": rows(np.arange(16, 0, -1).astype(np.float32)),
        "w_in": np.concatenate([i["L1_attn_w_v"], i["L1_attn_w_wqk"], i["L1_attn_w_qk"]], 1),
        "wo1": i["L1_attn_w_out"],
        "b_in": rows(i["L1_attn_b_v"], i["L1_attn_b_wqk"], i["L1_attn_b_qk"]),
        "bo1": rows(i["L1_attn_b_out"]),
        "pos": np.stack([pos[S - 1 - p], pos[S - 1 - P - p], wpos[S // 4 - 1 - p % (S // 4)]], 1),
        "wgu": wgu.reshape(D, -1),
        "wd": wd.transpose(1, 0, 2).reshape(P, -1),
        "router": i["L1_ffn_Wr"],
        "pick": pick.reshape(P, -1),
    }


def kernel(**inputs):
    import concourse.bacc as bacc
    from concourse.bass_utils import run_bass_kernel_spmd

    nc = bacc.Bacc("TRN2", target_bir_lowering=False, num_devices=1)
    arrays = {n: np.ascontiguousarray(v)
              for n, v in lay_out({n: np.asarray(v) for n, v in inputs.items()}).items()}
    args = {n: nc.dram_tensor("in_" + n, v.shape, F32, kind="ExternalInput").ap() for n, v in arrays.items()}
    out = nc.dram_tensor("out_x", (B * S, D), F32, kind="ExternalOutput").ap()
    sandwich(nc, args, out)
    r = run_bass_kernel_spmd(nc, [{"in_" + n: v for n, v in arrays.items()}], core_ids=[0])
    return r.results[0]["out_x"].reshape(B, S, D)
```

```python
from contextlib import ExitStack

import numpy as np

import concourse.bass as bass
from concourse import mybir

F32 = mybir.dt.float32
F32R = mybir.dt.float32r
ALU = mybir.AluOpType
ACT = mybir.ActivationFunctionType
AX = mybir.AxisListType

P = 128
D = 128
B, S = 16, 256
TILES = B * S // P
TPB = S // P
H, HD = 16, 8
G = 4
NG = H // G
UNITS = B * NG
SLOT = 32
SHIFT, BIAS_HI, BIAS_LO, WIN_A, WIN_B = 24, 25, 26, 27, 28
EPS = 1e-5
FAR = -1.0e30
RING = 8


def clip(n, top):
    return min(max(n, 0), top)


def before(step, lead=0):
    return clip(-(-step // NG) + lead, B)


class Step:

    def __init__(self, k, i=None, first=1, size=2 * NG):
        self.k, self.i, self.first, self.size = k, i, first, size

    def at(self, count):
        n = count(self.k)
        if self.i is None:
            return n
        grow = count(self.k + self.size) - n
        if grow == 0:
            return n
        return (self.i - self.first) * grow + n


X_FIRST = 2
ROUND = 2 * NG


def wait(eng, sem, value):
    if not isinstance(value, int) or value > 0:
        eng.wait_ge(sem, value)


def tiles(st, lead):
    return bass.ds(st.at(lambda k: (k // NG + lead) * TPB * D), TPB * D)


def stacked(v):
    return v.rearrange("p n s -> p (n s)").bitcast(F32)


def hold(eng, sem, value, passed):
    wait(eng, sem, value)
    if not isinstance(value, int):
        eng.sem_inc(passed, 1)


def first_attention(nc, X, Z, ident, a):
    FIRST, LAST = -3 * NG, UNITS + 3 * NG - 1
    LOOP = (2, B // 2 - 2)

    A_ORDER = ("T1", "T2", "K", "xT", "yT", "Q")
    B_ORDER = ("qp", "kp", "vp", "O2", "op", "O1")

    def steps(eng):
        for k in range(FIRST, LOOP[0] * ROUND):
            yield Step(k)
        with eng.Fori(*LOOP) as i:
            for j in range(ROUND):
                yield Step(LOOP[0] * ROUND + j, i, LOOP[0])
        for k in range(LOOP[1] * ROUND, LAST):
            yield Step(k)

    def unit(n):
        return 0 <= n < UNITS

    def batch(n):
        return 0 <= n < B

    with ExitStack() as ctx:
        def sb(name, shape, dt=F32):
            return ctx.enter_context(nc.sbuf_tensor("a0_" + name, shape, dt))

        def pb(name, shape):
            return ctx.enter_context(nc.psum_tensor("a0_" + name, shape, F32))

        def sem(name):
            return ctx.enter_context(nc.semaphore("a0_" + name))

        z1 = sb("z1", [P, TPB, D])
        qk = sb("qk", [P, 2, TPB, D])
        sq = sb("sq", [P, 2, TPB, D])
        scaled = sb("scaled", [P, 2, TPB, D])
        ss = sb("ss", [P, 2 * TPB * H])
        rn = sb("rn", [P, 2 * TPB * H])
        vt = sb("vt", [P, 2, TPB, D])
        qt = sb("qt", [P, 2, TPB * H, SLOT], F32R)
        kt = sb("kt", [P, 2, TPB * H, SLOT], F32R)
        state = sb("state", [P, TPB * G, HD])
        qt2 = sb("qt2", [P, 2, TPB * G, SLOT], F32R)
        r1 = sb("r1", [P, TPB * G])
        r2 = sb("r2", [P, TPB * G])
        out2 = sb("out2", [P, 2, TPB, D])
        y = sb("y", [P, TPB, D])
        bn = sb("bn", [P, 2 * TPB, 6])
        mv_a = sb("mv_a", [P, 2 * TPB, 2])
        mv_b = sb("mv_b", [P, 2 * TPB, 2])
        rs_a = sb("rs_a", [P, 2 * TPB])
        rs_b = sb("rs_b", [P, 2 * TPB])
        ve = sb("ve", [P, 2 * TPB])
        half = sb("half", [P, 2 * TPB * H])
        xT = sb("xT", [P, S])
        yT = sb("yT", [P, S])
        ks = sb("ks", [P, 2, S], F32R)
        kpad = sb("kpad", [P, RING, G, S], F32R)
        qs1 = sb("qs1", [P, RING, S], F32R)
        qs2 = sb("qs2", [P, 2, S], F32R)
        qs2m = sb("qs2m", [P, S], F32R)
        v32 = sb("v32", [P, RING, TPB, G, SLOT])
        p1 = sb("p1", [P, 2, G, TPB, S])
        p2 = sb("p2", [P, 2, G, TPB, S])
        o1 = sb("o1", [P, S])
        o2 = sb("o2", [P, S])
        ps_s = pb("ps_s", [P, 2, 1024])
        ps_m = pb("ps_m", [P, 2, S])
        ps_o = pb("ps_o", [P, 512])[:, 0:S]
        ps_a = pb("ps_a", [P, 512])[:, 0:S]
        ps_b = pb("ps_b", [P, 512])[:, 0:S]

        tiles_ready = sem("tiles_ready")
        scores_full, exp_done = sem("scores_full"), sem("exp_done")
        o1_full, o1_copied = sem("o1_full"), sem("o1_copied")
        o2_full, o2_copied = sem("o2_full"), sem("o2_copied")
        max_full, max_done = sem("max_full"), sem("max_done")
        a_full, a_done = sem("a_full"), sem("a_done")
        b_full, b_done = sem("b_full"), sem("b_done")
        qt2_ready = sem("qt2_ready")
        kpad_loaded = [sem(f"kpad_loaded{n}") for n in range(RING)]
        v_ready = sem("v_ready")
        recip1, state_ready, recip2 = sem("recip1"), sem("state_ready"), sem("recip2")
        z1_ready, stats_a, stats_b = sem("z1_ready"), sem("stats_a"), sem("stats_b")
        rs_a_ready, rs_b_ready, pool_ve = sem("rs_a_ready"), sem("rs_b_ready"), sem("pool_ve")
        squares, norms, clipped, rn_ready = sem("squares"), sem("norms"), sem("clipped"), sem("rn_ready")
        qk_scaled, parts_hi, stacks_ready = sem("qk_scaled"), sem("parts_hi"), sem("stacks_ready")
        bn_done, x_part, x_new, z_new = (
            sem("bn_done"), sem("x_part"), sem("x_new"), sem("z_new"))
        z0_ready, zb_ready = sem("z0_ready"), sem("zb_ready")
        set_up, pool_set_up, kpad_zero = sem("set_up"), sem("pool_set_up"), sem("kpad_zero")
        passed = sem("passed")
        block = ctx.enter_context(nc.Block())

        def a_count(k, task):
            n = (clip(k - 2, UNITS) + clip(k - 3, UNITS) + 2 * clip(k + NG, UNITS)
                 + before(k - 1, -2) + before(k - 2, 3))
            b, r = k // NG, k % NG
            live = {"T1": unit(k - 2), "T2": unit(k - 3), "K": unit(k + NG), "Q": unit(k + NG),
                    "yT": r == 1 and batch(b - 2), "xT": r == 2 and batch(b + 3)}
            for name in A_ORDER:
                n += live[name]
                if name == task:
                    return n

        def b_count(k, task):
            n = 3 * before(k - 3, 3) + clip(k - 4, UNITS) + before(k - 2, -2) + clip(k - 1, UNITS)
            b, r = k // NG, k % NG
            projects = r == 3 and batch(b + 3)
            live = {"qp": projects, "kp": projects, "vp": projects, "O2": unit(k - 4),
                    "op": r == 2 and batch(b - 2), "O1": unit(k - 1)}
            for name in B_ORDER:
                n += live[name]
                if name == task:
                    return n

        def chunks(k, which):
            n = 2 * clip(k, UNITS) + 2 * clip(k - 3, UNITS)
            order = [unit(k), unit(k), unit(k - 3), unit(k - 3)]
            return n + sum(order[:which + 1])

        def bn_count(k, which):
            n = before(k, -3) + before(k, 3) + before(k - 1, -3) + before(k - 1, 3)
            live = [("y", k % NG == 0 and batch(k // NG - 3)), ("x", k % NG == 0 and batch(k // NG + 3)),
                    ("z", k % NG == 1 and batch(k // NG + 3)), ("new", k % NG == 1 and batch(k // NG - 3))]
            for name, on in live:
                n += on
                if name == which:
                    return n

        @block.sync
        def _(sp):
            a["load"](sp)
            sp.wait_ge(kpad_zero, 1)
            for st in steps(sp):
                k = st.k
                if not unit(k + NG):
                    continue
                hold(sp, a_done, st.at(lambda k: a_count(k, "K")), passed)
                if k - NG >= 0:
                    hold(sp, scores_full, st.at(lambda k: chunks(k - 1, 3)), passed)
                u = k + NG
                for j in range(G):
                    rows = slice(SLOT * j, SLOT * j + SLOT)
                    sp.dma_start(kpad[rows, u % RING, j, :].bitcast(F32), ks[rows, u % 2, :].bitcast(F32)
                                 ).then_inc(kpad_loaded[u % RING], 16)
            sp.wait_ge(a["later"], 16 * a["laters"])

        @block.tensor
        def _(pe):
            pe.wait_ge(a["loaded"], 16 * a["loads"])

            def wait_b(st, task):
                wait(pe, b_done, st.at(lambda k: b_count(k, task) - 1))

            def wait_a(st, task):
                wait(pe, a_done, st.at(lambda k: a_count(k, task) - 1))

            def score_chunk(st, which, q):
                u = st.k if which < 2 else st.k - 3
                wait(pe, exp_done, st.at(lambda k: chunks(k, which) - 2))
                n = chunks(st.k, which) - 1
                for jj in range(2):
                    j = 2 * (which % 2) + jj
                    for t in range(TPB):
                        last = nc.tensor.matmul(ps_s[:, n % 2, jj * 512 + t * S:jj * 512 + (t + 1) * S],
                                                kpad[:, u % RING, j, t * P:(t + 1) * P], q, start=True, stop=True)
                last.then_inc(scores_full, 1)

            def maxima(st, part):
                if not unit(st.k - 2):
                    return
                u, t, c = st.k - 2, part // 2, part % 2
                wait(pe, max_done, st.at(lambda k: 4 * clip(k - 2, UNITS) + part))
                nc.tensor.matmul(ps_m[:, :, :].rearrange("p a b -> p (a b)"), qs2[:, u % 2, t * P:(t + 1) * P],
                                 kpad[:, u % RING, 2 * c:2 * c + 2, :].rearrange("p a b -> p (a b)"),
                                 start=True, stop=True).then_inc(max_full, 1)

            def attend(u, probs, full):
                for t in range(TPB):
                    for j in range(G):
                        last = nc.tensor.matmul(ps_o[SLOT * j:SLOT * (j + 1), :], v32[:, u % RING, t, j, :],
                                                probs[:, u % 2, j, t, :], start=t == 0, stop=t == TPB - 1)
                last.then_inc(full, 1)

            def transposes(out, parts, done):
                for t in range(TPB):
                    last = nc.tensor.transpose(out[:, t * P:(t + 1) * P], parts(t), ident[:, :])
                last.then_inc(done, 1)

            def project(st, n, task):
                wait_b(st, task)
                for t in range(TPB):
                    last = nc.tensor.matmul(ps_b[:, t * P:(t + 1) * P], xT[:, t * P:(t + 1) * P],
                                            a["wqkv"][:, n * D:(n + 1) * D], start=True, stop=True)
                last.then_inc(b_full, 1)

            for st in steps(pe):
                k = st.k
                b, r = k // NG, k % NG
                projects = r == 3 and batch(b + 3)
                if unit(k):
                    pe.wait_ge(kpad_loaded[k % RING], st.at(lambda k: 64 * (k // RING + 1)))
                    pe.wait_ge(a_done, st.at(lambda k: a_count(k - NG, "Q")))
                    score_chunk(st, 0, qs1[:, k % RING, :])
                if projects:
                    pe.wait_ge(a_done, st.at(lambda k: a_count(k - 1, "xT")))
                    project(st, 0, "qp")
                if unit(k - 2):
                    pe.wait_ge(qt2_ready, st.at(lambda k: k - 1))
                    wait_a(st, "T1")
                    transposes(ps_a, lambda t: stacked(qt2[:, k % 2, t * G:(t + 1) * G, :]), a_full)
                if unit(k - 4):
                    pe.wait_ge(exp_done, st.at(lambda k: chunks(k - 1, 3)))
                    wait(pe, o1_copied, st.at(lambda k: clip(k - 1, UNITS)))
                    attend(k - 4, p2, o2_full)
                if unit(k):
                    score_chunk(st, 1, qs1[:, k % RING, :])
                if unit(k - 2):
                    pe.wait_ge(a_done, st.at(lambda k: a_count(k, "T1")))
                maxima(st, 0)
                if projects:
                    project(st, 1, "kp")
                if unit(k - 3):
                    wait_a(st, "T2")
                    pe.wait_ge(max_done, st.at(lambda k: 4 * (k - 2)))
                    transposes(ps_a, lambda t: stacked(qt2[:, (k - 3) % 2, t * G:(t + 1) * G, :]), a_full)
                if unit(k - 1):
                    pe.wait_ge(exp_done, st.at(lambda k: chunks(k - 1, 1)))
                    pe.wait_ge(v_ready, st.at(lambda k: k))
                    wait(pe, o2_copied, st.at(lambda k: clip(k - 3, UNITS)))
                    attend(k - 1, p1, o1_full)
                if projects:
                    project(st, 2, "vp")
                if unit(k + NG):
                    nb, g = (k + NG) // NG, r
                    pe.wait_ge(stacks_ready, st.at(lambda k: 2 * ((k + NG) // NG + 1)))
                    wait_a(st, "K")
                    transposes(ps_a, lambda t: stacked(kt[:, nb % 2, t * H + g * G:t * H + (g + 1) * G, :]), a_full)
                maxima(st, 1)
                if r == 2 and batch(b + 3):
                    pe.wait_ge(z1_ready, st.at(lambda k: k // NG + 4))
                    wait_a(st, "xT")
                    transposes(ps_a, lambda t: z1[:, t, :], a_full)
                if unit(k - 4):
                    wait_b(st, "O2")
                    pe.wait_ge(o2_copied, st.at(lambda k: k - 3))
                    transposes(ps_b, lambda t: o2[:, t * P:(t + 1) * P], b_full)
                if r == 1 and batch(b - 2):
                    pe.wait_ge(b_done, st.at(lambda k: b_count(k - 2, "O2")))
                    wait_a(st, "yT")
                    transposes(ps_a, lambda t: out2[:, b % 2, t, :], a_full)
                if unit(k - 3):
                    pe.wait_ge(a_done, st.at(lambda k: a_count(k, "T2")))
                    score_chunk(st, 2, qs2m[:, :])
                maxima(st, 2)
                if r == 2 and batch(b - 2):
                    pe.wait_ge(a_done, st.at(lambda k: a_count(k - 1, "yT")))
                    wait_b(st, "op")
                    for t in range(TPB):
                        last = nc.tensor.matmul(ps_b[:, t * P:(t + 1) * P], yT[:, t * P:(t + 1) * P],
                                                a["wo"][:, :], start=True, stop=True)
                    last.then_inc(b_full, 1)
                if unit(k + NG):
                    nb, g = (k + NG) // NG, r
                    pe.wait_ge(stacks_ready, st.at(lambda k: 2 * ((k + NG) // NG + 1)))
                    wait_a(st, "Q")
                    transposes(ps_a, lambda t: stacked(qt[:, nb % 2, t * H + g * G:t * H + (g + 1) * G, :]), a_full)
                if unit(k - 1):
                    wait_b(st, "O1")
                    pe.wait_ge(o1_copied, st.at(lambda k: k))
                    transposes(ps_b, lambda t: o1[:, t * P:(t + 1) * P], b_full)
                if unit(k - 3):
                    score_chunk(st, 3, qs2m[:, :])
                maxima(st, 3)

        @block.scalar
        def _(act):
            def exps(st, which, u, probs, full, used):
                act.wait_ge(scores_full, st.at(lambda k: chunks(k, which)))
                if which % 2 == 0:
                    wait(act, full, st.at(used))
                n = chunks(st.k, which) - 1
                c = which % 2
                nc.scalar.activation(probs[:, u % 2, 2 * c:2 * c + 2, :, :].rearrange("p a b c -> p (a b c)"),
                                     ps_s[:, n % 2, :], ACT.Exp).then_inc(exp_done, 1)

            def copy_a(st, task, dst):
                act.wait_ge(a_full, st.at(lambda k: a_count(k, task)))
                nc.scalar.copy(dst, ps_a).then_inc(a_done, 1)

            act.wait_ge(a["loaded"], 16 * a["loads"])
            for st in steps(act):
                k = st.k
                b, r = k // NG, k % NG
                if unit(k - 2):
                    copy_a(st, "T1", qs2[:, k % 2, :])
                if unit(k - 4):
                    act.wait_ge(o2_full, st.at(lambda k: k - 3))
                    nc.scalar.copy(o2[:, :], ps_o).then_inc(o2_copied, 1)
                if unit(k):
                    exps(st, 0, k, p1, o1_full, lambda k: k - 1)
                if unit(k - 3):
                    copy_a(st, "T2", qs2m[:, :])
                if unit(k):
                    exps(st, 1, k, p1, o1_full, lambda k: k - 1)
                if unit(k + NG):
                    u = k + NG
                    if unit(u - 2):
                        act.wait_ge(kpad_loaded[(u - 2) % RING], st.at(lambda k: 64 * ((k + NG - 2) // RING + 1)))
                    copy_a(st, "K", ks[:, u % 2, :])
                if unit(k - 1):
                    act.wait_ge(o1_full, st.at(lambda k: k))
                    nc.scalar.copy(o1[:, :], ps_o).then_inc(o1_copied, 1)
                if r == 2 and batch(b + 3):
                    act.wait_ge(a_full, st.at(lambda k: a_count(k, "xT")))
                    nc.scalar.activation(xT[:, :], ps_a, ACT.Identity, scale=a["ln_w"][:, 0:1],
                                         bias=a["ln_b"][:, 0:1]).then_inc(a_done, 1)
                if r == 1 and batch(b - 2):
                    copy_a(st, "yT", yT[:, :])
                if unit(k - 3):
                    exps(st, 2, k - 3, p2, o2_full, lambda k: k - 4)
                if unit(k + NG):
                    copy_a(st, "Q", qs1[:, (k + NG) % RING, :])
                if unit(k - 3):
                    exps(st, 3, k - 3, p2, o2_full, lambda k: k - 4)
                if r == 2 and batch(b + 2):
                    act.wait_ge(qk_scaled, st.at(lambda k: k // NG + 3))
                    if batch(b):
                        act.wait_ge(a_full, st.at(lambda k: a_count(k - 3, "Q")))
                    val, n = scaled[:].rearrange("p a t (h d) -> p a (t h) d", d=HD), TPB * H
                    qd, kd = qt[:, b % 2, :, :], kt[:, b % 2, :, :]
                    nc.scalar.copy(qd[:, :, 0:2 * HD].rearrange("p n (c d) -> p n c d", c=2),
                                   val[:, 0, :, :].unsqueeze(2).to_broadcast([P, n, 2, HD]))
                    nc.scalar.copy(kd[:, :, 0:4 * HD].rearrange("p n (c d) -> p n c d", c=2)[:, :, :, 0:HD],
                                   val[:, 1, :, :].unsqueeze(2).to_broadcast([P, n, 2, HD])).then_inc(parts_hi, 1)

        @block.vector
        def _(dve):
            nc.vector.memset(mv_a[:, :, :], 1.0).then_inc(set_up, 1)
            nc.vector.memset(mv_b[:, :, :], 1.0).then_inc(set_up, 1)
            nc.vector.memset(qt2[:].rearrange("p a b c -> p (a b c)").bitcast(F32), 0.0).then_inc(set_up, 1)
            dve.wait_ge(set_up, 3)
            dve.wait_ge(a["loaded"], 16 * a["loads"])

            def normalise(x, mv, rs, n, out):
                for t in range(TPB):
                    last = nc.vector.tensor_scalar(out(t), x(t), mv[:, n + t, 0:1], rs[:, n + t:n + t + 1],
                                                   ALU.subtract, ALU.mult)
                return last

            def heads_out(v):
                return v.rearrange("p (n s) -> p n s", s=SLOT)

            def rows_of(M, st, lead):
                return M[:, tiles(st, lead)].rearrange("p (t d) -> p t d", d=D)

            def stats(x, place):
                for t in range(TPB):
                    last = nc.vector.bn_stats(bn[:, place + t, :], x[:, t, :])
                last.then_inc(bn_done, 1)

            def moments(st, which, place, mv):
                hold(dve, bn_done, st.at(lambda k: bn_count(k, which)), passed)
                for t in range(TPB):
                    last = nc.vector.bn_aggr(mv[:, place + t, :], bn[:, place + t, :])
                return last

            def projected(st, n, task, dst):
                dve.wait_ge(b_full, st.at(lambda k: b_count(k, task)))
                bias = a["bqkv"][:, n * D:(n + 1) * D].unsqueeze(1).to_broadcast([P, TPB, D])
                nc.vector.tensor_tensor(dst, ps_b.rearrange("p (t d) -> p t d", d=D), bias, ALU.add).then_inc(b_done, 1)

            for st in steps(dve):
                k = st.k
                b, r = k // NG, k % NG

                def maxima(part):
                    if not unit(k - 2):
                        return
                    dve.wait_ge(max_full, st.at(lambda k: 4 * clip(k - 2, UNITS) + part + 1))
                    nc.vector.tensor_reduce(qt2[:, k % 2, 2 * part:2 * part + 2, SHIFT], ps_m[:, :, :], AX.X, ALU.max,
                                            negate=True).then_inc(max_done, 1)

                if r == 0 and batch(b + 2):
                    dve.wait_ge(squares, st.at(lambda k: k // NG + 3))
                    nc.vector.tensor_reduce(ss[:, :], sq[:].rearrange("p a t (h d) -> p (a t h) d", d=HD), AX.X,
                                            ALU.add).then_inc(norms, 1)
                if r == 2 and batch(b + 3):
                    dve.wait_ge(rs_b_ready, st.at(lambda k: k // NG + 4))
                    if batch(b + 2):
                        dve.wait_ge(a_full, st.at(lambda k: a_count(k - NG, "xT")))
                    zz = rows_of(Z, st, 3)
                    normalise(lambda t: zz[:, t, :], mv_b, rs_b, TPB, lambda t: z1[:, t, :]).then_inc(z1_ready, 1)
                if r == 1 and batch(b - 3):
                    dve.wait_ge(rs_a_ready, st.at(lambda k: k // NG + 4))
                    normalise(lambda t: y[:, t, :], mv_a, rs_a, 0, lambda t: y[:, t, :]).then_inc(x_part, 1)
                if r == 2 and batch(b + 2):
                    dve.wait_ge(rn_ready, st.at(lambda k: 4 * (k // NG + 3)))
                    wait(dve, stacks_ready, st.at(lambda k: 2 * (k // NG + 2)))
                    nc.vector.tensor_tensor(
                        scaled[:].rearrange("p a t (h d) -> p (a t h) d", d=HD),
                        qk[:].rearrange("p a t (h d) -> p (a t h) d", d=HD),
                        rn[:, :].unsqueeze(2).to_broadcast([P, 2 * TPB * H, HD]), ALU.mult).then_inc(qk_scaled, 1)
                if r == 0 and batch(b - 3):
                    hold(dve, b_done, st.at(lambda k: b_count(k - 2, "op")), passed)
                    stats(y, 0)
                if r == 1 and batch(b + 3):
                    dve.wait_ge(rs_a_ready, st.at(lambda k: k // NG + 4))
                    xx, zz = rows_of(X, st, 3), rows_of(Z, st, 3)
                    normalise(lambda t: xx[:, t, :], mv_a, rs_a, TPB, lambda t: zz[:, t, :]).then_inc(z0_ready, 1)
                if r == 1 and batch(b - 3):
                    dve.wait_ge(x_part, st.at(lambda k: k // NG - 2))
                    xx = X[:, tiles(st, -3)]
                    nc.vector.tensor_tensor(xx, xx, y[:].rearrange("p t d -> p (t d)"), ALU.add).then_inc(x_new, 1)
                if r == 0 and batch(b + 3):
                    dve.wait_ge(a["x_loaded"][b + 3 >= X_FIRST], 16)
                    stats(rows_of(X, st, 3), TPB)
                if r == 3 and batch(b + 3):
                    if batch(b + 2):
                        dve.wait_ge(qk_scaled, st.at(lambda k: k // NG + 3))
                    projected(st, 0, "qp", qk[:, 0, :, :])
                maxima(0)
                if r == 1 and batch(b + 3):
                    hold(dve, z0_ready, st.at(lambda k: k // NG + 4), passed)
                    stats(rows_of(Z, st, 3), TPB)
                if r == 3 and batch(b + 3):
                    projected(st, 1, "kp", qk[:, 1, :, :])
                    wait(dve, v_ready, st.at(lambda k: NG * (k // NG + 2)))
                    projected(st, 2, "vp", vt[:, (b + 3) % 2, :, :])
                if r == 1 and batch(b - 3):
                    hold(dve, x_new, st.at(lambda k: k // NG - 2), passed)
                    stats(rows_of(X, st, -3), 0)
                if r == 0 and batch(b - 3):
                    last = moments(st, "y", 0, mv_a)
                    if not batch(b + 3):
                        last.then_inc(stats_a, 1)
                if r == 2 and batch(b - 3):
                    dve.wait_ge(rs_b_ready, st.at(lambda k: k // NG + 4))
                    xx, zz = rows_of(X, st, -3), rows_of(Z, st, -3)
                    normalise(lambda t: xx[:, t, :], mv_b, rs_b, 0, lambda t: zz[:, t, :]).then_inc(z_new, 1)
                if r == 1 and batch(b + 3):
                    last = moments(st, "z", TPB, mv_b)
                    if not batch(b - 3):
                        last.then_inc(stats_b, 1)
                maxima(1)
                if unit(k - 4):
                    dve.wait_ge(b_full, st.at(lambda k: b_count(k, "O2")))
                    src = heads_out(ps_b)
                    nc.vector.reciprocal(r2[:, :], src[:, :, HD]).then_inc(recip2, 1)
                    dve.wait_ge(recip2, st.at(lambda k: k - 3))
                    dst = out2[:, (b - 1) % 2, :, r * G * HD:(r + 1) * G * HD]
                    nc.vector.tensor_tensor(
                        dst.rearrange("p t (h d) -> p t h d", d=HD),
                        src[:, :, 0:HD].rearrange("p (t h) d -> p t h d", t=TPB),
                        r2[:, :].rearrange("p (t h) -> p t h", t=TPB).unsqueeze(3).to_broadcast([P, TPB, G, HD]),
                        ALU.mult).then_inc(b_done, 1)
                if r == 2 and batch(b - 2):
                    dve.wait_ge(b_full, st.at(lambda k: b_count(k, "op")))
                    dve.wait_ge(zb_ready, st.at(lambda k: k // NG - 1))
                    nc.vector.tensor_tensor(y[:].rearrange("p t d -> p (t d)"), ps_b, Z[:, tiles(st, -2)],
                                            ALU.add).then_inc(b_done, 1)
                if r == 1 and batch(b - 3):
                    moments(st, "new", 0, mv_b).then_inc(stats_b, 1)
                if r == 0 and batch(b + 3):
                    moments(st, "x", TPB, mv_a).then_inc(stats_a, 1)
                maxima(2)
                if unit(k - 1):
                    dve.wait_ge(b_full, st.at(lambda k: b_count(k, "O1")))
                    src = heads_out(ps_b)
                    nc.vector.reciprocal(r1[:, :], src[:, :, HD]).then_inc(recip1, 1)
                    new = qt2[:, (k - 1) % 2, :, :]
                    dve.wait_ge(recip1, st.at(lambda k: k))
                    nc.vector.memset(new[:, :, SHIFT].bitcast(F32), 0.0)
                    nc.vector.tensor_tensor(state[:, :, :], src[:, :, 0:HD],
                                            r1[:, :].unsqueeze(2).to_broadcast([P, TPB * G, HD]), ALU.mult)
                    nc.vector.tensor_tensor(
                        new[:, :, 0:2 * HD].rearrange("p n (c d) -> p n c d", c=2),
                        src[:, :, 0:HD].unsqueeze(2).to_broadcast([P, TPB * G, 2, HD]),
                        r1[:, :].unsqueeze(2).unsqueeze(3).to_broadcast([P, TPB * G, 2, HD]),
                        ALU.mult).then_inc(b_done, 1)
                    dve.wait_ge(b_done, st.at(lambda k: b_count(k, "O1")))
                    nc.vector.tensor_tensor(new[:, :, 2 * HD:3 * HD], state[:, :, :],
                                            new[:, :, 0:HD].bitcast(F32), ALU.subtract).then_inc(qt2_ready, 1)
                if r == 3 and batch(b + 3):
                    dve.wait_ge(b_done, st.at(lambda k: b_count(k, "kp")))
                    flat = "p a t d -> p (a t d)"
                    nc.vector.tensor_tensor(sq[:].rearrange(flat), qk[:].rearrange(flat), qk[:].rearrange(flat),
                                            ALU.mult).then_inc(squares, 1)
                maxima(3)
            dve.wait_ge(z_new, B)

        @block.gpsimd
        def _(pool):
            nc.gpsimd.memset(half[:, :], -0.5)
            nc.gpsimd.memset(qt[:].rearrange("p a b c -> p (a b c)").bitcast(F32), 0.0)
            nc.gpsimd.memset(kt[:].rearrange("p a b c -> p (a b c)").bitcast(F32), 0.0).then_inc(pool_set_up, 1)
            pool.wait_ge(pool_set_up, 1)
            nc.gpsimd.memset(kt[:, :, :, SHIFT].bitcast(F32), 1.0).then_inc(pool_set_up, 1)
            pool.wait_ge(pool_set_up, 2)

            def rstd(st, stats, mv, rs, ready):
                hold(pool, stats, st.at(lambda k: k // NG + 4), passed)
                nc.gpsimd.tensor_scalar(ve[:, :], mv[:, :, 1], EPS, None, ALU.add).then_inc(pool_ve, 1)
                hold(pool, pool_ve, st.at(lambda k: 2 * (k // NG + 3) + k % NG + 1), passed)
                nc.gpsimd.tensor_tensor(rs[:, :], ve[:, :], half[:, 0:2 * TPB], ALU.pow).then_inc(ready, 1)

            def norm_powers(part):
                c = 2 * TPB * H // 4
                nc.gpsimd.tensor_tensor(rn[:, part * c:(part + 1) * c], ss[:, part * c:(part + 1) * c],
                                        half[:, 0:c], ALU.pow).then_inc(rn_ready, 1)

            for st in steps(pool):
                k = st.k
                b, r = k // NG, k % NG
                val = scaled[:].rearrange("p a t (h d) -> p a (t h) d", d=HD)
                n = TPB * H
                qd, kd = qt[:, b % 2, :, :], kt[:, b % 2, :, :]
                if r == 3 and batch(b + 2):
                    hold(pool, parts_hi, st.at(lambda k: k // NG + 3), passed)
                    nc.gpsimd.tensor_tensor(qd[:, :, 2 * HD:3 * HD], val[:, 0, :, :], qd[:, :, 0:HD].bitcast(F32),
                                            ALU.subtract).then_inc(stacks_ready, 1)
                    nc.gpsimd.tensor_tensor(kd[:, :, HD:2 * HD], val[:, 1, :, :], kd[:, :, 0:HD].bitcast(F32),
                                            ALU.subtract).then_inc(stacks_ready, 1)
                if r == 0 and batch(b + 2):
                    hold(pool, norms, st.at(lambda k: k // NG + 3), passed)
                    nc.gpsimd.tensor_scalar(ss[:, :], ss[:, :], 1e-24, None, ALU.max).then_inc(clipped, 1)
                    hold(pool, clipped, st.at(lambda k: k // NG + 3), passed)
                if r < 2 and batch(b + 2):
                    norm_powers(2 * r)
                if unit(k + NG):
                    u = k + NG
                    hold(pool, b_done, st.at(lambda k: b_count(NG * (k // NG - 2) + 3, "vp")), passed)
                    hold(pool, o2_full, st.at(lambda k: clip(k - NG + 1, UNITS)), passed)
                    hs = slice(r * G * HD, (r + 1) * G * HD)
                    nc.gpsimd.tensor_copy(v32[:, u % RING, :, :, 0:HD],
                                          vt[:, (b + 1) % 2, :, hs].rearrange("p t (h d) -> p t h d", d=HD)
                                          ).then_inc(v_ready, 1)
                if r == 0 and (batch(b - 3) or batch(b + 3)):
                    rstd(st, stats_a, mv_a, rs_a, rs_a_ready)
                if r == 1 and (batch(b - 3) or batch(b + 3)):
                    rstd(st, stats_b, mv_b, rs_b, rs_b_ready)
                if r < 2 and batch(b + 2):
                    norm_powers(2 * r + 1)
                if r == 3 and batch(b + 3):
                    hold(pool, z1_ready, st.at(lambda k: k // NG + 4), passed)
                    zz = Z[:, tiles(st, 3)].rearrange("p (t d) -> p t d", d=D)
                    nc.gpsimd.tensor_tensor(zz, zz, a["bo"][:, :].unsqueeze(1).to_broadcast([P, TPB, D]),
                                            ALU.add).then_inc(zb_ready, 1)
                if k == FIRST + 3:
                    nc.gpsimd.memset(v32[:].rearrange("p a b c d -> p (a b c d)"), 0.0).then_inc(pool_set_up, 1)
                    nc.gpsimd.memset(kpad[:].rearrange("p a b c -> p (a b c)").bitcast(F32), 0.0
                                     ).then_inc(kpad_zero, 1)
                    pool.wait_ge(pool_set_up, 3)
                    nc.gpsimd.memset(v32[:, :, :, :, HD].rearrange("p a b c -> p (a b c)"),
                                     1.0).then_inc(pool_set_up, 1)
                    pool.wait_ge(pool_set_up, 4)


def second_attention(nc, X, Z, ident, a):
    FIRST, LAST = -2 * NG, UNITS + 2 * NG
    LOOP = (1, B // 2 - 1)
    KEEP = 4
    W = S // 4
    SCALE = float(HD) ** -0.5
    WINDOWED, GLOBAL = 0, 1

    A_ORDER = ("Mg", "Kw", "Mw", "Qg", "yT", "xT", "Kg", "Qw")
    B_ORDER = ("wq", "q", "v", "wk", "k", "Og", "Ow", "op")

    def steps(eng):
        for k in range(FIRST, LOOP[0] * ROUND):
            yield Step(k)
        with eng.Fori(*LOOP) as i:
            for j in range(ROUND):
                yield Step(LOOP[0] * ROUND + j, i, LOOP[0])
        for k in range(LOOP[1] * ROUND, LAST):
            yield Step(k)

    def unit(n):
        return 0 <= n < UNITS

    def batch(n):
        return 0 <= n < B

    with ExitStack() as ctx:
        def sb(name, shape, dt=F32):
            return ctx.enter_context(nc.sbuf_tensor("a1_" + name, shape, dt))

        def pb(name):
            return ctx.enter_context(nc.psum_tensor("a1_" + name, [P, 512], F32))

        def sem(name):
            return ctx.enter_context(nc.semaphore("a1_" + name))

        proj = sb("proj", [P, 4, TPB, D])
        vt = sb("vt", [P, 2, TPB, D])
        qt = sb("qt", [P, 2, 2, TPB * H, SLOT], F32R)
        kt = sb("kt", [P, 2, 2, TPB * H, SLOT], F32R)
        rg, rw = sb("rg", [P, TPB * G]), sb("rw", [P, TPB * G])
        og, ow = sb("og", [P, TPB * G, HD]), sb("ow", [P, TPB * G, HD])
        out = sb("out", [P, 2, TPB, D])
        y = sb("y", [P, TPB, D])
        bn = sb("bn", [P, TPB, 6])
        mv_y, mv_x = sb("mv_y", [P, TPB, 2]), sb("mv_x", [P, TPB, 2])
        rs_y, rs_x = sb("rs_y", [P, TPB]), sb("rs_x", [P, TPB])
        ve = sb("ve", [P, TPB])
        half = sb("half", [P, TPB])
        bias_hi, bias_lo = sb("bias_hi", [P, TPB + 1], F32R), sb("bias_lo", [P, TPB + 1], F32R)
        bwq = sb("bwq", [P, D])
        zc = sb("zc", [P, S])
        xT, yT = sb("xT", [P, S]), sb("yT", [P, S])
        ks = sb("ks", [P, 2, 2, S], F32R)
        kpad = sb("kpad", [P, KEEP, 2, G, S], F32R)
        qs = sb("qs", [P, 2, 2, S], F32R)
        qsm = sb("qsm", [P, 2, S], F32R)
        v32 = sb("v32", [P, KEEP, TPB, G, SLOT])
        pg = sb("pg", [P, 2, G, TPB, S])
        pw = sb("pw", [P, 2, G, TPB, P])
        otg, otw = sb("otg", [P, S]), sb("otw", [P, S])
        ps_s = ctx.enter_context(nc.psum_tensor("a1_ps_s", [P, 2, 1024], F32))
        ps_m, ps_o = pb("ps_m"), pb("ps_o")[:, 0:S]
        ps_a, ps_b = pb("ps_a")[:, 0:S], pb("ps_b")[:, 0:S]

        scores_full, exp_done = sem("scores_full"), sem("exp_done")
        g_full, g_copied, w_full, w_copied = sem("g_full"), sem("g_copied"), sem("w_full"), sem("w_copied")
        max_full, max_done = sem("max_full"), sem("max_done")
        a_full, a_done, b_full, b_done = sem("a_full"), sem("a_done"), sem("b_full"), sem("b_done")
        kpad_loaded = [sem(f"kpad_loaded{n}") for n in range(KEEP)]
        v_ready, stacks_ready, parts_hi = sem("v_ready"), sem("stacks_ready"), sem("parts_hi")
        recip_g, recip_w, zc_ready = sem("recip_g"), sem("recip_w"), sem("zc_ready")
        out_ready = sem("out_ready")
        bn_done, stats_y, stats_x = sem("bn_done"), sem("stats_y"), sem("stats_x")
        rs_y_ready, rs_x_ready, pool_step = sem("rs_y_ready"), sem("rs_x_ready"), sem("pool_step")
        x_part, x_new, z_new = sem("x_part"), sem("x_new"), sem("z_new")
        cleared, kt_cleared, kpad_zero = sem("cleared"), sem("kt_cleared"), sem("kpad_zero")
        set_up, consts = sem("set_up"), sem("consts")
        passed = sem("passed")
        block = ctx.enter_context(nc.Block())

        def a_count(k, task):
            n = (2 * clip(k - 1, UNITS) + 2 * clip(k + 2, UNITS) + 2 * clip(k + 1, UNITS)
                 + before(k - 1, 2) + before(k - 2, -1))
            b, r = k // NG, k % NG
            live = {"Mg": unit(k - 1), "Mw": unit(k - 1), "Kg": unit(k + 2), "Kw": unit(k + 2),
                    "Qg": unit(k + 1), "Qw": unit(k + 1), "xT": r == 1 and batch(b + 2),
                    "yT": r == 2 and batch(b - 1)}
            for name in A_ORDER:
                n += live[name]
                if name == task:
                    return n

        def b_count(k, task):
            n = (2 * clip(k - 2, UNITS) + 2 * before(k - 2, 2) + 2 * before(k - 3, 2) + before(k, 1)
                 + before(k - 3, -1))
            b, r = k // NG, k % NG
            live = {"wq": r == 2 and batch(b + 2), "wk": r == 2 and batch(b + 2), "q": r == 3 and batch(b + 2),
                    "k": r == 3 and batch(b + 2), "v": r == 0 and batch(b + 1), "Og": unit(k - 2),
                    "Ow": unit(k - 2), "op": r == 3 and batch(b - 1)}
            for name in B_ORDER:
                n += live[name]
                if name == task:
                    return n

        def chunk(k, which):
            return 3 * clip(k - 1, UNITS) + which + 1

        def maxes(k, part):
            return 6 * clip(k, UNITS) + part + 1

        @block.sync
        def _(sp):
            a["load"](sp)
            sp.wait_ge(kpad_zero, 1)
            for st in steps(sp):
                u = st.k + 2
                if not unit(u):
                    continue
                if unit(u - KEEP):
                    hold(sp, scores_full, st.at(lambda k: chunk(k - 1, 2)), passed)
                for kind, task in ((WINDOWED, "Kw"), (GLOBAL, "Kg")):
                    hold(sp, a_done, st.at(lambda k: a_count(k, task)), passed)
                    for j in range(G):
                        rows = slice(SLOT * j, SLOT * j + SLOT)
                        sp.dma_start(kpad[rows, u % KEEP, kind, j, :].bitcast(F32),
                                     ks[rows, u % 2, kind, :].bitcast(F32)).then_inc(kpad_loaded[u % KEEP], 16)

        @block.tensor
        def _(pe):
            def wait_a(st, task):
                wait(pe, a_done, st.at(lambda k: a_count(k, task) - 1))

            def wait_b(st, task):
                wait(pe, b_done, st.at(lambda k: b_count(k, task) - 1))

            def transposes(dst, parts, done):
                for t in range(TPB):
                    last = nc.tensor.transpose(dst[:, t * P:(t + 1) * P], parts(t), ident[:, :])
                last.then_inc(done, 1)

            def global_scores(st, c):
                u = st.k - 1
                wait(pe, exp_done, st.at(lambda k: chunk(k, c) - 2))
                n = chunk(st.k, c) - 1
                for jj in range(2):
                    for t in range(TPB):
                        last = nc.tensor.matmul(ps_s[:, n % 2, jj * 512 + t * S:jj * 512 + (t + 1) * S],
                                                kpad[:, u % KEEP, GLOBAL, 2 * c + jj, t * P:(t + 1) * P],
                                                qsm[:, GLOBAL, :], start=True, stop=True)
                last.then_inc(scores_full, 1)

            def window_scores(st):
                u = st.k - 1
                wait(pe, exp_done, st.at(lambda k: chunk(k, 2) - 2))
                n = chunk(st.k, 2) - 1
                for j in range(G):
                    for t in range(TPB):
                        tile = slice(t * P, (t + 1) * P)
                        last = nc.tensor.matmul(ps_s[:, n % 2, (j * TPB + t) * P:(j * TPB + t + 1) * P],
                                                kpad[:, u % KEEP, WINDOWED, j, tile], qsm[:, WINDOWED, tile],
                                                start=True, stop=True)
                last.then_inc(scores_full, 1)

            def maxima(st, part):
                if not unit(st.k):
                    return
                u = st.k
                wait(pe, max_done, st.at(lambda k: maxes(k, part) - 1))
                if part < 4:
                    t, c = part // 2, part % 2
                    nc.tensor.matmul(ps_m[:, :], qs[:, u % 2, GLOBAL, t * P:(t + 1) * P],
                                     kpad[:, u % KEEP, GLOBAL, 2 * c:2 * c + 2, :].rearrange("p a b -> p (a b)"),
                                     start=True, stop=True).then_inc(max_full, 1)
                else:
                    tile = slice((part - 4) * P, (part - 3) * P)
                    nc.tensor.matmul(ps_m[:, :].rearrange("p (a b) -> p a b", a=G), qs[:, u % 2, WINDOWED, tile],
                                     kpad[:, u % KEEP, WINDOWED, :, tile], start=True,
                                     stop=True).then_inc(max_full, 1)

            def stack(st, task, src, u):
                t0 = (u % NG) * G
                half, kind = (u // NG) % 2, GLOBAL if task[1] == "g" else WINDOWED
                wait_a(st, task)
                transposes(ps_a, lambda t: stacked(src[:, half, kind, t * H + t0:t * H + t0 + G, :]), a_full)

            def project(st, task):
                n = ("v", "wq", "wk", "q", "k").index(task)
                wait_b(st, task)
                for t in range(TPB):
                    last = nc.tensor.matmul(ps_b[:, t * P:(t + 1) * P], xT[:, t * P:(t + 1) * P],
                                            a["w"][:, n * D:(n + 1) * D], start=True, stop=True)
                last.then_inc(b_full, 1)

            for st in steps(pe):
                k = st.k
                b, r = k // NG, k % NG
                if unit(k - 1):
                    pe.wait_ge(max_done, st.at(lambda k: maxes(k - 1, 3)))
                    stack(st, "Mg", qt, k - 1)
                if r == 2 and batch(b + 2):
                    pe.wait_ge(a_done, st.at(lambda k: a_count(k - 1, "xT")))
                    project(st, "wq")
                if unit(k):
                    pe.wait_ge(kpad_loaded[k % KEEP], st.at(lambda k: 128 * (k // KEEP + 1)))
                    pe.wait_ge(a_done, st.at(lambda k: a_count(k - 1, "Qw")))
                if r == 3 and batch(b + 2):
                    project(st, "q")
                maxima(st, 0)
                if unit(k + 2):
                    if not unit(k + 1):
                        pe.wait_ge(consts, 1)
                    pe.wait_ge(stacks_ready, st.at(lambda k: 2 * ((k + 2) // NG) + 1))
                    stack(st, "Kw", kt, k + 2)
                if r == 0 and batch(b + 1):
                    project(st, "v")
                if unit(k - 2):
                    pe.wait_ge(exp_done, st.at(lambda k: chunk(k - 1, 1)))
                    pe.wait_ge(v_ready, st.at(lambda k: k - 1))
                    wait(pe, w_copied, st.at(lambda k: k - 2))
                    for t in range(TPB):
                        for j in range(G):
                            last = nc.tensor.matmul(ps_o[SLOT * j:SLOT * (j + 1), :], v32[:, (k - 2) % KEEP, t, j, :],
                                                    pg[:, k % 2, j, t, :], start=t == 0, stop=t == TPB - 1)
                    last.then_inc(g_full, 1)
                maxima(st, 1)
                if unit(k - 1):
                    pe.wait_ge(max_done, st.at(lambda k: maxes(k - 1, 5)))
                    stack(st, "Mw", qt, k - 1)
                if unit(k - 1):
                    pe.wait_ge(a_done, st.at(lambda k: a_count(k, "Mg")))
                    global_scores(st, 0)
                if r == 2 and batch(b + 2):
                    project(st, "wk")
                if unit(k + 1):
                    stack(st, "Qg", qt, k + 1)
                maxima(st, 2)
                if r == 3 and batch(b + 2):
                    project(st, "k")
                if unit(k - 1):
                    pe.wait_ge(a_done, st.at(lambda k: a_count(k, "Mg")))
                    global_scores(st, 1)
                if unit(k - 2):
                    pe.wait_ge(exp_done, st.at(lambda k: chunk(k - 1, 2)))
                    pe.wait_ge(g_copied, st.at(lambda k: k - 1))
                    for t in range(TPB):
                        for j in range(G):
                            last = nc.tensor.matmul(ps_o[SLOT * j:SLOT * (j + 1), t * P:(t + 1) * P],
                                                    v32[:, (k - 2) % KEEP, t, j, :], pw[:, k % 2, j, t, :],
                                                    start=True, stop=True)
                    last.then_inc(w_full, 1)
                if r == 2 and batch(b - 1):
                    pe.wait_ge(out_ready, st.at(lambda k: NG * (k // NG)))
                    wait_a(st, "yT")
                    transposes(ps_a, lambda t: out[:, (b - 1) % 2, t, :], a_full)
                if r == 1 and batch(b + 2):
                    wait_a(st, "xT")
                    pe.wait_ge(zc_ready, st.at(lambda k: k // NG + 3))
                    transposes(ps_a, lambda t: zc[:, t * P:(t + 1) * P], a_full)
                maxima(st, 3)
                if unit(k - 2):
                    wait_b(st, "Og")
                    pe.wait_ge(g_copied, st.at(lambda k: k - 1))
                    transposes(ps_b, lambda t: otg[:, t * P:(t + 1) * P], b_full)
                if unit(k - 1):
                    pe.wait_ge(a_done, st.at(lambda k: a_count(k, "Mw")))
                    window_scores(st)
                if unit(k + 2):
                    pe.wait_ge(stacks_ready, st.at(lambda k: 2 * ((k + 2) // NG) + 2))
                    stack(st, "Kg", kt, k + 2)
                maxima(st, 4)
                if unit(k - 2):
                    wait_b(st, "Ow")
                    pe.wait_ge(w_copied, st.at(lambda k: k - 1))
                    transposes(ps_b, lambda t: otw[:, t * P:(t + 1) * P], b_full)
                if unit(k + 1):
                    stack(st, "Qw", qt, k + 1)
                maxima(st, 5)
                if r == 3 and batch(b - 1):
                    pe.wait_ge(a_done, st.at(lambda k: a_count(k - 1, "yT")))
                    wait_b(st, "op")
                    for t in range(TPB):
                        last = nc.tensor.matmul(ps_b[:, t * P:(t + 1) * P], yT[:, t * P:(t + 1) * P], a["wo"][:, :],
                                                start=True, stop=True)
                    last.then_inc(b_full, 1)

        @block.scalar
        def _(act):
            def copy_a(st, task, dst):
                act.wait_ge(a_full, st.at(lambda k: a_count(k, task)))
                nc.scalar.copy(dst, ps_a).then_inc(a_done, 1)

            def global_exp(st, c):
                wait(act, g_full, st.at(lambda k: k - 2))
                act.wait_ge(scores_full, st.at(lambda k: chunk(k, c)))
                nc.scalar.activation(pg[:, (st.k - 1) % 2, 2 * c:2 * c + 2, :, :].rearrange("p a b c -> p (a b c)"),
                                     ps_s[:, (chunk(st.k, c) - 1) % 2, :], ACT.Exp).then_inc(exp_done, 1)

            for st in steps(act):
                k = st.k
                b, r = k // NG, k % NG
                if unit(k - 1):
                    copy_a(st, "Mg", qsm[:, GLOBAL, :])
                if unit(k + 2):
                    if unit(k):
                        act.wait_ge(kpad_loaded[k % KEEP], st.at(lambda k: 128 * (k // KEEP + 1)))
                    copy_a(st, "Kw", ks[:, k % 2, WINDOWED, :])
                if unit(k - 2):
                    act.wait_ge(g_full, st.at(lambda k: k - 1))
                    nc.scalar.copy(otg[:, :], ps_o).then_inc(g_copied, 1)
                if unit(k - 1):
                    copy_a(st, "Mw", qsm[:, WINDOWED, :])
                if unit(k - 1):
                    global_exp(st, 0)
                if unit(k + 1):
                    copy_a(st, "Qg", qs[:, (k + 1) % 2, GLOBAL, :])
                if unit(k - 1):
                    global_exp(st, 1)
                if r == 2 and batch(b - 1):
                    copy_a(st, "yT", yT[:, :])
                if unit(k - 2):
                    act.wait_ge(w_full, st.at(lambda k: k - 1))
                    nc.scalar.copy(otw[:, :], ps_o).then_inc(w_copied, 1)
                if r == 1 and batch(b + 2):
                    copy_a(st, "xT", xT[:, :])
                if unit(k + 2):
                    copy_a(st, "Kg", ks[:, k % 2, GLOBAL, :])
                if unit(k + 1):
                    copy_a(st, "Qw", qs[:, (k + 1) % 2, WINDOWED, :])
                if unit(k - 1):
                    wait(act, w_full, st.at(lambda k: k - 2))
                    act.wait_ge(scores_full, st.at(lambda k: chunk(k, 2)))
                    nc.scalar.activation(pw[:, (k - 1) % 2, :, :, :].rearrange("p a b c -> p (a b c)"),
                                         ps_s[:, (chunk(k, 2) - 1) % 2, :], ACT.Exp).then_inc(exp_done, 1)

        @block.vector
        def _(dve):
            nc.vector.memset(kt[:].rearrange("p a b c d -> p (a b c d)").bitcast(F32), 0.0).then_inc(kt_cleared, 1)
            nc.vector.tensor_copy(bias_hi[:, :], a["pos"][:, :]).then_inc(set_up, 1)
            nc.vector.tensor_scalar(bwq[:, :], a["b"][:, D:2 * D], SCALE, None, ALU.mult)
            dve.wait_ge(set_up, 1)
            nc.vector.tensor_tensor(bias_lo[:, :], a["pos"][:, :], bias_hi[:, :].bitcast(F32),
                                    ALU.subtract).then_inc(set_up, 1)
            dve.wait_ge(set_up, 2)
            dve.wait_ge(kt_cleared, 1)
            nc.vector.memset(kt[:].rearrange("p a b c d -> p (a b) c d")[:, :, :, SHIFT].bitcast(F32), 1.0)
            dve.wait_ge(cleared, 2)
            nc.vector.memset(kt[0:W, :, WINDOWED, :, WIN_B].bitcast(F32), 1.0)
            nc.vector.memset(kt[W:P, :, WINDOWED, :, WIN_A].bitcast(F32), 1.0)
            nc.vector.memset(qt[0:W, :, WINDOWED, :, WIN_A].bitcast(F32), FAR)
            nc.vector.memset(qt[W:P, :, WINDOWED, :, WIN_B].bitcast(F32), FAR)
            for par in range(2):
                for kind in (WINDOWED, GLOBAL):
                    for t in range(TPB):
                        c = t if kind == GLOBAL else TPB
                        for slot, part in ((BIAS_HI, bias_hi), (BIAS_LO, bias_lo)):
                            last = nc.vector.tensor_copy(kt[:, par, kind, t * H:(t + 1) * H, slot],
                                                         part[:, c:c + 1].bitcast(F32).to_broadcast([P, H]))
            last.then_inc(consts, 1)

            def normalise(x, mv, rs, dst):
                for t in range(TPB):
                    last = nc.vector.tensor_scalar(dst(t), x(t), mv[:, t, 0:1], rs[:, t:t + 1],
                                                   ALU.subtract, ALU.mult)
                return last

            def heads_out():
                return ps_b.rearrange("p (n s) -> p n s", s=SLOT)

            def maxima(part):
                if not unit(k):
                    return
                dve.wait_ge(max_full, st.at(lambda k: maxes(k, part)))
                if part < 4:
                    n = (part // 2) * H + r * G + 2 * (part % 2)
                    dst, src = qt[:, b % 2, GLOBAL, n:n + 2, SHIFT], ps_m[:, :].rearrange("p (j s) -> p j s", s=S)
                else:
                    n = (part - 4) * H + r * G
                    dst, src = qt[:, b % 2, WINDOWED, n:n + G, SHIFT], ps_m[:, :].rearrange("p (j s) -> p j s", s=P)
                nc.vector.tensor_reduce(dst, src, AX.X, ALU.max, negate=True).then_inc(max_done, 1)

            def projected(st, task):
                c = ("v", "wq", "wk", "q", "k").index(task)
                dve.wait_ge(b_full, st.at(lambda k: b_count(k, task)))
                src = ps_b.rearrange("p (t d) -> p t d", d=D)
                if task == "wq":
                    nc.vector.scalar_tensor_tensor(
                        out=proj[:, 0, :, :], in0=src, scalar=SCALE,
                        in1=bwq[:, :].unsqueeze(1).to_broadcast([P, TPB, D]), op0=ALU.mult,
                        op1=ALU.add).then_inc(b_done, 1)
                    return
                dst = vt[:, (st.k // NG + 1) % 2, :, :] if task == "v" else proj[:, c - 1, :, :]
                nc.vector.tensor_tensor(dst, src, a["b"][:, c * D:(c + 1) * D].unsqueeze(1).to_broadcast([P, TPB, D]),
                                        ALU.add).then_inc(b_done, 1)

            def moments(st, count, mv, ready):
                hold(dve, bn_done, st.at(count), passed)
                for t in range(TPB):
                    last = nc.vector.bn_aggr(mv[:, t, :], bn[:, t, :])
                last.then_inc(ready, 1)

            for st in steps(dve):
                k = st.k
                b, r = k // NG, k % NG
                if r == 0 and batch(b - 2):
                    hold(dve, b_done, st.at(lambda k: b_count(k - 1, "op")), passed)
                    for t in range(TPB):
                        last = nc.vector.bn_stats(bn[:, t, :], y[:, t, :])
                    last.then_inc(bn_done, 1)
                if r == 1 and batch(b - 2):
                    dve.wait_ge(rs_y_ready, st.at(lambda k: k // NG - 1))
                    normalise(lambda t: y[:, t, :], mv_y, rs_y, lambda t: y[:, t, :]).then_inc(x_part, 1)
                    dve.wait_ge(x_part, st.at(lambda k: k // NG - 1))
                    xx = X[:, tiles(st, -2)]
                    nc.vector.tensor_tensor(xx, xx, y[:].rearrange("p t d -> p (t d)"), ALU.add).then_inc(x_new, 1)
                maxima(0)
                if r == 0 and batch(b - 2):
                    moments(st, lambda k: 2 * (k // NG) - 3, mv_y, stats_y)
                if r == 1 and batch(b - 2):
                    hold(dve, x_new, st.at(lambda k: k // NG - 1), passed)
                    xx = X[:, tiles(st, -2)]
                    for t in range(TPB):
                        last = nc.vector.bn_stats(bn[:, t, :], xx[:, t * D:(t + 1) * D])
                    last.then_inc(bn_done, 1)
                if r == 2 and batch(b + 2):
                    wait(dve, stacks_ready, st.at(lambda k: 2 * (k // NG + 2)))
                    projected(st, "wq")
                if r == 1 and batch(b - 2):
                    moments(st, lambda k: 2 * (k // NG) - 2, mv_x, stats_x)
                if r == 3 and batch(b + 2):
                    projected(st, "q")
                if r == 0 and batch(b + 1):
                    wait(dve, v_ready, st.at(lambda k: NG * (k // NG)))
                    projected(st, "v")
                maxima(1)
                if r == 2 and batch(b + 2):
                    projected(st, "wk")
                maxima(2)
                if r == 3 and batch(b + 2):
                    projected(st, "k")
                if r == 3 and batch(b - 2):
                    dve.wait_ge(rs_x_ready, st.at(lambda k: k // NG - 1))
                    xx, zz = X[:, tiles(st, -2)], Z[:, tiles(st, -2)]
                    normalise(lambda t: xx[:, t * D:(t + 1) * D], mv_x, rs_x,
                              lambda t: zz[:, t * D:(t + 1) * D]).then_inc(z_new, 1)
                maxima(3)
                if unit(k - 2):
                    dve.wait_ge(b_full, st.at(lambda k: b_count(k, "Og")))
                    nc.vector.reciprocal(rg[:, :], heads_out()[:, :, HD]).then_inc(recip_g, 1)
                    dve.wait_ge(recip_g, st.at(lambda k: k - 1))
                    nc.vector.tensor_tensor(og[:, :, :], heads_out()[:, :, 0:HD],
                                            rg[:, :].unsqueeze(2).to_broadcast([P, TPB * G, HD]),
                                            ALU.mult).then_inc(b_done, 1)
                maxima(4)
                if unit(k - 2):
                    dve.wait_ge(b_full, st.at(lambda k: b_count(k, "Ow")))
                    nc.vector.reciprocal(rw[:, :], heads_out()[:, :, HD]).then_inc(recip_w, 1)
                    dve.wait_ge(recip_w, st.at(lambda k: k - 1))
                    nc.vector.tensor_tensor(ow[:, :, :], heads_out()[:, :, 0:HD],
                                            rw[:, :].unsqueeze(2).to_broadcast([P, TPB * G, HD]),
                                            ALU.mult).then_inc(b_done, 1)
                maxima(5)
                if unit(k - 2):
                    dve.wait_ge(b_done, st.at(lambda k: b_count(k, "Ow")))
                    g = (k - 2) % NG
                    dst = out[:, ((k - 2) // NG) % 2, :, g * G * HD:(g + 1) * G * HD]
                    nc.vector.tensor_tensor(dst, og[:].rearrange("p (t h) d -> p t (h d)", t=TPB),
                                            ow[:].rearrange("p (t h) d -> p t (h d)", t=TPB),
                                            ALU.add).then_inc(out_ready, 1)
                if r == 3 and batch(b - 1):
                    dve.wait_ge(b_full, st.at(lambda k: b_count(k, "op")))
                    nc.vector.tensor_tensor(y[:, :, :], ps_b.rearrange("p (t d) -> p t d", d=D),
                                            a["bo"][:, :].unsqueeze(1).to_broadcast([P, TPB, D]),
                                            ALU.add).then_inc(b_done, 1)
            dve.wait_ge(z_new, B)

        @block.gpsimd
        def _(pool):
            nc.gpsimd.memset(half[:, :], -0.5).then_inc(pool_step, 1)

            def clear():
                nc.gpsimd.memset(qt[:].rearrange("p a b c d -> p (a b c d)").bitcast(F32), 0.0).then_inc(cleared, 1)
                pool.wait_ge(cleared, 1)
                nc.gpsimd.memset(qt[:].rearrange("p a b c d -> p (a b) c d")[:, :, :, BIAS_HI:BIAS_LO + 1].bitcast(F32),
                                 1.0).then_inc(cleared, 1)
                nc.gpsimd.memset(v32[:].rearrange("p a b c d -> p (a b c d)"), 0.0).then_inc(cleared, 1)
                nc.gpsimd.memset(kpad[:].rearrange("p a b c d -> p (a b c d)").bitcast(F32), 0.0).then_inc(kpad_zero, 1)
                pool.wait_ge(cleared, 3)
                nc.gpsimd.memset(v32[:, :, :, :, HD].rearrange("p a b c -> p (a b c)"), 1.0).then_inc(cleared, 1)
                pool.wait_ge(cleared, 4)

            def rstd(st, stats, mv, rs, ready, n):
                hold(pool, stats, st.at(lambda k: k // NG - 1), passed)
                nc.gpsimd.tensor_scalar(ve[:, :], mv[:, :, 1], EPS, None, ALU.add).then_inc(pool_step, 1)
                hold(pool, pool_step, st.at(lambda k: 1 + 2 * (k // NG - 2) + n), passed)
                nc.gpsimd.tensor_tensor(rs[:, :], ve[:, :], half[:, :], ALU.pow).then_inc(ready, 1)

            def split(st, kind, projected_by, transposed):
                n, par = TPB * H, (st.k // NG + 1) % 2
                val = proj[:].rearrange("p a t (h d) -> p a (t h) d", d=HD)
                hold(pool, b_done, st.at(projected_by), passed)
                if unit(st.k - 1):
                    hold(pool, a_full, st.at(transposed), passed)
                qd, kd = qt[:, par, kind, :, :], kt[:, par, kind, :, :]
                nc.gpsimd.memset(qd[:, :, SHIFT].bitcast(F32), 0.0)
                nc.gpsimd.tensor_copy(qd[:, :, 0:2 * HD].rearrange("p n (c d) -> p n c d", c=2),
                                      val[:, 2 * kind, :, :].unsqueeze(2).to_broadcast([P, n, 2, HD]))
                nc.gpsimd.tensor_copy(
                    kd[:, :, 0:4 * HD].rearrange("p n (c d) -> p n c d", c=2)[:, :, :, 0:HD],
                    val[:, 2 * kind + 1, :, :].unsqueeze(2).to_broadcast([P, n, 2, HD])).then_inc(parts_hi, 1)
                hold(pool, parts_hi, st.at(lambda k: 2 * (k // NG + 1) + kind + 1), passed)
                nc.gpsimd.tensor_tensor(qd[:, :, 2 * HD:3 * HD], val[:, 2 * kind, :, :],
                                        qd[:, :, 0:HD].bitcast(F32), ALU.subtract)
                nc.gpsimd.tensor_tensor(kd[:, :, HD:2 * HD], val[:, 2 * kind + 1, :, :],
                                        kd[:, :, 0:HD].bitcast(F32), ALU.subtract).then_inc(stacks_ready, 1)

            for st in steps(pool):
                k = st.k
                b, r = k // NG, k % NG
                if r == 0 and batch(b + 2):
                    if batch(b + 1):
                        hold(pool, a_full, st.at(lambda k: a_count(k - 3, "xT")), passed)
                    nc.gpsimd.tensor_copy(zc[:, :], Z[:, tiles(st, 2)]).then_inc(zc_ready, 1)
                if k == FIRST:
                    clear()
                if r == 0 and batch(b - 2):
                    rstd(st, stats_y, mv_y, rs_y, rs_y_ready, 1)
                if r == 0 and batch(b + 1):
                    split(st, WINDOWED, lambda k: b_count(k - 2, "wk"), lambda k: a_count(k, "Mw"))
                if r == 1 and batch(b + 1):
                    split(st, GLOBAL, lambda k: b_count(k - 2, "k"), lambda k: a_count(k - 1, "Mg"))
                if r == 2 and batch(b - 2):
                    rstd(st, stats_x, mv_x, rs_x, rs_x_ready, 2)
                if unit(k + 2):
                    u = k + 2
                    hold(pool, b_done, st.at(lambda k: b_count(NG * ((k + 2) // NG - 1), "v")), passed)
                    hold(pool, w_full, st.at(lambda k: clip(k + 2 - KEEP + 1, UNITS)), passed)
                    hs = slice((u % NG) * G * HD, (u % NG + 1) * G * HD)
                    nc.gpsimd.tensor_copy(v32[:, u % KEEP, :, :, 0:HD],
                                          vt[:, (u // NG) % 2, :, hs].rearrange("p t (h d) -> p t h d", d=HD)
                                          ).then_inc(v_ready, 1)


TOK = 512
TT = TOK // P
NT = B * S // TOK


def token_steps(eng, last, first=1):
    for k in range(first):
        yield Step(k)
    with eng.Fori(first, NT - 1) as i:
        yield Step(first, i, first, 1)
    for k in range(NT - 1, last + 1):
        yield Step(k)


def block_of(st, lead=0):
    return bass.ds(st.at(lambda k: (k + lead) * TT * D), TT * D)


class Chain:

    def __init__(self, eng, sem, per_step):
        self.eng, self.sem, self.per_step, self.n = eng, sem, per_step, 0

    def begin(self, st):
        assert self.n in (0, self.per_step)
        self.st, self.n = st, 0

    def __call__(self, instruction, passed=None):
        self.n += 1
        n = self.n
        instruction.then_inc(self.sem, 1)
        value = self.st.at(lambda k: k * self.per_step + n)
        if passed:
            hold(self.eng, self.sem, value, passed)
        else:
            self.eng.wait_ge(self.sem, value)


def best(nc, link, val, rev, top, first, key, sel):
    shape = list(val.shape)
    link(nc.vector.tensor_reduce(top, val, AX.X, ALU.max))
    link(nc.vector.tensor_tensor(key, val, top.unsqueeze(2).to_broadcast(shape), ALU.is_equal))
    link(nc.vector.tensor_tensor(key, key, rev.unsqueeze(1).to_broadcast(shape), ALU.mult))
    link(nc.vector.tensor_reduce(first, key, AX.X, ALU.max))
    link(nc.vector.tensor_tensor(sel, key, first.unsqueeze(2).to_broadcast(shape), ALU.is_equal))


BEST_LINKS = 5


def statistics(nc, link, x, bn, mv, passed):
    for t in range(TT):
        last = nc.vector.bn_stats(bn[:, t, :], x[:, t * D:(t + 1) * D])
    link(last, passed)
    for t in range(TT):
        last = nc.vector.bn_aggr(mv[:, t, :], bn[:, t, :])
    return last


def normalise_tiles(nc, x, mv, rs, out):
    for t in range(TT):
        last = nc.vector.tensor_scalar(out[:, t * D:(t + 1) * D], x[:, t * D:(t + 1) * D], mv[:, t, 0:1],
                                       rs[:, t:t + 1], ALU.subtract, ALU.mult)
    return last


def first_ffn(nc, X, Z, ident, a):
    E = 8
    NE = E + 1
    LAG = 2
    HC = 4
    HID = HC * P
    LINKS = 2 * BEST_LINKS + 1 + 7

    def live(n):
        return 0 <= n < NT

    with ExitStack() as ctx:
        def sb(name, shape, dt=F32):
            return ctx.enter_context(nc.sbuf_tensor("f0_" + name, shape, dt))

        def pb(name, shape):
            return ctx.enter_context(nc.psum_tensor("f0_" + name, shape, F32))

        def sem(name):
            return ctx.enter_context(nc.semaphore("f0_" + name))

        w1l, w2l = sb("w1l", [P, NE * HID], F32R), sb("w2l", [P, NE * HID], F32R)
        pick = sb("pick", [P, E, P], F32R)
        w1h, w2h = sb("w1h", [P, NE * HID], F32R), sb("w2h", [P, NE * HID], F32R)
        gwh, gwl = sb("gwh", [P, E], F32R), sb("gwl", [P, E], F32R)
        zc = sb("zc", [P, TOK])
        xh, xl = sb("xh", [P, TOK], F32R), sb("xl", [P, TOK], F32R)
        s = sb("s", [P, 2, HC, TOK])
        sh, sl = sb("sh", [P, 3, HC, TOK], F32R), sb("sl", [P, 3, HC, TOK], F32R)
        tmp, acc, y = sb("tmp", [P, 2, TOK]), sb("acc", [P, TOK]), sb("y", [P, TOK])
        lg, key, sel1, sel2, far = [sb(n, [P, TT, E]) for n in ("lg", "key", "sel1", "sel2", "far")]
        cw = sb("cw", [P, TT, P], F32R)
        gt = sb("gt", [P, TOK], F32R)
        gates = sb("gates", [P, 2, TOK])
        m1, m2, first, diff, e2, den, g1, g2 = [
            sb(n, [P, TT]) for n in ("m1", "m2", "first", "diff", "e2", "den", "g1", "g2")]
        bn, mv, rs, ve = sb("bn", [P, TT, 6]), sb("mv", [P, TT, 2]), sb("rs", [P, TT]), sb("ve", [P, TT])
        half, euler = sb("half", [P, TT]), sb("euler", [P, TT])
        ps_u = pb("ps_u", [P, 2, 1024])
        ps_y = pb("ps_y", [P, 2, TOK])
        ps_g, ps_x = pb("ps_g", [P, TOK]), pb("ps_x", [P, TOK])

        w1h_ready, w1l_ready, w2h_ready, w2l_ready = (
            sem("w1h_ready"), sem("w1l_ready"), sem("w2h_ready"), sem("w2l_ready"))
        gw_ready, gw_hi, pick_ready = sem("gw_ready"), sem("gw_hi"), sem("pick_ready")
        zc_ready, x_full, xh_ready, x_done = sem("zc_ready"), sem("x_full"), sem("xh_ready"), sem("x_done")
        up_full, silu_done, sh_done, sl_done = sem("up_full"), sem("silu_done"), sem("sh_done"), sem("sl_done")
        gates_copied = sem("gates_copied")
        gates_full, y_full, y_done, summed = sem("gates_full"), sem("y_full"), sem("y_done"), sem("summed")
        link_sem, diff_ready, e2_ready, cw_ready = sem("link"), sem("diff_ready"), sem("e2_ready"), sem("cw_ready")
        bn_done, stats_ready, rs_ready, ve_ready = sem("bn_done"), sem("stats_ready"), sem("rs_ready"), sem("ve_ready")
        y_normed, x_new, z_new, consts = sem("y_normed"), sem("x_new"), sem("z_new"), sem("consts")
        passed = sem("passed")
        block = ctx.enter_context(nc.Block())

        def x_count(k, task):
            n = min(k + 1, NT) + 2 * clip(k, NT) + clip(k - 1, NT)
            for name, on in (("start", 0), ("logits", live(k)), ("sum", live(k - 1)), ("cw", live(k)),
                             ("xT", live(k + 1))):
                n += on
                if name == task:
                    return n

        def last_use(k, e):
            return NE * k + max(e - 1, 0)

        def lagged(e):
            return (e - LAG, 0) if e >= LAG else (e - LAG + NE, 1)

        @block.tensor
        def _(pe):
            def take_x(st, task):
                pe.wait_ge(x_done, st.at(lambda k: x_count(k, task) - 1))

            def transposes(parts):
                for t in range(TT):
                    last = nc.tensor.transpose(ps_x[:, t * P:(t + 1) * P], parts(t), ident[:, :])
                last.then_inc(x_full, 1)

            def up(st, e):
                if st.k == 0:
                    pe.wait_ge(w1h_ready, e + 1)
                    pe.wait_ge(w1l_ready, e + 1)
                for c2 in range(2):
                    wait(pe, silu_done, st.at(lambda k: 2 * NE * k + 2 * e + c2 + 1 - 2))
                    for c in (2 * c2, 2 * c2 + 1):
                        dst = ps_u[:, c2, (c % 2) * TOK:(c % 2 + 1) * TOK]
                        w = slice(e * HID + c * P, e * HID + (c + 1) * P)
                        nc.tensor.matmul(dst, w1h[:, w], xh[:, :], start=True, stop=False)
                        nc.tensor.matmul(dst, w1h[:, w], xl[:, :], start=False, stop=False)
                        last = nc.tensor.matmul(dst, w1l[:, w], xh[:, :], start=False, stop=True)
                    last.then_inc(up_full, 1)
                    if e == 3 and c2 == 0:
                        take_x(st, "cw")
                        pe.wait_ge(cw_ready, st.at(lambda k: k + 1))
                        transposes(lambda t: cw[:, t, :].bitcast(F32))

            def down(st, e, ago):
                if st.k == 0:
                    pe.wait_ge(w2h_ready, e + 1)
                    pe.wait_ge(w2l_ready, e + 1)
                wait(pe, y_done, st.at(lambda k: last_use(k - ago, e)))
                if e > 0:
                    wait(pe, gates_copied, st.at(lambda k: E * (k - ago) + e - 1))
                    nc.tensor.matmul(ps_g[:, :], pick[:, e - 1, :], gt[:, :], start=True,
                                     stop=True).then_inc(gates_full, 1)
                pe.wait_ge(sh_done, st.at(lambda k: 2 * (NE * (k - ago) + e) + 2))
                pe.wait_ge(sl_done, st.at(lambda k: 2 * (NE * (k - ago) + e) + 2))
                for c in range(HC):
                    w = slice(e * HID + c * P, e * HID + (c + 1) * P)
                    dst = ps_y[:, e % 2, :]
                    nc.tensor.matmul(dst, w2h[:, w], sh[:, e % 3, c, :], start=c == 0, stop=False)
                    nc.tensor.matmul(dst, w2h[:, w], sl[:, e % 3, c, :], start=False, stop=False)
                    last = nc.tensor.matmul(dst, w2l[:, w], sh[:, e % 3, c, :], start=False, stop=c == HC - 1)
                last.then_inc(y_full, 1)

            pe.wait_ge(zc_ready, 1)
            transposes(lambda t: zc[:, t * P:(t + 1) * P])
            pe.wait_ge(gw_ready, 1)
            for st in token_steps(pe, NT):
                k = st.k
                if live(k):
                    take_x(st, "logits")
                    for t in range(TT):
                        tok, dst = slice(t * P, (t + 1) * P), ps_x[:, t * E:(t + 1) * E]
                        nc.tensor.matmul(dst, xh[:, tok], gwh[:, :], start=True, stop=False)
                        nc.tensor.matmul(dst, xh[:, tok], gwl[:, :], start=False, stop=False)
                        last = nc.tensor.matmul(dst, xl[:, tok], gwh[:, :], start=False, stop=True)
                    last.then_inc(x_full, 1)
                for e in range(NE):
                    if live(k):
                        up(st, e)
                    if e == 3 and live(k):
                        pe.wait_ge(x_done, st.at(lambda k: x_count(k, "cw")))
                    if e == NE - 1 and live(k + 1):
                        pe.wait_ge(zc_ready, st.at(lambda k: k + 2))
                        take_x(st, "xT")
                        transposes(lambda t: zc[:, t * P:(t + 1) * P])
                    expert, ago = lagged(e)
                    if live(k - ago):
                        down(st, expert, ago)
                    if e == 2 and live(k - 1):
                        take_x(st, "sum")
                        pe.wait_ge(summed, st.at(lambda k: E * k))
                        transposes(lambda t: acc[:, t * P:(t + 1) * P])

        @block.scalar
        def _(act):
            def split(e, w, hi, ready):
                cols = slice(e * HID, (e + 1) * HID)
                nc.scalar.copy(hi[:, cols], a[w][:, cols]).then_inc(ready, 1)

            for e in range(NE):
                split(e, "w1", w1h, w1h_ready)
            for st in token_steps(act, NT):
                k = st.k
                for e in range(NE):
                    if k == 0:
                        split(e, "w2", w2h, w2h_ready)
                    if live(k):
                        for c2 in range(2):
                            act.wait_ge(up_full, st.at(lambda k: 2 * NE * k + 2 * e + c2 + 1))
                            if c2 == 0:
                                wait(act, sl_done, st.at(lambda k: 2 * last_use(k, e)))
                            nc.scalar.activation(s[:, e % 2, 2 * c2:2 * c2 + 2, :].rearrange("p a b -> p (a b)"),
                                                 ps_u[:, c2, :], ACT.Silu).then_inc(silu_done, 1)
                            if e == 3 and c2 == 0:
                                act.wait_ge(x_full, st.at(lambda k: x_count(k, "cw")))
                                nc.scalar.copy(gt[:, :], ps_x[:, :]).then_inc(x_done, 1)
                    if e == NE - 1 and live(k + 1):
                        act.wait_ge(x_full, st.at(lambda k: x_count(k, "xT")))
                        nc.scalar.copy(xh[:, :], ps_x[:, :]).then_inc(xh_ready, 1)
                    expert, ago = lagged(e)
                    if live(k - ago) and expert > 0:
                        act.wait_ge(gates_full, st.at(lambda k: E * (k - ago) + expert))
                        wait(act, y_done, st.at(lambda k: NE * (k - ago) + expert - 1))
                        nc.scalar.copy(gates[:, expert % 2, :], ps_g[:, :]).then_inc(gates_copied, 1)
                    if live(k):
                        for c2 in range(2):
                            act.wait_ge(silu_done, st.at(lambda k: 2 * NE * k + 2 * e + c2 + 1))
                            if c2 == 0:
                                wait(act, y_full, st.at(lambda k: NE * k + e + 1 - 3))
                            nc.scalar.copy(sh[:, e % 3, 2 * c2:2 * c2 + 2, :].rearrange("p a b -> p (a b)"),
                                           s[:, e % 2, 2 * c2:2 * c2 + 2, :].rearrange("p a b -> p (a b)")
                                           ).then_inc(sh_done, 1)
                    if e == 2 and live(k - 1):
                        act.wait_ge(x_full, st.at(lambda k: x_count(k, "sum")))
                        nc.scalar.copy(y[:, :], ps_x[:, :]).then_inc(x_done, 1)

        @block.vector
        def _(dve):
            link = Chain(dve, link_sem, LINKS)
            shape = [P, TT, E]

            def split_x(st, lead):
                if lead == 0:
                    dve.wait_ge(x_full, 1)
                    nc.vector.tensor_copy(xh[:, :], ps_x[:, :]).then_inc(xh_ready, 1)
                dve.wait_ge(xh_ready, st.at(lambda k: k + lead + 1))
                nc.vector.tensor_tensor(xl[:, :], ps_x[:, :], xh[:, :].bitcast(F32), ALU.subtract).then_inc(x_done, 1)

            def split(e, w, hi, lo, hi_ready, ready):
                dve.wait_ge(hi_ready, e + 1)
                cols = slice(e * HID, (e + 1) * HID)
                nc.vector.tensor_tensor(lo[:, cols], a[w][:, cols], hi[:, cols].bitcast(F32),
                                        ALU.subtract).then_inc(ready, 1)

            nc.vector.tensor_copy(gwh[:, :], a["gate"][:, :]).then_inc(gw_hi, 1)
            nc.vector.tensor_copy(pick[:].rearrange("p a b -> p (a b)"), a["pick"][:, :]).then_inc(pick_ready, 1)
            dve.wait_ge(gw_hi, 1)
            nc.vector.tensor_tensor(gwl[:, :], a["gate"][:, :], gwh[:, :].bitcast(F32),
                                    ALU.subtract).then_inc(gw_ready, 1)
            split_x(Step(0), 0)
            for e in range(NE):
                split(e, "w1", w1h, w1l, w1h_ready, w1l_ready)
            dve.wait_ge(consts, 1)
            dve.wait_ge(pick_ready, 1)
            for st in token_steps(dve, NT):
                k = st.k
                rev = a["rev"][:, 0:E]

                def add(st, e, ago):
                    dve.wait_ge(y_full, st.at(lambda k: NE * (k - ago) + e + 1))
                    if e == 0:
                        if live(k - 1):
                            dve.wait_ge(x_full, st.at(lambda k: x_count(k, "sum")))
                        nc.vector.tensor_copy(acc[:, :], ps_y[:, 0, :]).then_inc(y_done, 1)
                        return
                    dve.wait_ge(gates_copied, st.at(lambda k: E * (k - ago) + e))
                    nc.vector.tensor_tensor(tmp[:, e % 2, :], ps_y[:, e % 2, :], gates[:, e % 2, :],
                                            ALU.mult).then_inc(y_done, 1)
                    dve.wait_ge(y_done, st.at(lambda k: NE * (k - ago) + e + 1))
                    if e > 1:
                        dve.wait_ge(summed, st.at(lambda k: E * (k - ago) + e - 1))
                    nc.vector.tensor_tensor(acc[:, :], acc[:, :], tmp[:, e % 2, :], ALU.add).then_inc(summed, 1)

                if live(k):
                    link.begin(st)
                    dve.wait_ge(x_full, st.at(lambda k: x_count(k, "logits")))
                    nc.vector.tensor_copy(lg[:].rearrange("p t e -> p (t e)"), ps_x[:, 0:TT * E]).then_inc(x_done, 1)
                    dve.wait_ge(x_done, st.at(lambda k: x_count(k, "logits")))
                for e in range(NE):
                    if e == 0 and live(k):
                        best(nc, link, lg[:, :, :], rev, m1[:, :], first[:, :], key[:, :, :], sel1[:, :, :])
                    if e == 1 and live(k):
                        link(nc.vector.scalar_tensor_tensor(out=far[:, :, :], in0=sel1[:, :, :], scalar=FAR,
                                                            in1=lg[:, :, :], op0=ALU.mult, op1=ALU.add))
                        best(nc, link, far[:, :, :], rev, m2[:, :], first[:, :], key[:, :, :], sel2[:, :, :])
                        nc.vector.tensor_tensor(diff[:, :], m2[:, :], m1[:, :], ALU.subtract).then_inc(diff_ready, 1)
                    if e == 2 and live(k):
                        dve.wait_ge(e2_ready, st.at(lambda k: k + 1))
                        link(nc.vector.tensor_scalar(den[:, :], e2[:, :], 1.0, None, ALU.add))
                        link(nc.vector.reciprocal(g1[:, :], den[:, :]))
                        link(nc.vector.tensor_tensor(g2[:, :], e2[:, :], g1[:, :], ALU.mult))
                        link(nc.vector.tensor_tensor(sel1[:, :, :], sel1[:, :, :],
                                                     g1[:, :].unsqueeze(2).to_broadcast(shape), ALU.mult))
                        link(nc.vector.tensor_tensor(sel2[:, :, :], sel2[:, :, :],
                                                     g2[:, :].unsqueeze(2).to_broadcast(shape), ALU.mult))
                        link(nc.vector.tensor_tensor(sel1[:, :, :], sel1[:, :, :], sel2[:, :, :], ALU.add))
                        link(nc.vector.tensor_copy(cw[:, :, 0:E], sel1[:, :, :]))
                        nc.vector.tensor_tensor(cw[:, :, E:2 * E], sel1[:, :, :], cw[:, :, 0:E].bitcast(F32),
                                                ALU.subtract).then_inc(cw_ready, 1)
                    if e == NE - 1 and live(k + 1):
                        split_x(st, 1)
                    if live(k):
                        for c2 in range(2):
                            dve.wait_ge(sh_done, st.at(lambda k: 2 * NE * k + 2 * e + c2 + 1))
                            if c2 == 0:
                                wait(dve, y_full, st.at(lambda k: NE * k + e + 1 - 3))
                            part = slice(2 * c2, 2 * c2 + 2)
                            nc.vector.tensor_tensor(sl[:, e % 3, part, :], s[:, e % 2, part, :],
                                                    sh[:, e % 3, part, :].bitcast(F32),
                                                    ALU.subtract).then_inc(sl_done, 1)
                    if k == 0:
                        split(e, "w2", w2h, w2l, w2h_ready, w2l_ready)
                    expert, ago = lagged(e)
                    if live(k - ago):
                        add(st, expert, ago)
                    if not live(k - 1):
                        continue
                    if e == 4:
                        hold(dve, x_done, st.at(lambda k: x_count(k, "sum")), passed)
                        for t in range(TT):
                            last = nc.vector.bn_stats(bn[:, t, :], y[:, t * D:(t + 1) * D])
                        last.then_inc(bn_done, 1)
                        hold(dve, bn_done, st.at(lambda k: 2 * k - 1), passed)
                        for t in range(TT):
                            last = nc.vector.bn_aggr(mv[:, t, :], bn[:, t, :])
                        last.then_inc(stats_ready, 1)
                    if e == 5:
                        dve.wait_ge(rs_ready, st.at(lambda k: 2 * k - 1))
                        normalise_tiles(nc, y, mv, rs, y).then_inc(y_normed, 1)
                    if e == 6:
                        hold(dve, x_new, st.at(lambda k: k), passed)
                        for t in range(TT):
                            last = nc.vector.bn_stats(bn[:, t, :], X[:, block_of(st, -1)][:, t * D:(t + 1) * D])
                        last.then_inc(bn_done, 1)
                        hold(dve, bn_done, st.at(lambda k: 2 * k), passed)
                        for t in range(TT):
                            last = nc.vector.bn_aggr(mv[:, t, :], bn[:, t, :])
                        last.then_inc(stats_ready, 1)
                    if e == 8:
                        dve.wait_ge(rs_ready, st.at(lambda k: 2 * k))
                        normalise_tiles(nc, X[:, block_of(st, -1)], mv, rs, Z[:, block_of(st, -1)]).then_inc(z_new, 1)
            dve.wait_ge(z_new, NT)

        @block.gpsimd
        def _(pool):
            nc.gpsimd.tensor_copy(zc[:, :], Z[:, 0:TOK]).then_inc(zc_ready, 1)
            nc.gpsimd.memset(half[:, :], -0.5)
            nc.gpsimd.memset(cw[:].rearrange("p t e -> p (t e)").bitcast(F32), 0.0)
            nc.gpsimd.memset(euler[:, :], float(np.exp(1.0))).then_inc(consts, 1)
            pool.wait_ge(consts, 1)
            for st in token_steps(pool, NT):
                if live(st.k):
                    hold(pool, diff_ready, st.at(lambda k: k + 1), passed)
                    nc.gpsimd.tensor_tensor(e2[:, :], euler[:, :], diff[:, :], ALU.pow).then_inc(e2_ready, 1)
                if live(st.k + 1):
                    hold(pool, x_full, st.at(lambda k: x_count(k, "start")), passed)
                    nc.gpsimd.tensor_copy(zc[:, :], Z[:, block_of(st, 1)]).then_inc(zc_ready, 1)
                if not live(st.k - 1):
                    continue
                for n in range(2):
                    hold(pool, stats_ready, st.at(lambda k: 2 * k - 1 + n), passed)
                    nc.gpsimd.tensor_scalar(ve[:, :], mv[:, :, 1], EPS, None, ALU.add).then_inc(ve_ready, 1)
                    hold(pool, ve_ready, st.at(lambda k: 2 * k - 1 + n), passed)
                    nc.gpsimd.tensor_tensor(rs[:, :], ve[:, :], half[:, :], ALU.pow).then_inc(rs_ready, 1)
                    if n == 0:
                        hold(pool, y_normed, st.at(lambda k: k), passed)
                        xx = X[:, block_of(st, -1)]
                        nc.gpsimd.tensor_tensor(xx, xx, y[:, :], ALU.add).then_inc(x_new, 1)


def second_ffn(nc, X, Z, ident, a, out):
    E = 16
    NQ = E // 2 + 1
    LAST = NT + 1
    LINKS = 2 * BEST_LINKS + 8

    def live(n):
        return 0 <= n < NT

    with ExitStack() as ctx:
        def sb(name, shape, dt=F32):
            return ctx.enter_context(nc.sbuf_tensor("f1_" + name, shape, dt))

        def pb(name, shape):
            return ctx.enter_context(nc.psum_tensor("f1_" + name, shape, F32))

        def sem(name):
            return ctx.enter_context(nc.semaphore("f1_" + name))

        wh, wl = sb("wh", [P, NQ, 2, P], F32R), sb("wl", [P, NQ, 2, P], F32R)
        rwh, rwl = sb("rwh", [P, E], F32R), sb("rwl", [P, E], F32R)
        pick = sb("pick", [P, NQ - 1, P], F32R)
        zc = sb("zc", [P, TOK])
        xh, xl = sb("xh", [P, TOK], F32R), sb("xl", [P, TOK], F32R)
        s = sb("s", [P, 3, TOK])
        h = sb("h", [P, NQ, TOK])
        p = sb("p", [P, 2, TOK])
        lg, ex, key, sel1, sel2, far = [sb(n, [P, TT, E]) for n in ("lg", "ex", "key", "sel1", "sel2", "far")]
        cw = sb("cw", [P, TT, P], F32R)
        gt = sb("gt", [P, TOK], F32R)
        m1, m2, first, total, inv = [sb(n, [P, TT]) for n in ("m1", "m2", "first", "total", "inv")]
        bn, mv, rs, ve = sb("bn", [P, TT, 6]), sb("mv", [P, TT, 2]), sb("rs", [P, TT]), sb("ve", [P, TT])
        half = sb("half", [P, TT])
        acc = sb("acc", [P, TOK])
        ps_g, ps_u = pb("ps_g", [P, 2, TOK]), pb("ps_u", [P, 3, TOK])
        ps_t, ps_x, ps_y = pb("ps_t", [P, TOK]), pb("ps_x", [P, TOK]), pb("ps_y", [P, TOK])

        wh_ready, wl_ready, rw_hi, rw_ready = sem("wh_ready"), sem("wl_ready"), sem("rw_hi"), sem("rw_ready")
        zc_ready, xh_ready, t_full, t_done = sem("zc_ready"), sem("xh_ready"), sem("t_full"), sem("t_done")
        gates_full, p_ready = sem("gates_full"), sem("p_ready")
        gate_full, up_full, silu_done, h_done = sem("gate_full"), sem("up_full"), sem("silu_done"), sem("h_done")
        down_done, y_copied, cw_ready = sem("down_done"), sem("y_copied"), sem("cw_ready")
        shifted, ex_ready, link_sem = sem("shifted"), sem("ex_ready"), sem("link")
        bn_done, stats_ready, rs_ready, ve_ready = sem("bn_done"), sem("stats_ready"), sem("rs_ready"), sem("ve_ready")
        y_normed, x_new, stored, consts = sem("y_normed"), sem("x_new"), sem("stored"), sem("consts")
        passed = sem("passed")
        block = ctx.enter_context(nc.Block())

        def t_count(k, task):
            n = clip(k, NT) * 2 + min(k + 1, NT)
            n += {"start": 0, "logits": 1, "cw": 2, "xT": 2}[task] * live(k)
            return n + (task == "xT" and live(k + 1))

        def gate_count(k, q):
            return (NQ - 1) * clip(k - 1, NT) + q

        @block.sync
        def _(sp):
            for st in token_steps(sp, LAST, 2):
                if live(st.k - 2):
                    hold(sp, x_new, st.at(lambda k: k - 1), passed)
                    sp.dma_start(out[bass.ds(st.at(lambda k: (k - 2) * TOK), TOK), :].rearrange(
                        "(t p) d -> p t d", p=P), X[:, block_of(st, -2)].rearrange("p (t d) -> p t d", d=D)
                        ).then_inc(stored, 16)
            sp.wait_ge(stored, 16 * NT)

        @block.tensor
        def _(pe):
            def transpose_x():
                for t in range(TT):
                    last = nc.tensor.transpose(ps_t[:, t * P:(t + 1) * P], zc[:, t * P:(t + 1) * P], ident[:, :])
                last.then_inc(t_full, 1)

            def gates(st, q):
                wait(pe, p_ready, st.at(lambda k: gate_count(k, q) - 1))
                nc.tensor.matmul(ps_x[:, :], pick[:, q - 1, :], gt[:, :], start=True,
                                 stop=True).then_inc(gates_full, 1)

            def down(st, q, block):
                if q == 0:
                    wait(pe, y_copied, st.at(lambda k: k - block))
                else:
                    pe.wait_ge(p_ready, st.at(lambda k: gate_count(k + 1 - block, q)))
                for t in range(TT):
                    src = h[:, 0, t * P:(t + 1) * P] if q == 0 else p[:, q % 2, t * P:(t + 1) * P]
                    last = nc.tensor.matmul(ps_y[:, t * D:(t + 1) * D], src, a["wd"][:, q * D:(q + 1) * D],
                                            start=q == 0 and t == 0, stop=q == NQ - 1 and t == TT - 1,
                                            skip_group_check=True)
                last.then_inc(down_done, 1)

            def up(st, q):
                if st.k == 0:
                    pe.wait_ge(wh_ready, q + 1)
                    pe.wait_ge(wl_ready, q + 1)
                for ps, banks, half_, free, full in ((ps_g, 2, 0, silu_done, gate_full), (ps_u, 3, 1, h_done, up_full)):
                    wait(pe, free, st.at(lambda k: NQ * k + q + 1 - banks + (banks == 2 and q == 0)))
                    dst = ps[:, q % banks, :]
                    nc.tensor.matmul(dst, wh[:, q, half_, :], xh[:, :], start=True, stop=False)
                    nc.tensor.matmul(dst, wh[:, q, half_, :], xl[:, :], start=False, stop=False)
                    nc.tensor.matmul(dst, wl[:, q, half_, :], xh[:, :], start=False,
                                     stop=True).then_inc(full, 1)

            pe.wait_ge(zc_ready, 1)
            transpose_x()
            pe.wait_ge(rw_ready, 1)
            pe.wait_ge(consts, 2)
            for st in token_steps(pe, LAST, 2):
                k = st.k
                if live(k - 2):
                    down(st, NQ - 1, 2)
                if live(k):
                    pe.wait_ge(t_done, st.at(lambda k: t_count(k, "start")))
                    for t in range(TT):
                        tok, dst = slice(t * P, (t + 1) * P), ps_t[:, t * E:(t + 1) * E]
                        nc.tensor.matmul(dst, xh[:, tok], rwh[:, :], start=True, stop=False)
                        nc.tensor.matmul(dst, xh[:, tok], rwl[:, :], start=False, stop=False)
                        last = nc.tensor.matmul(dst, xl[:, tok], rwh[:, :], start=False, stop=True)
                    last.then_inc(t_full, 1)
                    up(st, 0)
                for q in range(1, NQ - 1):
                    if live(k):
                        up(st, q)
                    if live(k - 1):
                        if q == 1:
                            pe.wait_ge(t_done, st.at(lambda k: t_count(k - 1, "cw")))
                        gates(st, q)
                        down(st, q - 1, 1)
                if live(k - 1):
                    gates(st, NQ - 1)
                if live(k):
                    pe.wait_ge(cw_ready, st.at(lambda k: k + 1))
                    pe.wait_ge(t_done, st.at(lambda k: t_count(k, "logits")))
                    for t in range(TT):
                        last = nc.tensor.transpose(ps_t[:, t * P:(t + 1) * P], cw[:, t, :].bitcast(F32), ident[:, :])
                    last.then_inc(t_full, 1)
                    up(st, NQ - 1)
                if live(k + 1):
                    pe.wait_ge(zc_ready, st.at(lambda k: k + 2))
                    pe.wait_ge(t_done, st.at(lambda k: t_count(k, "cw")))
                    transpose_x()
                if live(k - 1):
                    down(st, NQ - 2, 1)

        @block.scalar
        def _(act):
            for q in range(NQ):
                nc.scalar.copy(wh[:, q, :, :].rearrange("p a b -> p (a b)"),
                               a["wgu"][:, q * 2 * P:(q + 1) * 2 * P]).then_inc(wh_ready, 1)
            for st in token_steps(act, LAST, 3):
                k = st.k
                for q in range(NQ):
                    if q == NQ - 1 and live(k):
                        act.wait_ge(t_full, st.at(lambda k: t_count(k, "cw")))
                        if live(k - 1):
                            act.wait_ge(gates_full, st.at(lambda k: gate_count(k, NQ - 1)))
                        nc.scalar.copy(gt[:, :], ps_t[:, :]).then_inc(t_done, 1)
                    if live(k):
                        act.wait_ge(gate_full, st.at(lambda k: NQ * k + q + 1))
                        wait(act, h_done, st.at(lambda k: NQ * k + q + 1 - 3))
                        nc.scalar.activation(s[:, q % 3, :], ps_g[:, q % 2, :], ACT.Silu).then_inc(silu_done, 1)
                    if q == 0 and live(k - 2):
                        act.wait_ge(down_done, st.at(lambda k: NQ * (k - 1)))
                        wait(act, x_new, st.at(lambda k: k - 2))
                        nc.scalar.copy(acc[:, :], ps_y[:, :]).then_inc(y_copied, 1)
                    if q == 2 and live(k):
                        act.wait_ge(shifted, st.at(lambda k: k + 1))
                        nc.scalar.activation(ex[:].rearrange("p t e -> p (t e)"), lg[:].rearrange("p t e -> p (t e)"),
                                             ACT.Exp).then_inc(ex_ready, 1)
                if live(k + 1):
                    act.wait_ge(t_full, st.at(lambda k: t_count(k, "xT")))
                    nc.scalar.copy(xh[:, :], ps_t[:, :]).then_inc(xh_ready, 1)

        @block.vector
        def _(dve):
            link = Chain(dve, link_sem, LINKS)

            def split_x(st, lead):
                if lead == 0:
                    dve.wait_ge(t_full, 1)
                    nc.vector.tensor_copy(xh[:, :], ps_t[:, :]).then_inc(xh_ready, 1)
                dve.wait_ge(xh_ready, st.at(lambda k: k + lead + 1))
                nc.vector.tensor_tensor(xl[:, :], ps_t[:, :], xh[:, :].bitcast(F32), ALU.subtract).then_inc(t_done, 1)

            nc.vector.tensor_copy(rwh[:, :], a["router"][:, :]).then_inc(rw_hi, 1)
            nc.vector.tensor_copy(pick[:].rearrange("p a b -> p (a b)"), a["pick"][:, :]).then_inc(consts, 1)
            dve.wait_ge(rw_hi, 1)
            nc.vector.tensor_tensor(rwl[:, :], a["router"][:, :], rwh[:, :].bitcast(F32),
                                    ALU.subtract).then_inc(rw_ready, 1)
            split_x(Step(0), 0)
            for q in range(NQ):
                dve.wait_ge(wh_ready, q + 1)
                nc.vector.tensor_tensor(wl[:, q, :, :].rearrange("p a b -> p (a b)"),
                                        a["wgu"][:, q * 2 * P:(q + 1) * 2 * P],
                                        wh[:, q, :, :].rearrange("p a b -> p (a b)").bitcast(F32),
                                        ALU.subtract).then_inc(wl_ready, 1)
            dve.wait_ge(consts, 2)
            for st in token_steps(dve, LAST, 2):
                k = st.k
                rev = a["rev"][:, 0:E]

                def by_gate(q):
                    if not live(k - 1):
                        return
                    dve.wait_ge(gates_full, st.at(lambda k: gate_count(k, q)))
                    wait(dve, down_done, st.at(lambda k: NQ * (k - 1) + q - 1 - (q == 1)))
                    nc.vector.tensor_tensor(p[:, q % 2, :], h[:, q, :], ps_x[:, :], ALU.mult).then_inc(p_ready, 1)

                def hidden(q):
                    if not live(k):
                        return
                    if live(k - 1):
                        if q == 0:
                            dve.wait_ge(down_done, st.at(lambda k: NQ * (k - 1) + 1))
                        else:
                            dve.wait_ge(p_ready, st.at(lambda k: gate_count(k, q)))
                    dve.wait_ge(silu_done, st.at(lambda k: NQ * k + q + 1))
                    dve.wait_ge(up_full, st.at(lambda k: NQ * k + q + 1))
                    nc.vector.tensor_tensor(h[:, q, :], s[:, q % 3, :], ps_u[:, q % 3, :],
                                            ALU.mult).then_inc(h_done, 1)

                if live(k):
                    link.begin(st)
                    dve.wait_ge(t_full, st.at(lambda k: t_count(k, "logits")))
                    nc.vector.tensor_copy(lg[:].rearrange("p t e -> p (t e)"), ps_t[:, 0:TT * E]).then_inc(t_done, 1)
                    dve.wait_ge(t_done, st.at(lambda k: t_count(k, "logits")))
                    link(nc.vector.tensor_reduce(m1[:, :], lg[:, :, :], AX.X, ALU.max))
                    nc.vector.tensor_tensor(lg[:, :, :], lg[:, :, :], m1[:, :].unsqueeze(2).to_broadcast([P, TT, E]),
                                            ALU.subtract).then_inc(shifted, 1)
                for q in range(1, NQ):
                    by_gate(q)
                    if q == 6 and live(k):
                        link(nc.vector.scalar_tensor_tensor(out=far[:, :, :], in0=sel1[:, :, :], scalar=FAR,
                                                            in1=ex[:, :, :], op0=ALU.mult, op1=ALU.add))
                        best(nc, link, far[:, :, :], rev, m2[:, :], first[:, :], key[:, :, :], sel2[:, :, :])
                    if q == 7 and live(k):
                        link(nc.vector.tensor_tensor(sel1[:, :, :], sel1[:, :, :], sel2[:, :, :], ALU.add))
                        link(nc.vector.tensor_tensor(ex[:, :, :], sel1[:, :, :], ex[:, :, :], ALU.mult))
                        link(nc.vector.tensor_copy(cw[:, :, 0:E], ex[:, :, :]))
                        nc.vector.tensor_tensor(cw[:, :, E:2 * E], ex[:, :, :], cw[:, :, 0:E].bitcast(F32),
                                                ALU.subtract).then_inc(cw_ready, 1)
                    if q == 1:
                        hidden(0)
                    hidden(q)
                    if q == 1 and live(k - 2):
                        hold(dve, y_copied, st.at(lambda k: k - 1), passed)
                        for t in range(TT):
                            last = nc.vector.bn_stats(bn[:, t, :], acc[:, t * D:(t + 1) * D])
                        last.then_inc(bn_done, 1)
                    if q == 2 and live(k - 2):
                        hold(dve, bn_done, st.at(lambda k: k - 1), passed)
                        for t in range(TT):
                            last = nc.vector.bn_aggr(mv[:, t, :], bn[:, t, :])
                        last.then_inc(stats_ready, 1)
                    if q == 7 and live(k - 2):
                        dve.wait_ge(rs_ready, st.at(lambda k: k - 1))
                        normalise_tiles(nc, acc, mv, rs, acc).then_inc(y_normed, 1)
                    if not live(k):
                        continue
                    if q == 3:
                        dve.wait_ge(ex_ready, st.at(lambda k: k + 1))
                        link(nc.vector.tensor_reduce(total[:, :], ex[:, :, :], AX.X, ALU.add))
                        link(nc.vector.reciprocal(inv[:, :], total[:, :]))
                        link(nc.vector.tensor_tensor(ex[:, :, :], ex[:, :, :], inv[:, :].unsqueeze(2).to_broadcast(
                            [P, TT, E]), ALU.mult))
                    if q == 4:
                        best(nc, link, ex[:, :, :], rev, m1[:, :], first[:, :], key[:, :, :], sel1[:, :, :])
                if live(k + 1):
                    split_x(st, 1)

        @block.gpsimd
        def _(pool):
            nc.gpsimd.tensor_copy(zc[:, :], Z[:, 0:TOK]).then_inc(zc_ready, 1)
            nc.gpsimd.memset(half[:, :], -0.5)
            nc.gpsimd.memset(cw[:].rearrange("p t e -> p (t e)").bitcast(F32), 0.0).then_inc(consts, 1)
            for st in token_steps(pool, LAST, 2):
                if live(st.k + 1):
                    hold(pool, t_full, st.at(lambda k: t_count(k, "start")), passed)
                    nc.gpsimd.tensor_copy(zc[:, :], Z[:, block_of(st, 1)]).then_inc(zc_ready, 1)
                if live(st.k - 2):
                    hold(pool, stats_ready, st.at(lambda k: k - 1), passed)
                    nc.gpsimd.tensor_scalar(ve[:, :], mv[:, :, 1], EPS, None, ALU.add).then_inc(ve_ready, 1)
                    hold(pool, ve_ready, st.at(lambda k: k - 1), passed)
                    nc.gpsimd.tensor_tensor(rs[:, :], ve[:, :], half[:, :], ALU.pow).then_inc(rs_ready, 1)
                    hold(pool, y_normed, st.at(lambda k: k - 1), passed)
                    xx = X[:, block_of(st, -2)]
                    nc.gpsimd.tensor_tensor(xx, xx, acc[:, :], ALU.add).then_inc(x_new, 1)


def sandwich(nc, args, out):
    with ExitStack() as ctx:
        def sb(name, shape):
            return ctx.enter_context(nc.sbuf_tensor(name, shape, F32))

        def sem(name):
            return ctx.enter_context(nc.semaphore(name))

        X, Z = sb("X", [P, TILES * D]), sb("Z", [P, TILES * D])
        early = ["ident", "wqkv", "wo0", "bqkv", "bo0", "ln_w", "ln_b"]
        small = ["gate", "rev", "w_in", "wo1", "b_in", "bo1", "pos"]
        t = {n: sb(n, [P, args[n].shape[1]]) for n in early + small}
        loaded, later, last_loaded = sem("loaded"), sem("later"), sem("last_loaded")
        x_loaded = [sem("x_first"), sem("x_rest")]
        x_dram = args["x"].rearrange("(n p) d -> p n d", p=P)
        X3 = X[:, :].rearrange("p (n d) -> p n d", d=D)
        cut = X_FIRST * TPB
        ffn0, ffn1 = ["w1", "w2", "pick0"], ["wgu", "wd", "router", "pick"]

        def load(sp):
            sp.dma_start(X3[:, 0:cut, :], x_dram[:, 0:cut, :]).then_inc(x_loaded[0], 16)
            for n in early:
                sp.dma_start(t[n][:, :], args[n]).then_inc(loaded, 16)
            sp.dma_start(X3[:, cut:, :], x_dram[:, cut:, :]).then_inc(x_loaded[1], 16)
            for n in small + ffn0:
                sp.dma_start(t[n][:, :], args[n]).then_inc(later, 16)

        def load_last(sp):
            for n in ffn1:
                sp.dma_start(t[n][:, :], args[n]).then_inc(last_loaded, 16)
            sp.wait_ge(last_loaded, 16 * len(ffn1))

        with ExitStack() as first_layer:
            for n in ffn0:
                t[n] = first_layer.enter_context(nc.sbuf_tensor(n, [P, args[n].shape[1]], F32))
            first_attention(nc, X, Z, t["ident"], dict(
                wqkv=t["wqkv"], wo=t["wo0"], bqkv=t["bqkv"], bo=t["bo0"], ln_w=t["ln_w"], ln_b=t["ln_b"],
                x_loaded=x_loaded, loaded=loaded, loads=len(early), load=load, later=later,
                laters=len(small + ffn0)))
            first_layer.close()
            first_ffn(nc, X, Z, t["ident"], dict(w1=t["w1"], w2=t["w2"], gate=t["gate"], rev=t["rev"],
                                                     pick=t["pick0"]))
        for n in ffn1:
            t[n] = sb(n, [P, args[n].shape[1]])
        second_attention(nc, X, Z, t["ident"], dict(w=t["w_in"], wo=t["wo1"], b=t["b_in"], bo=t["bo1"], pos=t["pos"],
                                                    load=load_last))
        second_ffn(nc, X, Z, t["ident"], dict(wgu=t["wgu"], wd=t["wd"], router=t["router"], rev=t["rev"],
                                              pick=t["pick"]), out)


def lay_out(i):
    def rows(*vectors):
        v = np.concatenate(vectors)
        return np.ascontiguousarray(np.broadcast_to(v, (P, v.shape[0])))

    def chunks_of(w):
        e, d, hid = w.shape
        return w.reshape(e, d, hid // P, P).transpose(3, 0, 2, 1).reshape(P, -1)

    w1 = np.concatenate([i["L0_ffn_shared_w1"][None], i["L0_ffn_experts_w1"]])
    w2 = np.concatenate([i["L0_ffn_shared_w2"][None], i["L0_ffn_experts_w2"]])
    n, d, f = i["L1_ffn_Wg"].shape
    pairs = [i[w].reshape(n // 2, 2, d, f).transpose(2, 0, 1, 3).reshape(d, n // 2, 2 * f)
             for w in ("L1_ffn_Wg", "L1_ffn_Wu")]
    wgu = np.stack([np.concatenate([sh[:, None, :], w], 1)
                    for sh, w in zip((i["L1_ffn_Sg"], i["L1_ffn_Su"]), pairs)], 2)
    wd = np.concatenate([i["L1_ffn_Sd"][None], i["L1_ffn_Wd"].reshape(n // 2, 2 * f, d)])
    p = np.arange(P)
    pos, wpos = i["L1_attn_pos_embedding"], i["L1_attn_w_pos_embedding"]
    pick = np.zeros((P, n // 2, P), np.float32)
    for e in range(n):
        for row in (e, n + e):
            pick[row, e // 2, (e % 2) * f:(e % 2 + 1) * f] = 1
    experts = i["L0_ffn_experts_w1"].shape[0]
    pick0 = np.zeros((P, experts, P), np.float32)
    for e in range(experts):
        pick0[[e, experts + e], e] = 1
    return {
        "pick0": pick0.reshape(P, -1),
        "x": i["L0_attn_hidden_states"].reshape(B * S, D),
        "ident": np.eye(P, dtype=np.float32),
        "wqkv": np.concatenate([i["L0_attn_Wq"], i["L0_attn_Wk"], i["L0_attn_Wv"]], 1),
        "wo0": i["L0_attn_Wo"],
        "bqkv": rows(i["L0_attn_bq"], i["L0_attn_bk"], i["L0_attn_bv"]),
        "bo0": rows(i["L0_attn_bo"]),
        "ln_w": i["L0_attn_ln_w"][:, None],
        "ln_b": i["L0_attn_ln_b"][:, None],
        "w1": w1.transpose(2, 0, 1).reshape(D, -1),
        "w2": chunks_of(w2),
        "gate": i["L0_ffn_gate_w"].T,
        "rev": rows(np.arange(16, 0, -1).astype(np.float32)),
        "w_in": np.concatenate([i["L1_attn_w_v"], i["L1_attn_w_wqk"], i["L1_attn_w_qk"]], 1),
        "wo1": i["L1_attn_w_out"],
        "b_in": rows(i["L1_attn_b_v"], i["L1_attn_b_wqk"], i["L1_attn_b_qk"]),
        "bo1": rows(i["L1_attn_b_out"]),
        "pos": np.stack([pos[S - 1 - p], pos[S - 1 - P - p], wpos[S // 4 - 1 - p % (S // 4)]], 1),
        "wgu": wgu.reshape(D, -1),
        "wd": wd.transpose(1, 0, 2).reshape(P, -1),
        "router": i["L1_ffn_Wr"],
        "pick": pick.reshape(P, -1),
    }


def kernel(**inputs):
    import concourse.bacc as bacc
    from concourse.bass_utils import run_bass_kernel_spmd

    nc = bacc.Bacc("TRN2", target_bir_lowering=False, num_devices=1)
    arrays = {n: np.ascontiguousarray(v)
              for n, v in lay_out({n: np.asarray(v) for n, v in inputs.items()}).items()}
    args = {n: nc.dram_tensor("in_" + n, v.shape, F32, kind="ExternalInput").ap() for n, v in arrays.items()}
    out = nc.dram_tensor("out_x", (B * S, D), F32, kind="ExternalOutput").ap()
    sandwich(nc, args, out)
    r = run_bass_kernel_spmd(nc, [{"in_" + n: v for n, v in arrays.items()}], core_ids=[0])
    return r.results[0]["out_x"].reshape(B, S, D)
```
